# Optimizing a Trainium2 kernel written in Bass

```python
import numpy as np
import jax
import jax.numpy as jnp

def _softmax(x, axis=-1):
    return jax.nn.softmax(x, axis=axis)

def _gelu(x):
    return jax.nn.gelu(x, approximate=True)

def _silu(x):
    return jax.nn.silu(x)

def _sigmoid(x):
    return jax.nn.sigmoid(x)

def _layernorm(x, axis=-1, eps=1e-05):
    m = jnp.mean(x, axis=axis, keepdims=True)
    v = jnp.var(x, axis=axis, keepdims=True)
    return (x - m) / jnp.sqrt(v + eps)

def _scatter_add(tgt, idx, src, axis=0):
    return tgt.at[idx].add(src)

def _segment_sum(src, seg, n):
    return jax.ops.segment_sum(src, seg, n)
kernel_name = 'mk_decoder_preln_d1_seqx_r8_054053'

def setup_inputs(seed: int=0):
    np.random.seed(seed)
    _w = jnp.asarray

    def _rec_inputs():
        import jax
        import jax.numpy as jnp
        _rk = jax.random.key(seed)
        x = 0.5 + 0.2887 * jax.random.normal(jax.random.fold_in(_rk, 1), (4, 256, 256), jnp.float32)
        _lenS = 256 - jax.random.randint(jax.random.fold_in(_rk, 7), (4,), 0, max(1, 256 // 4) + 1, jnp.int32)
        _lenS2 = 256 - jax.random.randint(jax.random.fold_in(_rk, 8), (4,), 0, max(1, 256 // 4) + 1, jnp.int32)
        _ctx_512P = jax.random.normal(jax.random.fold_in(_rk, 11), (4, 16, 64), jnp.float32)
        _ctx_512c = jax.random.dirichlet(jax.random.fold_in(_rk, 511), 0.3 * jnp.ones((16,), jnp.float32), (4, 256))
        _ctx_512t = jnp.einsum('bsk,bkd->bsd', _ctx_512c, _ctx_512P)
        _ctx_512t = _ctx_512t * jax.lax.rsqrt(jnp.mean(jnp.square(_ctx_512t)) + 1e-12) * 0.953939
        ctx_512 = 7.22013e-05 + 1.00017 * (_ctx_512t + 0.3 * jax.random.normal(jax.random.fold_in(_rk, 611), (4, 256, 64), jnp.float32))
        _validS = jnp.arange(256)[None, :] < _lenS[:, None]
        _validS2 = jnp.arange(256)[None, :] < _lenS2[:, None]
        _causal = jnp.tril(jnp.ones((256, 256), dtype=bool))
        mask_SxS2_bk1 = jnp.broadcast_to(_validS2[0:1, :], (256, 256))
        mask_BxS2_bf0 = jnp.logical_not(jnp.ones((4, 256), dtype=bool))
        return (x, ctx_512, mask_SxS2_bk1, mask_BxS2_bf0)
    x, ctx_512, mask_SxS2_bk1, mask_BxS2_bf0 = _rec_inputs()

    def _L0_attn_setup():
        import jax, jax.numpy as jnp
        import numpy as np
        HEAD_DIM = 128
        N_HEADS = 16
        N_KV_HEADS = 4
        CHUNK = 32
        TOPK = 4
        ROPE_THETA = 10000.0

        def apply_rope(x, pos):
            d = x.shape[-1]
            inv_freq = 1.0 / ROPE_THETA ** (jnp.arange(0, d, 2, dtype=jnp.float32) / d)
            ang = pos.astype(jnp.float32)[:, None] * inv_freq[None, :]
            cos = jnp.cos(ang)[None, :, None, :]
            sin = jnp.sin(ang)[None, :, None, :]
            x1, x2 = (x[..., :d // 2], x[..., d // 2:])
            return jnp.concatenate([x1 * cos - x2 * sin, x2 * cos + x1 * sin], axis=-1)
        key = jax.random.key(seed)
        ks = jax.random.split(key, 5)
        B, S, H = (2, 256, 256)
        hidden_states = jax.random.normal(ks[0], (B, S, H), dtype=jnp.float32)
        wq = jax.random.normal(ks[1], (H, N_HEADS * HEAD_DIM), dtype=jnp.float32) * 0.02
        wk = jax.random.normal(ks[2], (H, N_KV_HEADS * HEAD_DIM), dtype=jnp.float32) * 0.02
        wv = jax.random.normal(ks[3], (H, N_KV_HEADS * HEAD_DIM), dtype=jnp.float32) * 0.02
        wo = jax.random.normal(ks[4], (N_HEADS * HEAD_DIM, H), dtype=jnp.float32) * 0.02
        return {'hidden_states': hidden_states, 'wq': wq, 'wk': wk, 'wv': wv, 'wo': wo}
    _L0_attn_all = _L0_attn_setup()
    _L0_attn_in = {k: v for k, v in _L0_attn_all.items() if k in ('wq', 'wk', 'wv', 'wo')}
    del _L0_attn_all

    def _L0_xattn_setup():
        import jax, jax.numpy as jnp
        import numpy as np
        B, S, H = (8, 256, 64)
        key = jax.random.key(seed)
        kq, kk, kqc, kwq, kwk = jax.random.split(key, 5)
        q = jax.random.normal(kq, (B, S, H), dtype=jnp.float32)
        k = jax.random.normal(kk, (B, S, H), dtype=jnp.float32)
        qc_score = jax.random.uniform(kqc, (B, S, S), dtype=jnp.float32)
        attn_mask = jnp.triu(jnp.ones((S, S), dtype=bool), k=1)
        key_padding_mask = jnp.zeros((B, S), dtype=bool)
        scale = 1.0 / np.sqrt(H)
        Wq = jax.random.normal(kwq, (H, H), dtype=jnp.float32) * scale
        Wk = jax.random.normal(kwk, (H, H), dtype=jnp.float32) * scale
        bq = jnp.zeros((H,), dtype=jnp.float32)
        bk = jnp.zeros((H,), dtype=jnp.float32)
        return {'q': q, 'k': k, 'attn_mask': attn_mask, 'key_padding_mask': key_padding_mask, 'qc_score': qc_score, 'Wq': Wq, 'bq': bq, 'Wk': Wk, 'bk': bk}
    _L0_xattn_all = _L0_xattn_setup()
    _L0_xattn_in = {k: v for k, v in _L0_xattn_all.items() if k in ('Wq', 'bq', 'Wk', 'bk')}
    del _L0_xattn_all

    def _L0_ffn_setup():
        import jax, jax.numpy as jnp
        import numpy as np
        B, S, D_IN, D_OUT, E = (4, 128, 256, 256, 32)
        MASK_DENSITY = 0.3
        THRESH = 0.5
        key = jax.random.key(seed)
        k_x, k_w, k_m, k_r = jax.random.split(key, 4)
        x = jax.random.normal(k_x, (B, S, D_IN), dtype=jnp.float32)
        bound = np.sqrt(1.0 / D_IN) * np.sqrt(3.0)
        weight = jax.random.uniform(k_w, (D_OUT, D_IN), minval=-bound, maxval=bound, dtype=jnp.float32)
        scale = jnp.ones((D_OUT,), dtype=jnp.float32)
        expert_masks = (jax.random.uniform(k_m, (E, D_OUT, D_IN)) < MASK_DENSITY).astype(jnp.float32)
        router_w = 0.01 * jax.random.normal(k_r, (E, D_IN), dtype=jnp.float32)
        return {'x': x, 'weight': weight, 'scale': scale, 'expert_masks': expert_masks, 'router_w': router_w}
    _L0_ffn_all = _L0_ffn_setup()
    _L0_ffn_in = {k: v for k, v in _L0_ffn_all.items() if k in ('weight', 'scale', 'expert_masks', 'router_w')}
    del _L0_ffn_all
    return {'x': x, 'ctx_512': ctx_512, 'mask_SxS2_bk1': mask_SxS2_bk1, 'mask_BxS2_bf0': mask_BxS2_bf0, 'L0_attn_wq': _L0_attn_in['wq'], 'L0_attn_wk': _L0_attn_in['wk'], 'L0_attn_wv': _L0_attn_in['wv'], 'L0_attn_wo': _L0_attn_in['wo'], 'L0_xattn_Wq': _L0_xattn_in['Wq'], 'L0_xattn_bq': _L0_xattn_in['bq'], 'L0_xattn_Wk': _L0_xattn_in['Wk'], 'L0_xattn_bk': _L0_xattn_in['bk'], 'L0_ffn_weight': _L0_ffn_in['weight'], 'L0_ffn_scale': _L0_ffn_in['scale'], 'L0_ffn_expert_masks': _L0_ffn_in['expert_masks'], 'L0_ffn_router_w': _L0_ffn_in['router_w']}

def reference(x, ctx_512, mask_SxS2_bk1, mask_BxS2_bf0, L0_attn_wq, L0_attn_wk, L0_attn_wv, L0_attn_wo, L0_xattn_Wq, L0_xattn_bq, L0_xattn_Wk, L0_xattn_bk, L0_ffn_weight, L0_ffn_scale, L0_ffn_expert_masks, L0_ffn_router_w):
    import jax
    import jax.numpy as jnp

    def _L0_attn_ref(hidden_states, wq, wk, wv, wo):
        import jax, jax.numpy as jnp
        import numpy as np
        HEAD_DIM = 128
        N_HEADS = 16
        N_KV_HEADS = 4
        CHUNK = 32
        TOPK = 4
        ROPE_THETA = 10000.0

        def apply_rope(x, pos):
            d = x.shape[-1]
            inv_freq = 1.0 / ROPE_THETA ** (jnp.arange(0, d, 2, dtype=jnp.float32) / d)
            ang = pos.astype(jnp.float32)[:, None] * inv_freq[None, :]
            cos = jnp.cos(ang)[None, :, None, :]
            sin = jnp.sin(ang)[None, :, None, :]
            x1, x2 = (x[..., :d // 2], x[..., d // 2:])
            return jnp.concatenate([x1 * cos - x2 * sin, x2 * cos + x1 * sin], axis=-1)
        B, S, _ = hidden_states.shape
        q = (hidden_states @ wq).reshape(B, S, N_HEADS, HEAD_DIM)
        k = (hidden_states @ wk).reshape(B, S, N_KV_HEADS, HEAD_DIM)
        v = (hidden_states @ wv).reshape(B, S, N_KV_HEADS, HEAD_DIM)
        pos = jnp.arange(S)
        q = apply_rope(q, pos)
        k = apply_rope(k, pos)
        g = N_HEADS // N_KV_HEADS
        k = jnp.repeat(k, g, axis=2)
        v = jnp.repeat(v, g, axis=2)
        N = S // CHUNK
        kmean = k.reshape(B, N, CHUNK, N_HEADS, HEAD_DIM).mean(axis=2)
        gate = jnp.einsum('bnhd,bshd->bhsn', kmean, q)
        chunk_ids = jnp.arange(N)
        chunk_end = (chunk_ids + 1) * CHUNK
        q_chunk = pos // CHUNK
        gate = jnp.where(pos[None, None, :, None] >= chunk_end[None, None, None, :], gate, -jnp.inf)
        gate = jnp.where(q_chunk[None, None, :, None] == chunk_ids[None, None, None, :], jnp.inf, gate)
        _, idx = jax.lax.top_k(gate, min(TOPK, N))
        sel = jnp.any(idx[..., None] == chunk_ids, axis=-2)
        allowed = sel[:, :, :, pos // CHUNK]
        causal = pos[:, None] >= pos[None, :]
        mask = allowed & causal[None, None]
        scale = HEAD_DIM ** (-0.5)
        scores = jnp.einsum('bshd,bthd->bhst', q, k) * scale
        scores = jnp.where(mask, scores, -jnp.inf)
        probs = jax.nn.softmax(scores, axis=-1)
        o = jnp.einsum('bhst,bthd->bshd', probs, v).reshape(B, S, N_HEADS * HEAD_DIM)
        return o @ wo

    def _L0_xattn_ref(q, k, attn_mask, key_padding_mask, qc_score, Wq, bq, Wk, bk):
        import jax, jax.numpy as jnp
        import numpy as np
        B, S, H = (8, 256, 64)
        qp = jnp.einsum('bsh,oh->bso', q, Wq) + bq
        kp = jnp.einsum('bth,oh->bto', k, Wk) + bk
        scaling = jnp.asarray(float(H) ** (-0.5), dtype=qp.dtype)
        scores = jnp.einsum('bsh,bth->bst', qp, kp) * scaling
        scores = scores * qc_score
        mask = attn_mask[None, :, :] | key_padding_mask[:, None, :]
        scores = jnp.where(mask, -jnp.inf, scores)
        return jax.nn.softmax(scores, axis=-1)

    def _L0_ffn_ref(x, weight, scale, expert_masks, router_w):
        import jax, jax.numpy as jnp
        import numpy as np
        B, S, D_IN, D_OUT, E = (4, 128, 256, 256, 32)
        MASK_DENSITY = 0.3
        THRESH = 0.5
        logits = jnp.einsum('bsd,ed->bse', x, router_w)
        probs = jax.nn.softmax(logits, axis=-1)
        top1_w = jnp.max(probs, axis=-1)
        top1_idx = jnp.argmax(probs, axis=-1)
        w_q = jnp.clip(jnp.round(weight / THRESH), -1.0, 1.0)
        w_scaled = w_q * scale[:, None]
        out0 = jnp.zeros((x.shape[0], x.shape[1], weight.shape[0]), dtype=x.dtype)

        def body(out, inputs):
            e_idx, mask_e = inputs
            y = jnp.einsum('bsi,oi->bso', x, w_scaled * mask_e)
            sel = (top1_idx == e_idx)[..., None]
            out = jnp.where(sel, y * top1_w[..., None], out)
            return (out, None)
        out, _ = jax.lax.scan(body, out0, (jnp.arange(E), expert_masks))
        return out
    x = x + _L0_attn_ref(_layernorm(x, axis=-1), L0_attn_wq, L0_attn_wk, L0_attn_wv, L0_attn_wo)
    x = x + _L0_xattn_ref(ctx_512, ctx_512, mask_SxS2_bk1, mask_BxS2_bf0, _layernorm(x, axis=-1), L0_xattn_Wq, L0_xattn_bq, L0_xattn_Wk, L0_xattn_bk)
    x = x + _L0_ffn_ref(_layernorm(x, axis=-1), L0_ffn_weight, L0_ffn_scale, L0_ffn_expert_masks, L0_ffn_router_w)
    return x

_drawn_inputs = setup_inputs


def setup_inputs(seed=0):
    import zlib

    import numpy as np

    out = dict(_drawn_inputs(seed))
    spreads = {'L0_xattn_bq': (0.0, 0.8), 'L0_xattn_bk': (0.0, 0.8), 'L0_ffn_scale': (1.0, 0.2)}
    factors = {}
    for name, (base, spread) in spreads.items():
        noise = np.random.default_rng([zlib.crc32(name.encode()), seed]).standard_normal(out[name].shape)
        drawn = base * np.exp(spread * noise) if base else spread * noise
        out[name] = jnp.asarray(drawn.astype(out[name].dtype))
    for name, factor in factors.items():
        out[name] = (out[name] * factor).astype(out[name].dtype)
    return out
```

```python
import concourse.bass as bass
from concourse import mybir
from contextlib import ExitStack

B, S, H = 4, 256, 256
NH, NG, D = 16, 4, 128
HG = NH // NG
CHUNK, NCH, TOPK = 32, 8, 4
E_N = 32
CTX = 64
P = 128
KC = H // P
TT = S // P
NT = B * TT
STEPS = NG * 2
SEGS = NT + E_N - 1
ROW = 264
EPS = 1e-5
SCALE = float(D) ** -0.5
NEG = -1.0e30
NCAND = NCH - 1

USES = {0: ["K", "Q", "V0", "V1"], 1: ["Q"], 2: ["K", "Q"], 3: ["Q"],
        4: ["K", "Q"], 5: ["Q"], 6: ["K", "Q"], 7: ["Q"]}
USE0 = {l: sum(len(USES[m]) for m in range(l)) for l in range(9)}
ROPE0 = {l: sum(u in ("K", "Q") for m in range(l) for u in USES[m]) for l in range(9)}
N_USE, N_ROPE, PRE = USE0[8], ROPE0[8], 3
SLICES = ["K", "Q0", "V", "Q1", "O0", "Q2", "Q3", "O1", "O2", "O3"]
EARLY = 4
LATE = {0: [4, 5], 2: [6, 7], 4: [8], 5: [9]}
RAW_E = 12


def program(nc, x, ctxT, smask, kmask, wq, wk, wv, wo, xwq, xwk, xbias, ffw, ffscale, masks, rw, cosT, sinT, ident, consts, tri, causal, out, scratch):
    fp32, f32r, bf16 = mybir.dt.float32, mybir.dt.float32r, mybir.dt.bfloat16
    u32, i32, u8 = mybir.dt.uint32, mybir.dt.int32, mybir.dt.uint8
    ALU, ACT, AX = mybir.AluOpType, mybir.ActivationFunctionType, mybir.AxisListType

    with ExitStack() as ctx:
        def sb(name, shape, dt=fp32):
            return ctx.enter_context(nc.sbuf_tensor(name, shape, dt))

        def pb(name, shape, dt=fp32):
            return ctx.enter_context(nc.psum_tensor(name, shape, dt))

        sems = {}

        def sem(name):
            sems[name] = ctx.enter_context(nc.semaphore(name))
            return sems[name]

        experts = sb("experts", [P, E_N, KC, H])
        exp_flat = experts[:, :, :, :].rearrange("p e k o -> p (e k o)")
        raw0 = RAW_E * KC * H
        raw = {}
        for i, name in enumerate(SLICES):
            raw[name] = exp_flat[:, raw0 + i * 1024:raw0 + (i + 1) * 1024]
        w_hi = sb("w_hi", [P, len(SLICES), 1024], f32r)
        w_lo = sb("w_lo", [P, len(SLICES), 1024], f32r)
        rows = sb("rows", [P, NT, ROW])
        xscore = sb("xscore", [P, NT, ROW])
        xnrow = sb("xnrow", [P, TT, H])
        xnT_hi = sb("xnT_hi", [P, KC, S], f32r)
        xnT_lo = sb("xnT_lo", [P, KC, S], f32r)
        qt = sb("qt", [P, 2, 2, S])
        kt = sb("kt", [P, 2, S + NCH])
        swap = sb("swap", [P, 2, 2, S])
        v_hi = sb("v_hi", [P, TT, NG * D], f32r)
        v_lo = sb("v_lo", [P, TT, NG * D], f32r)
        probs = sb("probs", [P, 2, 384])
        pT_hi = sb("pT_hi", [P, 2, 384], f32r)
        pT_lo = sb("pT_lo", [P, 2, 384], f32r)
        oT_hi = sb("oT_hi", [P, 2, S], f32r)
        oT_lo = sb("oT_lo", [P, 2, S], f32r)
        cos_sb = sb("cos_sb", [P, S])
        sin_sb = sb("sin_sb", [P, S])
        id_sb = sb("id_sb", [P, P])
        id_bf = sb("id_bf", [P, P], bf16)
        cau_bf = sb("cau_bf", [P, P], bf16)
        post = sb("post", [P, TT, H])
        bias_x = sb("bias_x", [P, TT, H], bf16)
        smask_sb = sb("smask_sb", [P, TT, S], u8)
        kmask_sb = sb("kmask_sb", [P, B, S], u8)
        small = sb("small", [P, 512])
        rw_sb = sb("rw_sb", [P, KC, E_N])
        con = sb("con", [P, 256])
        xw_sb = sb("xw_sb", [CTX, 2, CTX])
        xb_sb = sb("xb_sb", [CTX, 2])
        idx8 = sb("idx8", [P, 8], u32)

        tern = sb("tern", [P, KC, H])
        tern_flat = tern[:, :, :].rearrange("p k o -> p (k o)")
        fs_sb = probs[:, 0, 0:H]
        slot_u = sb("slot_u", [P, NT], u32)
        tok_u = sb("tok_u", [P, NT], u32)
        seg_i = sb("seg_i", [P, 4, 48], i32)
        mask_w = post[:, 0, :]
        seg_f = sb("seg_f", [P, SEGS])
        tri_sb = sin_sb[:, :].rearrange("p (a b) -> p a b", a=2)
        cau_f = probs[:, 1, 0:P]
        lg8x = sb("lg8x", [P, TT, 8])
        idxx = sb("idxx", [P, TT, 8], u32)
        xqk = experts[0:CTX, 8:12, :, :].rearrange("p e k o -> p (e k o)").rearrange("p (a n) -> p a n", a=2)
        oh = xnrow[:, 0, :]
        base = xnrow[:, 1, :]
        zero256 = cos_sb[:, :]
        stage_x = probs[:, :, :].rearrange("p a b -> p (a b)").rearrange("p (s k n) -> p s k n", s=3, k=KC)

        def sorted_T(kc):
            return (qt if kc == 0 else swap)[:, :, :, :].rearrange("p a b c -> p (a b c)")

        cand = con[:, 0:7]
        ncand = con[:, 8:15]
        lower = con[:, 16:65].rearrange("p (n m) -> p n m", n=NCAND)
        iota_e = con[:, 72:104]
        iota_j = con[:, 104:104 + SEGS]
        bound = con[:, 144:151]
        tile1 = con[:, 152:159]
        eps2, neg_half2 = con[:, 176:178], con[:, 178:180]
        token = con[:, 160:168]

        mx = [small[:, 4 * i:4 * i + 4] for i in range(2)]
        nm = [small[:, 8 + 4 * i:12 + 4 * i] for i in range(2)]
        sums = [small[:, 16 + 4 * i:20 + 4 * i] for i in range(2)]
        rsum = [small[:, 24 + 4 * i:28 + 4 * i] for i in range(2)]
        gate = small[:, 32:46].rearrange("p (h n) -> p h n", h=2)
        rank = small[:, 48:62].rearrange("p (h n) -> p h n", h=2)
        selb = small[:, 64:80].rearrange("p (h n) -> p h n", h=2)
        bn = small[:, 80:92].rearrange("p (t s) -> p t s", t=2)
        mv = small[:, 92:96].rearrange("p (t s) -> p t s", t=2)
        rstd = small[:, 96:98]
        bn2 = small[:, 100:112].rearrange("p (t s) -> p t s", t=2)
        mv2 = small[:, 112:116].rearrange("p (t s) -> p t s", t=2)
        rstd2 = small[:, 116:118]
        xmx, xnm, xsum, xrs = (small[:, 120 + 2 * i:122 + 2 * i] for i in range(4))
        xany = small[:, 128:130]
        logit = small[:, 136:200].rearrange("p (t e) -> p t e", t=2)
        lnm, lsum = small[:, 200:202], small[:, 202:204]
        cmp = small[:, 208:208 + 196].rearrange("p (a m) -> p a m", m=2 * NCAND)
        cmp_gt = cmp[:, :, 0:NCAND].rearrange("p (h n) m -> p h n m", h=2)
        cmp_eq = cmp[:, :, NCAND:].rearrange("p (h n) m -> p h n m", h=2)
        eidx = small[:, 404:406]

        proj = pb("proj", [P, 2, 512])
        sc = pb("sc", [P, 4, 512])
        ot = pb("ot", [P, 512])
        y = pb("y", [P, TT, H])

        ld_x, ld_w, ld_c, ld_m = sem("ld_x"), [sem(f"ld_w{i}") for i in range(len(SLICES))], sem("ld_c"), sem("ld_m")
        w_hi_ok, w_lo_ok = sem("w_hi_ok"), sem("w_lo_ok")
        xnr_ok, xt_full, xt_hi_ok, xt_lo_ok = sem("xnr_ok"), sem("xt_full"), sem("xt_hi_ok"), sem("xt_lo_ok")
        pj_full, pj_act, pj_dve = sem("pj_full"), sem("pj_act"), sem("pj_dve")
        pool_t2, rope_ok, km_ok = sem("pool_t2"), sem("rope_ok"), sem("km_ok")
        sc_full, nm_ok, exp_ok, pn_ok = sem("sc_full"), sem("nm_ok"), sem("exp_ok"), sem("pn_ok")
        pt_full, pt_hi_ok, pt_lo_ok = sem("pt_full"), sem("pt_hi_ok"), sem("pt_lo_ok")
        pv_full, ot_hi_ok, ot_lo_ok, o_done = sem("pv_full"), sem("ot_hi_ok"), sem("ot_lo_ok"), sem("o_done")
        d_sm, d_nm, d_ln, d_post = sem("d_sm"), sem("d_nm"), sem("d_ln"), sem("d_post")
        x1_ok, qc_ok, xm_ok, xs_ok = sem("x1_ok"), sem("qc_ok"), sem("xm_ok"), sem("xs_ok")
        xnm_ok, xexp_ok, xn3_ok, x3_full, x3_ok = sem("xnm_ok"), sem("xexp_ok"), sem("xn3_ok"), sem("x3_full"), sem("x3_ok")
        lg_m, lg_x = sem("lg_m"), sem("lg_x")
        lg_full, lg_ok, lnm_ok, lexp_ok, row_ok = sem("lg_full"), sem("lg_ok"), sem("lnm_ok"), sem("lexp_ok"), sem("row_ok")
        ld_x2 = sem("ld_x2")
        mb_ok, pace = sem("mb_ok"), sem("pace")
        rs_add, rs2_add = sem("rs_add"), sem("rs2_add")
        mv_ok, rs_ok, mv2_ok, rs2_ok = sem("mv_ok"), sem("rs_ok"), sem("mv2_ok"), sem("rs2_ok")
        p_bias, p_w = sem("p_bias"), sem("p_w")
        su_pe, su_act, su_dve, su_pool = sem("su_pe"), sem("su_act"), sem("su_dve"), sem("su_pool")
        tl = {n: sem("tl_" + n) for n in ("oh", "pe", "dve", "slot", "scat", "back", "xn", "xt", "xte", "reg", "seg", "stage", "acc", "out")}

        def use(b, l, name):
            return PRE + N_USE * b + USE0[l] + USES[l].index(name)

        def bank(l, name):
            return (PRE + USE0[l] + USES[l].index(name)) % 2

        def rope(b, l, name):
            return PRE + N_ROPE * b + ROPE0[l] + (0 if name == "K" or l % 2 else 1)

        def need(eng, s, n):
            if not isinstance(n, int) or n > 0:
                eng.wait_ge(s, n)

        def batches(eng, body):
            body(0, True, False)
            with eng.Fori(1, B - 1) as b:
                body(b, False, False)
            body(B - 1, False, True)

        def w(name, part):
            t = w_hi if part == 0 else w_lo
            return t[:, SLICES.index(name), :]

        PARTS = ((0, 0), (0, 1), (1, 0))

        def segments(eng, body):
            for k in range(3):
                body(k, k)
            with eng.Fori(3, SEGS, 3) as j:
                for k in range(3):
                    body(j + k, k)

        block = ctx.enter_context(nc.Block())

        @block.sync
        def _(sp):
            xr = x.rearrange("b (t p) n -> p (b t) n", p=P)
            wsrc = {"K": wk, "V": wv}
            wsrc.update({f"Q{g}": wq[:, g * 1024:(g + 1) * 1024] for g in range(NG)})
            wsrc.update({f"O{g}": wo[:, g * 1024:(g + 1) * 1024] for g in range(NG)})

            def load_w(i):
                sp.dma_start(raw[SLICES[i]], wsrc[SLICES[i]]).then_inc(ld_w[i], 16)
            sp.dma_start(rows[:, 0:TT, 0:H], xr[:, 0:TT]).then_inc(ld_x, 16)
            load_w(0)
            load_w(1)
            for i in range(2, len(SLICES)):
                load_w(i)
                if i == 3:
                    sp.dma_start(rows[:, TT:NT, 0:H], xr[:, TT:NT]).then_inc(ld_x2, 16)
            for i in range(8):
                if 4 * i == RAW_E:
                    sp.wait_ge(w_lo_ok, len(SLICES))
                    sp.wait_ge(w_hi_ok, len(SLICES))
                if i == 2:
                    sp.wait_ge(su_pe, 8)
                if i % 2 == 0 and i > 0:
                    sp.wait_ge(ld_m, 16 * i)
                sp.dma_start(experts[:, 4 * i:4 * i + 4].rearrange("p e k o -> p (e k o)"),
                             masks[:, 4 * i * KC * H:4 * (i + 1) * KC * H]).then_inc(ld_m, 16)

            sp.wait_ge(tl["scat"], 16 * NT)
            sp.dma_start(xscore[:, :, :], scratch.rearrange("(i p) n -> p i n", p=P)).then_inc(tl["back"], 16)

        @block.gpsimd
        def _(pool):
            for dst, src in ((id_sb[:, :], ident), (con[:, :], consts), (cos_sb[:, :], cosT), (sin_sb[:, :], sinT)):
                pool.dma_start(dst, src).then_inc(su_pool, 16)
            pool.dma_start(smask_sb[:, :, :], smask.rearrange("(t p) s -> p t s", p=P)).then_inc(p_bias, 16)
            pool.dma_start(kmask_sb[:, :, :].rearrange("p b s -> p (b s)"),
                           kmask.rearrange("b s -> (b s)").rearrange("(a n) -> a n", a=1).to_broadcast([P, B * S])).then_inc(p_bias, 16)

            def inverse_std(mv_, rstd_, s_in, n, s_out, s_add):
                pool.wait_ge(s_in, n)
                nc.gpsimd.tensor_tensor(rstd_, mv_[:, :, 1], eps2, ALU.add).then_inc(s_add, 1)
                pool.wait_ge(s_add, n)
                nc.gpsimd.tensor_tensor(rstd_, rstd_, neg_half2, ALU.pow).then_inc(s_out, 1)

            def rotate(i, r, n_, width, dst, free_sem, free_n):
                sw = swap[:, i % 2, 0:width, :]
                pool.wait_ge(pj_act, n_ + 1)
                nc.gpsimd.tensor_tensor(sw, sw, sin_sb[:, :].unsqueeze(1).to_broadcast([P, width, S]), ALU.mult).then_inc(pool_t2, 1)
                pool.wait_ge(pj_dve, n_ + 1)
                pool.wait_ge(pool_t2, r + 1)
                nc.gpsimd.tensor_tensor(dst, dst, sw, ALU.add).then_inc(rope_ok, 1)

            pool.wait_ge(su_pool, 64)
            inverse_std(mv, rstd, mv_ok, 1, rs_ok, rs_add)
            rotate(0, 0, 0, 1, kt[:, 0:1, 0:S], None, 0)
            rotate(1, 1, 1, 2, qt[:, 0], None, 0)
            rotate(2, 2, 2, 2, qt[:, 1], None, 0)

            def body(b, first, last):
                for l in range(STEPS):
                    v = b * STEPS + l
                    if not (last and l >= 6):
                        for name in USES[l]:
                            if name in ("K", "Q"):
                                r = rope(b, l, name)
                                i = PRE + ROPE0[l] + (0 if name == "K" or l % 2 else 1)
                                n_ = use(b, l, name)
                                if name == "K":
                                    g = (l // 2 + 1) % NG
                                    rotate(i, r, n_, 1, kt[:, g % 2:g % 2 + 1, 0:S], None, 0)
                                else:
                                    rotate(i, r, n_, 2, qt[:, l % 2], None, 0)
                    if l == 0:
                        pool.wait_ge(ld_m, 32 * (b + 1))
                    if first and l == 0:
                        pool.wait_ge(su_dve, 4)
                    e_ap = experts[:, bass.ds(b * STEPS + l, 1), :, :].rearrange("p a k o -> p (a k o)")
                    nc.gpsimd.tensor_tensor(e_ap, e_ap, tern_flat, ALU.mult).then_inc(p_w, 1)
                    if l == 3 and not last:
                        inverse_std(mv, rstd, mv_ok, b + 2, rs_ok, rs_add)
                    if not first and l in (1, 4):
                        inverse_std(mv2, rstd2, mv2_ok, 2 * (b - 1) + (1 if l == 1 else 2), rs2_ok, rs2_add)
                    if not first and l == 2:
                        cross_scores(b - 1)

            def cross_scores(p):
                pool.wait_ge(qc_ok, p + 1)
                if isinstance(p, int) and p == 0:
                    pool.wait_ge(su_dve, 6)
                nc.gpsimd.tensor_tensor(post[:, :, :], post[:, :, :], xscore[:, bass.ds(TT * p, TT), 0:S], ALU.mult).then_inc(xs_ok, 1)
                pool.wait_ge(xs_ok, 2 * p + 1)
                pool.wait_ge(mb_ok, 2 * p + 2)
                nc.gpsimd.tensor_tensor(post[:, :, :], post[:, :, :], bias_x[:, :, :], ALU.add).then_inc(xs_ok, 1)

            batches(pool, body)
            inverse_std(mv2, rstd2, mv2_ok, 2 * B - 1, rs2_ok, rs2_add)
            cross_scores(B - 1)
            inverse_std(mv2, rstd2, mv2_ok, 2 * B, rs2_ok, rs2_add)
            pool.wait_ge(rope_ok, PRE + N_ROPE * B - 3)
            pool.dma_start(tri_sb[:, :, :].rearrange("p a b -> p (a b)"), tri).then_inc(p_bias, 16)
            for i in range(NT):
                if i == 0:
                    pool.wait_ge(tl["slot"], 1)
                nc.gpsimd.indirect_dma_start(scratch, bass.IndirectOffsetOnAxis(slot_u[:, i:i + 1], 0),
                                             rows[:, i, :], None).then_inc(tl["scat"], 16)
            pool.wait_ge(tl["acc"], SEGS)
            pool.wait_ge(tl["dve"], 30)
            for i in range(NT):
                nc.gpsimd.indirect_dma_start(out, bass.IndirectOffsetOnAxis(tok_u[:, i:i + 1], 0),
                                             xscore[:, i, 0:H], None).then_inc(tl["out"], 16)
            pool.wait_ge(tl["out"], 16 * NT)


        @block.scalar
        def _(act):
            act.dma_start(rw_sb[:, :, :], rw).then_inc(ld_c, 16)
            act.dma_start(xw_sb[:, 0, :], xwq).then_inc(ld_c, 16)
            act.dma_start(xw_sb[:, 1, :], xwk).then_inc(ld_c, 16)
            act.dma_start(xb_sb[:, :], xbias).then_inc(ld_c, 16)
            act.dma_start(qt[0:CTX, :, :, :].rearrange("p a b c -> p (a b c)"), ctxT).then_inc(ld_c, 16)
            act.dma_start(tern[:, :, :], ffw).then_inc(ld_c, 16)
            act.dma_start(fs_sb[:, :], ffscale.rearrange("(a n) -> a n", a=1).to_broadcast([P, H])).then_inc(ld_c, 16)
            act.dma_start(cau_f, causal).then_inc(ld_c, 16)

            def split_hi(i):
                act.wait_ge(ld_w[i], 16)
                nc.scalar.activation(w_hi[:, i, :], raw[SLICES[i]], ACT.Copy).then_inc(w_hi_ok, 1)

            def copy_ot(dst, s_):
                nc.scalar.activation(dst, ot[:, :], ACT.Copy).then_inc(s_, 1)

            def halves(i, r, n_, bk, width):
                act.wait_ge(pj_full, n_ + 1)
                need(act, rope_ok, r - 1)
                src = proj[:, bk, 0:width * S].rearrange("p (h s) -> p h s", h=width)
                nc.scalar.activation(swap[0:64, i % 2, 0:width, :], src[64:128], ACT.Copy)
                nc.scalar.activation(swap[64:128, i % 2, 0:width, :], src[0:64], ACT.Copy).then_inc(pj_act, 1)

            for i in range(4):
                act.wait_ge(su_pe, i + 1)
                nc.scalar.activation(xqk[:, i % 2, (i // 2) * 512:(i // 2 + 1) * 512], sc[0:CTX, i, :], ACT.Identity,
                                     bias=xb_sb[:, i % 2:i % 2 + 1]).then_inc(su_act, 1)
            for i in range(2):
                split_hi(i)
            act.wait_ge(xt_full, 1)
            copy_ot(xnT_hi[:, :, :].rearrange("p k s -> p (k s)"), xt_hi_ok)
            for i in range(2, EARLY):
                split_hi(i)
            halves(0, 0, 0, 0, 1)
            halves(1, 1, 1, 1, 2)
            halves(2, 2, 2, 0, 2)

            def pt_hi(v):
                act.wait_ge(pt_full, v + 1)
                need(act, pv_full, v)
                q = (v if isinstance(v, int) else None)
                return q

            def body(b, first, last):
                for l in range(STEPS):
                    v = b * STEPS + l
                    if not (first and l == 0):
                        act.wait_ge(pt_full, v)
                        need(act, pv_full, v - 1)
                        qq = (l - 1) % 2
                        nc.scalar.activation(pT_hi[:, :, :], sc[:, 2 * qq:2 * qq + 2, 0:384], ACT.Copy).then_inc(pt_hi_ok, 1)
                    if l == 6 and not last:
                        act.wait_ge(xt_full, b + 2)
                        copy_ot(xnT_hi[:, :, :].rearrange("p k s -> p (k s)"), xt_hi_ok)

                    def swaps():
                        if not (last and l >= 6):
                            for name in USES[l]:
                                if name in ("K", "Q"):
                                    i = PRE + ROPE0[l] + (0 if name == "K" or l % 2 else 1)
                                    halves(i, rope(b, l, name), use(b, l, name), bank(l, name), 1 if name == "K" else 2)
                    if l != 6:
                        swaps()
                    act.wait_ge(nm_ok, v + 1)
                    need(act, pt_full, v)
                    q = l % 2
                    for h in range(2):
                        nc.scalar.activation(probs[:, h, 0:P], sc[:, 2 * q + h, 0:P], ACT.Exp, bias=nm[q][:, h:h + 1],
                                             scale=SCALE, accum_out=sums[q][:, h:h + 1])
                        last_i = nc.scalar.activation(probs[:, h, P:384], sc[:, 2 * q + h, P:384], ACT.Exp,
                                                      bias=nm[q][:, 2 + h:3 + h], scale=SCALE, accum_out=sums[q][:, 2 + h:3 + h])
                    last_i.then_inc(exp_ok, 1)
                    if not (first and l == 0):
                        act.wait_ge(pv_full, v)
                        need(act, o_done, v - 1)
                        copy_ot(oT_hi[:, :, :].rearrange("p k s -> p (k s)"), ot_hi_ok)
                    if l == 6:
                        swaps()
                    if l == 0:
                        for i, name in enumerate(("V0", "V1")):
                            act.wait_ge(pj_full, use(b, 0, name) + 1)
                            nc.scalar.activation(v_hi[:, i, :], proj[:, bank(0, name), :], ACT.Copy).then_inc(pj_act, 1)
                    if first:
                        for i in LATE.get(l, ()):
                            split_hi(i)
                    if not first:
                        post_act(b - 1, l)

            def post_act(p, l):
                if l == 3:
                    act.wait_ge(xnm_ok, p + 1)
                    for t in range(TT):
                        i = nc.scalar.activation(post[:, t, :], post[:, t, :], ACT.Exp, bias=xnm[:, t:t + 1],
                                                 accum_out=xsum[:, t:t + 1])
                    i.then_inc(xexp_ok, 1)
                if l == 6:
                    act.wait_ge(x3_full, p + 1)
                    copy_ot(post[:, :, :].rearrange("p k s -> p (k s)"), x3_ok)
                if l == 7:
                    act.wait_ge(lnm_ok, p + 1)
                    for t in range(TT):
                        i = nc.scalar.activation(logit[:, t, :], logit[:, t, :], ACT.Exp, bias=lnm[:, t:t + 1],
                                                 accum_out=lsum[:, t:t + 1])
                    i.then_inc(lexp_ok, 1)

            batches(act, body)
            V = B * STEPS
            act.wait_ge(pt_full, V)
            act.wait_ge(pv_full, V - 1)
            nc.scalar.activation(pT_hi[:, :, :], sc[:, 2:4, 0:384], ACT.Copy).then_inc(pt_hi_ok, 1)
            act.wait_ge(pv_full, V)
            act.wait_ge(o_done, V - 1)
            copy_ot(oT_hi[:, :, :].rearrange("p k s -> p (k s)"), ot_hi_ok)
            for l in range(STEPS):
                post_act(B - 1, l)
            for i in range(NT):
                act.wait_ge(tl["xt"], i + 1)
                nc.scalar.activation(sorted_T(0)[:, i * P:(i + 1) * P], sc[:, i % 4, 0:P], ACT.Copy)
                nc.scalar.activation(sorted_T(1)[:, i * P:(i + 1) * P], sc[:, i % 4, P:2 * P], ACT.Copy).then_inc(tl["xte"], 1)
            act.wait_ge(tl["reg"], 1)
            act.wait_ge(tl["xte"], NT)

            def stage(j, k):
                tile_col = act.value_load(seg_i[0:1, 0, bass.ds(j, 1)], min_val=0, max_val=(NT - 1) * P)
                if k is not None:
                    need(act, tl["seg"], j - 2)
                for kc in range(KC):
                    i = nc.scalar.activation(stage_x[:, k, kc, :], sorted_T(kc)[:, bass.ds(tile_col, P)], ACT.Copy)
                i.then_inc(tl["stage"], 1)
            segments(act, stage)

        @block.vector
        def _(dve):
            def tt(out_, a, b_, op):
                return nc.vector.tensor_tensor(out_, a, b_, op)

            def carrier():
                dve.sem_inc(pace, 1)

            class Chain:
                def __init__(self, s, per):
                    self.s, self.per, self.base, self.n = s, per, 0, 0

                def at(self, base):
                    self.base, self.n = base, 0

                def __call__(self, ins, carry=False):
                    self.n += 1
                    ins.then_inc(self.s, 1)
                    dve.wait_ge(self.s, self.base + self.n)
                    if carry:
                        carrier()

            def split_lo(i):
                dve.wait_ge(w_hi_ok, i + 1)
                nc.vector.tensor_tensor(w_lo[:, i, :], raw[SLICES[i]], w_hi[:, i, :].bitcast(fp32), ALU.subtract).then_inc(w_lo_ok, 1)

            def row_stats(chain, src, bn_, mv_, done):
                carrier()
                for t in range(TT):
                    i = nc.vector.bn_stats(bn_[:, t, :], src[:, t, :])
                chain(i, carry=True)
                for t in range(TT):
                    i = nc.vector.bn_aggr(mv_[:, t, :], bn_[:, t, :])
                i.then_inc(done, 1)

            def row_apply(src, dst, mv_, rstd_, done):
                for t in range(TT):
                    i = nc.vector.tensor_scalar(dst[:, t, :], src[:, t, :], mv_[:, t, 0:1], rstd_[:, t:t + 1], ALU.subtract, ALU.mult)
                i.then_inc(done, 1)

            LN_N = 1
            ln = Chain(d_ln, LN_N)

            def norm_stats(b):
                ln.at(b * LN_N)
                if isinstance(b, int) and b == 0:
                    dve.wait_ge(ld_x, 16)
                else:
                    dve.wait_ge(ld_x2, 16)
                row_stats(ln, rows[:, bass.ds(TT * b, TT), 0:H], bn, mv, mv_ok)

            def norm_apply(b):
                need(dve, xt_full, b)
                dve.wait_ge(rs_ok, b + 1)
                row_apply(rows[:, bass.ds(TT * b, TT), 0:H], xnrow, mv, rstd, xnr_ok)

            def xt_lo():
                return nc.vector.tensor_tensor(xnT_lo[:, :, :].rearrange("p k s -> p (k s)"), ot[:, :],
                                               xnT_hi[:, :, :].rearrange("p k s -> p (k s)").bitcast(fp32), ALU.subtract).then_inc(xt_lo_ok, 1)

            def times_cos(n_, bk, width, dst):
                dve.wait_ge(pj_act, n_ + 1)
                tt(dst, proj[:, bk, 0:width * S].rearrange("p (h s) -> p h s", h=width),
                   cos_sb[:, :].unsqueeze(1).to_broadcast([P, width, S]), ALU.mult).then_inc(pj_dve, 1)

            def chunk_sums(g, u, r):
                dve.wait_ge(rope_ok, r + 1)
                nc.vector.tensor_reduce(kt[:, g % 2, S:S + NCH], kt[:, g % 2, 0:S].rearrange("p (n c) -> p n c", c=CHUNK),
                                        AX.X, ALU.add).then_inc(km_ok, 1)

            norm_stats(0)
            nc.vector.memset(small[:, 64:80], 0.0).then_inc(su_dve, 1)
            dve.sem_inc(lg_ok, 1)
            norm_apply(0)
            dve.wait_ge(su_pool, 64)
            for i in range(2):
                split_lo(i)
            dve.wait_ge(xt_full, 1)
            dve.wait_ge(xt_hi_ok, 1)
            xt_lo()
            for i in range(2, 3):
                split_lo(i)
            dve.wait_ge(su_pe, 8)
            times_cos(0, 0, 1, kt[:, 0:1, 0:S])
            times_cos(1, 1, 2, qt[:, 0])
            times_cos(2, 0, 2, qt[:, 1])
            chunk_sums(0, 0, 0)
            split_lo(3)
            dve.wait_ge(ld_c, 128)
            nc.vector.tensor_copy(id_bf[:, :], id_sb[:, :])
            nc.vector.tensor_copy(cau_bf[:, :], cau_f[:, :]).then_inc(su_dve, 1)
            nc.vector.tensor_scalar(tern_flat, tern_flat, 2.0, 1.0, ALU.mult, ALU.min).then_inc(d_nm, 1)
            dve.wait_ge(d_nm, 1)
            nc.vector.tensor_scalar(tern_flat, tern_flat, -1.0, 12582912.0, ALU.max, ALU.add).then_inc(d_nm, 1)
            dve.wait_ge(d_nm, 2)
            nc.vector.tensor_scalar(tern_flat, tern_flat, 12582912.0, None, ALU.subtract).then_inc(su_dve, 1)
            dve.wait_ge(su_dve, 3)
            tt(tern[:, :, :], tern[:, :, :], fs_sb[:, :].unsqueeze(1).to_broadcast([P, KC, H]), ALU.mult).then_inc(su_dve, 1)
            for i in range(2):
                dve.wait_ge(su_pe, 6 + 2 * i)
                nc.vector.tensor_scalar(xscore[:, 4 * i:4 * i + 4, 0:S], sc[:, 2 * i:2 * i + 2, :].rearrange("p a (t n) -> p (a t) n", t=2), CTX ** -0.5, None, ALU.mult).then_inc(su_dve, 1)

            SM_N, NM_N = 5, 2
            sm, nrm = Chain(d_sm, SM_N), Chain(d_nm, NM_N)

            def softmax_max(v, l):
                q = l % 2
                s2 = sc[:, 2 * q:2 * q + 2, :]
                sm.at(v * SM_N)
                dve.wait_ge(sc_full, v + 1)
                sm(tt(gate, s2[:, :, 384:384 + NCAND], cand.unsqueeze(1).to_broadcast([P, 2, NCAND]), ALU.add))
                other = gate.unsqueeze(2).to_broadcast([P, 2, NCAND, NCAND])
                own = gate.unsqueeze(3).to_broadcast([P, 2, NCAND, NCAND])
                tt(cmp_gt, other, own, ALU.is_gt)
                sm(tt(cmp_eq, other, own, ALU.is_equal))
                for h in range(2):
                    i = tt(cmp_eq[:, h], cmp_eq[:, h], lower, ALU.mult)
                sm(i)
                sm(nc.vector.tensor_reduce(rank, cmp.rearrange("p (h n) m -> p h n m", h=2), AX.X, ALU.add))
                sm(nc.vector.scalar_tensor_tensor(selb[:, :, 0:NCAND], rank, float(TOPK - 1), ncand.unsqueeze(1).to_broadcast([P, 2, NCAND]),
                                                  ALU.is_ge, ALU.mult))
                nc.vector.tensor_reduce(mx[q][:, 0:2], s2[:, :, 0:P], AX.X, ALU.max)
                for h in range(2):
                    view = s2[:, h, P:384].rearrange("p (n c) -> p n c", c=CHUNK)
                    i = nc.vector.tensor_tensor_reduce(out=view, in0=view, in1=selb[:, h].unsqueeze(2).to_broadcast([P, NCH, CHUNK]),
                                                       scale=1.0, scalar=-3.0e38, op0=ALU.add, op1=ALU.max, accum_out=mx[q][:, 2 + h:3 + h])
                i.then_inc(d_nm, 1)
                dve.wait_ge(d_nm, 2 + NM_N * v + 1)
                nc.vector.tensor_scalar(nm[q], mx[q], -SCALE, None, ALU.mult).then_inc(nm_ok, 1)

            def normalise(v, l):
                q = l % 2
                dve.wait_ge(exp_ok, v + 1)
                nc.vector.reciprocal(rsum[q], sums[q]).then_inc(d_nm, 1)
                dve.wait_ge(d_nm, 2 + NM_N * v + 2)
                for h in range(2):
                    nc.vector.tensor_scalar(probs[:, h, 0:P], probs[:, h, 0:P], rsum[q][:, h:h + 1], None, ALU.mult)
                    i = nc.vector.tensor_scalar(probs[:, h, P:384], probs[:, h, P:384], rsum[q][:, 2 + h:3 + h], None, ALU.mult)
                i.then_inc(pn_ok, 1)

            def pt_lo(v1, q):
                dve.wait_ge(pt_hi_ok, v1 + 1)
                tt(pT_lo[:, :, :], sc[:, 2 * q:2 * q + 2, 0:384], pT_hi[:, :, :].bitcast(fp32), ALU.subtract).then_inc(pt_lo_ok, 1)

            def ot_lo(v1):
                dve.wait_ge(ot_hi_ok, v1 + 1)
                tt(oT_lo[:, :, :].rearrange("p k s -> p (k s)"), ot[:, :], oT_hi[:, :, :].rearrange("p k s -> p (k s)").bitcast(fp32),
                   ALU.subtract).then_inc(ot_lo_ok, 1)

            def body(b, first, last):
                for l in range(STEPS):
                    v = b * STEPS + l
                    softmax_max(v, l)
                    if not (first and l == 0):
                        pt_lo(v - 1, (l - 1) % 2)

                    def cosines():
                        if not (last and l >= 6):
                            for name in USES[l]:
                                if name == "K":
                                    g = (l // 2 + 1) % NG
                                    times_cos(use(b, l, name), bank(l, name), 1, kt[:, g % 2:g % 2 + 1, 0:S])
                                if name == "Q":
                                    times_cos(use(b, l, name), bank(l, name), 2, qt[:, l % 2])
                    if l == 6 and not last:
                        dve.wait_ge(xt_hi_ok, b + 2)
                        xt_lo()
                    if l != 6:
                        cosines()
                    normalise(v, l)
                    if not (first and l == 0):
                        ot_lo(v - 1)
                    if l == 6:
                        cosines()
                    if l == 0:
                        for i, name in enumerate(("V0", "V1")):
                            dve.wait_ge(pj_act, use(b, 0, name) + 1)
                            tt(v_lo[:, i, :], proj[:, bank(0, name), :], v_hi[:, i, :].bitcast(fp32), ALU.subtract).then_inc(pj_dve, 1)
                    if "K" in USES[l] and not (last and l >= 6):
                        chunk_sums((l // 2 + 1) % NG, 4 * b + l // 2 + 1, rope(b, l, "K"))
                    if first:
                        for i in LATE.get(l, ()):
                            split_lo(i)
                    if l == 3 and not last:
                        norm_stats(b + 1)
                    if l == 4 and not last:
                        norm_apply(b + 1)
                    if not first:
                        post_dve(b - 1, l)

            POST_N = 8
            pc = Chain(d_post, POST_N)

            def post_dve(p, l):
                base = p * POST_N
                r2 = rows[:, bass.ds(TT * p, TT), 0:H]
                if l == 1:
                    dve.wait_ge(o_done, STEPS * (p + 1))
                    tt(r2, r2, y[:, :, :], ALU.add).then_inc(x1_ok, 1)
                    pc.at(base)
                    dve.wait_ge(x1_ok, p + 1)
                    row_stats(pc, r2, bn2, mv2, mv2_ok)
                if l == 0:
                    if isinstance(p, int) and p == 0 or not isinstance(p, int):
                        dve.wait_ge(p_bias, 32)
                    tt(bias_x[:, :, :], smask_sb[:, :, :], kmask_sb[:, bass.ds(p, 1), :].to_broadcast([P, TT, S]), ALU.max).then_inc(mb_ok, 1)
                    dve.wait_ge(mb_ok, 2 * p + 1)
                    nc.vector.tensor_scalar(bias_x[:, :, :], bias_x[:, :, :], NEG, None, ALU.mult).then_inc(mb_ok, 1)
                if l == 2:
                    dve.wait_ge(rs2_ok, 2 * p + 1)
                    row_apply(r2, post, mv2, rstd2, qc_ok)
                if l == 3:
                    dve.wait_ge(xs_ok, 2 * p + 2)
                    pc.at(base + 1)
                    pc(nc.vector.tensor_reduce(xmx, post[:, :, :], AX.X, ALU.max))
                    nc.vector.tensor_scalar(xnm, xmx, -1.0, None, ALU.mult).then_inc(xnm_ok, 1)
                if l == 4:
                    dve.wait_ge(xexp_ok, p + 1)
                    pc.at(base + 2)
                    pc(nc.vector.tensor_scalar(xany, xmx, NEG / 2, None, ALU.is_gt))
                    pc(tt(xsum, xsum, xany, ALU.mult))
                    pc(nc.vector.reciprocal(xrs, xsum))
                    pc(tt(xrs, xrs, xany, ALU.mult))
                    for t in range(TT):
                        i = nc.vector.scalar_tensor_tensor(rows[:, bass.ds(TT * p + t, 1), 0:H].rearrange("p a n -> p (a n)"), post[:, t, :], xrs[:, t:t + 1],
                                                           rows[:, bass.ds(TT * p + t, 1), 0:H].rearrange("p a n -> p (a n)"), ALU.mult, ALU.add)
                    i.then_inc(xm_ok, 1)
                    dve.wait_ge(xm_ok, p + 1)
                    row_stats(pc, r2, bn2, mv2, mv2_ok)
                if l == 5:
                    dve.wait_ge(rs2_ok, 2 * p + 2)
                    row_apply(r2, post, mv2, rstd2, xn3_ok)
                if l == 7:
                    dve.wait_ge(lg_full, p + 1)
                    nc.vector.tensor_copy(logit, ot[:, 0:TT * E_N].rearrange("p (t e) -> p t e", t=TT)).then_inc(lg_ok, 1)
                    dve.wait_ge(lg_ok, p + 2)
                    carrier()
                    for t in range(TT):
                        nc.vector.max(lg8x[:, t, :], logit[:, t, :]).then_inc(lg_m, 1)
                    dve.wait_ge(lg_m, 2 * p + 2)
                    nc.vector.tensor_scalar(lnm, lg8x[:, :, 0], -1.0, None, ALU.mult).then_inc(d_post, 1)
                    dve.wait_ge(d_post, base + 8)
                    carrier()
                    for t in range(TT):
                        nc.vector.max_index(idxx[:, t, :], lg8x[:, t, :], logit[:, t, :]).then_inc(lg_x, 1)
                    dve.wait_ge(lg_x, 2 * p + 2)
                    dve.wait_ge(d_post, base + 8)
                    nc.vector.tensor_scalar(rows[:, bass.ds(TT * p, TT), 256:257].rearrange("p t a -> p (t a)"), idxx[:, :, 0],
                                            float(E_N - 1), None, ALU.min).then_inc(lnm_ok, 1)
                    nc.vector.tensor_copy(rows[:, bass.ds(TT * p, TT), 259:260].rearrange("p t a -> p (t a)"), mv2[:, :, 0])
                    nc.vector.tensor_copy(rows[:, bass.ds(TT * p, TT), 260:261].rearrange("p t a -> p (t a)"), rstd2)
                    dve.wait_ge(lexp_ok, p + 1)
                    nc.vector.reciprocal(rows[:, bass.ds(TT * p, TT), 257:258].rearrange("p t a -> p (t a)"), lsum).then_inc(row_ok, 1)

            batches(dve, body)
            V = B * STEPS
            pt_lo(V - 1, 1)
            ot_lo(V - 1)
            for l in range(STEPS):
                post_dve(B - 1, l)
            tc = Chain(tl["dve"], 0)
            dve.wait_ge(row_ok, B)
            tc(nc.vector.tensor_copy(rows[:, :, 258], token))
            tc(nc.vector.memset(rows[:, :, 261:264], 0.0))
            tc(nc.vector.memset(zero256, 0.0))
            oh3 = oh.rearrange("p (i e) -> p i e", i=NT)
            tt(oh3, rows[:, :, 256].unsqueeze(2).to_broadcast([P, NT, E_N]), iota_e.unsqueeze(1).to_broadcast([P, NT, E_N]),
               ALU.is_equal).then_inc(tl["oh"], 1)
            dve.wait_ge(tl["pe"], 2)
            cnt = post[:, 0, :].rearrange("p (e i) -> p e i", e=E_N)
            run = post[:, 1, :]
            tc(nc.vector.tensor_copy(cnt, proj[:, 1, 0:256].rearrange("p (i e) -> p e i", i=NT)))
            tc(nc.vector.tensor_tensor_scan(run, post[:, 0, :], zero256, 0.0, ALU.add, ALU.add))
            tc(tt(base, run, post[:, 0, :], ALU.subtract))
            wk1 = probs[:, 0, 0:256].rearrange("p (i e) -> p i e", i=NT)
            tc(tt(wk1, proj[:, 0, 0:256].rearrange("p (i e) -> p i e", i=NT), base.rearrange("p (e i) -> p i e", e=E_N), ALU.add))
            tc(tt(wk1, wk1, oh3, ALU.mult))
            place = small[:, 0:NT]
            tc(nc.vector.tensor_reduce(place, wk1, AX.X, ALU.add))
            nc.vector.tensor_copy(slot_u[:, :], place).then_inc(tl["slot"], 1)
            edge_c = probs[:, 1, 0:7 * E_N].rearrange("p (i e) -> p i e", i=NT - 1)
            incl = run.rearrange("p (e i) -> p e i", e=E_N)[:, :, NT - 1]
            tc(tt(edge_c, incl.unsqueeze(1).to_broadcast([P, NT - 1, E_N]), bound.unsqueeze(2).to_broadcast([P, NT - 1, E_N]), ALU.is_lt))
            edge = small[:, 16:23]
            tc(nc.vector.tensor_reduce(edge, edge_c, AX.X, ALU.add))
            tc(tt(edge, edge, tile1, ALU.add))
            seg_c = post[:, :, :].rearrange("p a b -> p (a b)")[:, 0:SEGS * (NT - 1)].rearrange("p (j i) -> p j i", i=NT - 1)
            tc(tt(seg_c, edge.unsqueeze(1).to_broadcast([P, SEGS, NT - 1]), iota_j.unsqueeze(2).to_broadcast([P, SEGS, NT - 1]), ALU.is_le))
            tile_f = small[:, 32:32 + SEGS]
            tc(nc.vector.tensor_reduce(tile_f, seg_c, AX.X, ALU.add))
            exp_f = small[:, 80:80 + SEGS]
            tc(tt(exp_f, iota_j, tile_f, ALU.subtract))
            nc.vector.tensor_scalar(seg_i[:, 0, 0:SEGS], tile_f, float(P), None, ALU.mult)
            nc.vector.tensor_scalar(seg_i[:, 2, 0:SEGS], tile_f, float(ROW), None, ALU.mult)
            nc.vector.tensor_copy(seg_i[:, 1, 0:SEGS], exp_f)
            tc(nc.vector.scalar_tensor_tensor(seg_f[:, :], tile_f, float(E_N), exp_f, ALU.mult, ALU.add))
            tc(nc.vector.tensor_copy(seg_i[:, 3, 0:SEGS], seg_f[:, :]))
            nc.vector.nop().then_inc(tl["reg"], 1)
            xns = xnrow
            for i in range(NT):
                dve.wait_ge(tl["back"], 16)
                need(dve, tl["xt"], i - 1)
                nc.vector.tensor_scalar(xns[:, i % 2, :], xscore[:, i, 0:H], xscore[:, i, 259:260], xscore[:, i, 260:261],
                                        ALU.subtract, ALU.mult).then_inc(tl["xn"], 1)
            m3 = mask_w.rearrange("p (i e) -> p i e", i=NT)
            tc(tt(m3, xscore[:, :, 256].unsqueeze(2).to_broadcast([P, NT, E_N]), iota_e.unsqueeze(1).to_broadcast([P, NT, E_N]), ALU.is_equal))
            tc(tt(m3, m3, xscore[:, :, 257].unsqueeze(2).to_broadcast([P, NT, E_N]), ALU.mult))
            tc(nc.vector.tensor_copy(tok_u[:, :], xscore[:, :, 258]))
            while tc.n < 30:
                tc(nc.vector.memset(small[:, 500:501], 0.0))

            xs_flat = xscore[:, :, :].rearrange("p i n -> p (i n)")

            def accumulate(j, k):
                row_col = dve.value_load(seg_i[0:1, 2, bass.ds(j, 1)], min_val=0, max_val=(NT - 1) * ROW)
                m_col = dve.value_load(seg_i[0:1, 3, bass.ds(j, 1)], min_val=0, max_val=NT * E_N - 1)
                dve.wait_ge(tl["seg"], j + 1)
                need(dve, tl["acc"], j)
                acc = xs_flat[:, bass.ds(row_col, H)]
                nc.vector.scalar_tensor_tensor(acc, sc[:, k, 0:H], mask_w[:, bass.ds(m_col, 1)], acc, ALU.mult, ALU.add).then_inc(tl["acc"], 1)
            segments(dve, accumulate)

        @block.tensor
        def _(pe):
            mm = nc.tensor.matmul

            pe.wait_ge(ld_c, 128)
            for i in range(4):
                mm(sc[0:CTX, i, :], xw_sb[:, i % 2, :], qt[0:CTX, :, :, :].rearrange("p a b c -> p (a b c)")[:, (i // 2) * 512:(i // 2 + 1) * 512],
                   start=True, stop=True).then_inc(su_pe, 1)
            pe.wait_ge(su_pool, 64)
            pe.wait_ge(xnr_ok, 1)

            def transposes(src):
                for t in range(TT):
                    for kc in range(KC):
                        i = nc.tensor.transpose(ot[:, kc * S + t * P:kc * S + (t + 1) * P], src[:, t, kc * P:(kc + 1) * P], id_sb[:, :])
                return i
            transposes(xnrow).then_inc(xt_full, 1)
            pe.wait_ge(su_act, 4)
            for i in range(NT):
                bb, t = i // TT, i % TT
                xs = mm(sc[:, i // 2, (i % 2) * S:(i % 2 + 1) * S], xqk[:, 0, bb * S + t * P:bb * S + (t + 1) * P],
                        xqk[:, 1, bb * S:(bb + 1) * S], start=True, stop=True)
                if i % 2:
                    xs.then_inc(su_pe, 1)

            def project(name, b, l, n_, bk, g):
                need(pe, pj_act, n_ - 1)
                need(pe, pj_dve, n_ - 1)
                if name == "K":
                    for n, (a, c) in enumerate(PARTS):
                        for kc in range(KC):
                            i = mm(proj[:, bk, 0:S], w("K", a)[:, kc * 512 + g * D:kc * 512 + (g + 1) * D],
                                   (xnT_hi if c == 0 else xnT_lo)[:, kc, :], start=(n + kc == 0), stop=(n == 2 and kc == KC - 1))
                elif name == "Q":
                    for h in range(2):
                        hh = 2 * (l % 2) + h
                        for n, (a, c) in enumerate(PARTS):
                            for kc in range(KC):
                                i = mm(proj[:, bk, h * S:(h + 1) * S], w(f"Q{g}", a)[:, kc * 512 + hh * D:kc * 512 + (hh + 1) * D],
                                       (xnT_hi if c == 0 else xnT_lo)[:, kc, :], start=(n + kc == 0), stop=(n == 2 and kc == KC - 1))
                else:
                    t = int(name[1])
                    for n, (a, c) in enumerate(PARTS):
                        for kc in range(KC):
                            i = mm(proj[:, bk, :], (xnT_hi if c == 0 else xnT_lo)[:, kc, t * P:(t + 1) * P],
                                   w("V", a)[:, kc * 512:(kc + 1) * 512], start=(n + kc == 0), stop=(n == 2 and kc == KC - 1))
                i.then_inc(pj_full, 1)

            def scores(v, l, u):
                q, g = l % 2, l // 2
                r = 2 + v if isinstance(v, int) and v < 2 else None
                need(pe, pt_hi_ok, v - 1)
                need(pe, pt_lo_ok, v - 1)
                for h in range(2):
                    bk = sc[:, 2 * q + h, :]
                    mm(bk[:, 0:P], qt[:, q, h, 0:P], kt[:, g % 2, 0:P], start=True, stop=False)
                    mm(bk[:, 0:P], id_bf[:, :], cau_bf[:, :], start=False, stop=True)
                    mm(bk[:, P:P + S + NCH], qt[:, q, h, P:S], kt[:, g % 2, :], start=True, stop=False)
                    i = mm(bk[:, S:S + P], id_bf[:, :], cau_bf[:, :], start=False, stop=True)
                i.then_inc(sc_full, 1)

            def transpose_probs(v, q):
                pe.wait_ge(pn_ok, v + 1)
                for h in range(2):
                    for n in range(3):
                        i = nc.tensor.transpose(sc[:, 2 * q + h, n * P:(n + 1) * P], probs[:, h, n * P:(n + 1) * P], id_sb[:, :])
                i.then_inc(pt_full, 1)

            def weigh(v, g):
                pe.wait_ge(pt_lo_ok, v + 1)
                pe.wait_ge(pt_hi_ok, v + 1)
                need(pe, ot_hi_ok, v)
                need(pe, ot_lo_ok, v)
                for h in range(2):
                    for n, (a, c) in enumerate(PARTS):
                        vv, pp = (v_hi, v_lo)[a], (pT_hi, pT_lo)[c]
                        mm(ot[:, h * S:(h + 1) * S], vv[:, 0, g * D:(g + 1) * D], pp[:, h, 0:S], start=(n == 0), stop=False)
                        i = mm(ot[:, h * S + P:(h + 1) * S], vv[:, 1, g * D:(g + 1) * D], pp[:, h, S:384], start=False, stop=(n == 2))
                i.then_inc(pv_full, 1)

            def output(v, l):
                pe.wait_ge(ot_hi_ok, v + 1)
                pe.wait_ge(ot_lo_ok, v + 1)
                for h in range(2):
                    hh = 2 * (l % 2) + h
                    for t in range(TT):
                        for n, (a, c) in enumerate(PARTS):
                            i = mm(y[:, t, :], (oT_hi, oT_lo)[a][:, h, t * P:(t + 1) * P], w(f"O{l // 2}", c)[:, hh * H:(hh + 1) * H],
                                   start=(l == 0 and h == 0 and t == 0 and n == 0), stop=(l == 7 and h == 1 and n == 2), skip_group_check=True)
                i.then_inc(o_done, 1)

            pe.wait_ge(w_lo_ok, 2)
            pe.wait_ge(xt_lo_ok, 1)
            project("K", 0, 0, 0, 0, 0)
            project("Q", 0, 0, 1, 1, 0)
            project("Q", 0, 1, 2, 0, 0)

            def body(b, first, last):
                for l in range(STEPS):
                    v = b * STEPS + l

                    def projections():
                        if last and l >= 6:
                            return
                        for name in USES[l]:
                            if name[0] == "V":
                                continue
                            g = ((l + 2) // 2) % NG
                            if first:
                                pe.wait_ge(w_lo_ok, SLICES.index(f"Q{g}") + 1)
                            project(name, b, l, use(b, l, name), bank(l, name), g)
                    if first and l < 2:
                        pe.wait_ge(rope_ok, 2 + l)
                    else:
                        lv = (l - 2) % STEPS
                        pe.wait_ge(rope_ok, rope(b if l >= 2 else b - 1, lv, "Q") + 1)
                    pe.wait_ge(km_ok, NG * b + l // 2 + 1)
                    if first and l == 0:
                        pe.wait_ge(su_dve, 6)
                    scores(v, l, None)
                    if l == 6 and not last:
                        pe.wait_ge(xnr_ok, b + 2)
                        pe.wait_ge(ot_hi_ok, v - 1)
                        pe.wait_ge(ot_lo_ok, v - 1)
                        transposes(xnrow).then_inc(xt_full, 1)
                    if not (first and l == 0):
                        transpose_probs(v - 1, (l - 1) % 2)
                    if l != 6:
                        projections()
                    if not (first and l < 2):
                        if first and l % 2 == 0:
                            pe.wait_ge(w_lo_ok, SLICES.index(f"O{(l - 2) // 2}") + 1)
                        if l == 2:
                            need(pe, x1_ok, b)
                        output(v - 2, (l - 2) % STEPS)
                    if not (first and l == 0):
                        if l == 6 and not last:
                            pe.wait_ge(xt_hi_ok, b + 2)
                            pe.wait_ge(xt_lo_ok, b + 2)
                        if not first and l == 7:
                            pe.wait_ge(x3_ok, b)
                        if not first and l == 0 and not (isinstance(b, int) and b == 1):
                            pe.wait_ge(lg_ok, b)
                        if first and l == 1:
                            pass
                        if l == 1:
                            pe.wait_ge(pj_dve, use(b, 0, "V1") + 1)
                            pe.wait_ge(pj_act, use(b, 0, "V1") + 1)
                        weigh(v - 1, ((l - 1) % STEPS) // 2)
                    if l == 6:
                        if not last:
                            pe.wait_ge(xt_hi_ok, b + 2)
                            pe.wait_ge(xt_lo_ok, b + 2)
                        projections()
                    if first and l == 7:
                        pe.wait_ge(w_lo_ok, len(SLICES))
                    if l == 0:
                        if first:
                            pe.wait_ge(w_lo_ok, 3)
                        for name in ("V0", "V1"):
                            project(name, b, 0, use(b, 0, name), bank(0, name), 0)
                    if not first:
                        post_pe(b - 1, l, v)

            def post_pe(p, l, v):
                if l == 6:
                    pe.wait_ge(xn3_ok, p + 1)
                    pe.wait_ge(ot_hi_ok, v)
                    pe.wait_ge(ot_lo_ok, v)
                    transposes(post).then_inc(x3_full, 1)
                if l == 7:
                    pe.wait_ge(x3_ok, p + 1)
                    pe.wait_ge(ot_hi_ok, v)
                    pe.wait_ge(ot_lo_ok, v)
                    for t in range(TT):
                        for kc in range(KC):
                            i = mm(ot[:, t * E_N:(t + 1) * E_N], post[:, kc, t * P:(t + 1) * P], rw_sb[:, kc, :], start=(kc == 0), stop=(kc == KC - 1))
                    i.then_inc(lg_full, 1)

            batches(pe, body)
            V = B * STEPS
            transpose_probs(V - 1, 1)
            output(V - 2, 6)
            pe.wait_ge(lg_ok, B)
            weigh(V - 1, NG - 1)
            output(V - 1, 7)
            for l in range(STEPS):
                post_pe(B - 1, l, V)
            pe.wait_ge(tl["oh"], 1)
            pe.wait_ge(p_bias, 48)
            mm(proj[:, 0, 0:256], tri_sb[:, 0, :], oh, start=True, stop=True).then_inc(tl["pe"], 1)
            mm(proj[:, 1, 0:256], tri_sb[:, 1, :], oh, start=True, stop=True).then_inc(tl["pe"], 1)
            for i in range(NT):
                pe.wait_ge(tl["xn"], i + 1)
                need(pe, tl["xte"], i - 3)
                for kc in range(KC):
                    t_ = nc.tensor.transpose(sc[:, i % 4, kc * P:(kc + 1) * P], xnrow[:, i % 2, kc * P:(kc + 1) * P], id_sb[:, :])
                t_.then_inc(tl["xt"], 1)
            pe.wait_ge(tl["xte"], NT)
            pe.wait_ge(tl["reg"], 1)
            pe.wait_ge(p_w, E_N)

            def segment(j, k):
                ex = pe.value_load(seg_i[0:1, 1, bass.ds(j, 1)], min_val=0, max_val=E_N - 1)
                pe.wait_ge(tl["stage"], j + 1)
                need(pe, tl["acc"], j - 2)
                for kc in range(KC):
                    i = mm(sc[:, k, 0:H], stage_x[:, k, kc, :], experts[:, bass.ds(ex, 1), kc, :].rearrange("p a n -> p (a n)"),
                           start=(kc == 0), stop=(kc == KC - 1))
                i.then_inc(tl["seg"], 1)
            segments(pe, segment)


def kernel(x, ctx_512, mask_SxS2_bk1, mask_BxS2_bf0, L0_attn_wq, L0_attn_wk, L0_attn_wv, L0_attn_wo, L0_xattn_Wq,
           L0_xattn_bq, L0_xattn_Wk, L0_xattn_bk, L0_ffn_weight, L0_ffn_scale, L0_ffn_expert_masks, L0_ffn_router_w):
    import numpy as np
    import concourse.bacc as bacc
    from concourse.bass_utils import run_bass_kernel_spmd

    def lay(a):
        return np.ascontiguousarray(a)

    def bits(a):
        return lay(a)

    inv = (1.0 / np.float32(10000.0) ** (np.arange(0, D, 2, dtype=np.float32) / np.float32(D))).astype(np.float32)
    ang = (np.arange(S, dtype=np.float32)[:, None] * inv[None, :]).astype(np.float32)
    cos, sin = np.cos(ang).astype(np.float32).T, np.sin(ang).astype(np.float32).T
    p_, f_ = np.arange(P)[:, None], np.arange(P)[None, :]
    con = np.zeros((P, 256), np.float32)
    past = np.arange(NCAND)[None, :] < (P // CHUNK + p_ // CHUNK)
    con[:, 0:7] = np.where(past, 0.0, NEG)
    con[:, 8:15] = np.where(past, NEG, 0.0)
    n_ = np.arange(NCAND)
    con[:, 16:65] = (n_[None, :] < n_[:, None]).astype(np.float32).reshape(1, -1)
    con[:, 72:104] = np.arange(E_N)
    con[:, 104:104 + SEGS] = np.arange(SEGS)
    con[:, 144:151] = P * np.arange(1, NT)
    con[:, 152:159] = np.arange(1, NT)
    con[:, 176:178], con[:, 178:180] = EPS, -0.5
    con[:, 160:168] = P * np.arange(NT)[None, :] + p_
    tri = np.stack([(p_ < f_) * 1.0, np.ones((P, P))], 1).astype(np.float32)

    def by_slices(a, cols):
        return lay(a.reshape(KC, P, -1, cols).transpose(1, 2, 0, 3).reshape(P, -1))

    arrays = {
        "x": lay(x),
        "ctxT": lay(ctx_512.reshape(B * S, CTX).T),
        "smask": bits(mask_SxS2_bk1),
        "kmask": bits(mask_BxS2_bf0),
        "wq": by_slices(L0_attn_wq, HG * D),
        "wk": by_slices(L0_attn_wk, NG * D),
        "wv": by_slices(L0_attn_wv, NG * D),
        "wo": lay(L0_attn_wo.reshape(NH, D, H).transpose(1, 0, 2).reshape(D, NH * H)),
        "xwq": lay(L0_xattn_Wq.T),
        "xwk": lay(L0_xattn_Wk.T),
        "xbias": lay(np.stack([L0_xattn_bq, L0_xattn_bk], 1)),
        "ffw": by_slices(L0_ffn_weight.T, H),
        "ffscale": lay(L0_ffn_scale),
        "masks": lay(L0_ffn_expert_masks.reshape(E_N, H, KC, P).transpose(3, 0, 2, 1).reshape(P, E_N * KC * H)),
        "rw": by_slices(L0_ffn_router_w.T, E_N),
        "cosT": lay(np.concatenate([cos, cos], 0)),
        "sinT": lay(np.concatenate([-sin, sin], 0)),
        "ident": np.eye(P, dtype=np.float32),
        "consts": con,
        "tri": lay(tri.reshape(P, 2 * P)),
        "causal": np.where(f_ <= p_, 0.0, NEG).astype(np.float32),
    }
    nc = bacc.Bacc("TRN2", target_bir_lowering=False, num_devices=1, dynamic_dma_scratch_size=8192)
    feeds, args = {}, []
    for name, a in arrays.items():
        feeds[f"in_{name}_dram"] = a
        args.append(nc.dram_tensor(f"in_{name}_dram", a.shape, mybir.dt.from_np(a.dtype), kind="ExternalInput").ap())
    out = nc.dram_tensor("out_0_dram", (B * S, H), mybir.dt.float32, kind="ExternalOutput").ap()
    scratch = nc.dram_tensor("scratch_rows", (B * S, ROW), mybir.dt.float32, kind="Internal").ap()
    program(nc, *args, out, scratch)
    r = run_bass_kernel_spmd(nc, [feeds], core_ids=[0])
    return r.results[0]["out_0_dram"].reshape(B, S, H)
```

```python
import concourse.bass as bass
from concourse import mybir
from contextlib import ExitStack

B, S, H = 4, 256, 256
NH, NG, D = 16, 4, 128
HG = NH // NG
CHUNK, NCH, TOPK = 32, 8, 4
E_N = 32
CTX = 64
P = 128
KC = H // P
TT = S // P
NT = B * TT
STEPS = NG * 2
SEGS = NT + E_N - 1
SEG_ROWS = (SEGS + 1) // 4
TC_END = 16
ROW = 264
EPS = 1e-5
SCALE = float(D) ** -0.5
NEG = -1.0e30
MARK, PICKED = 2.0e38, 3.0e38
NCAND = NCH - 1

USES = {0: ["K", "Q", "V0", "V1"], 1: ["Q"], 2: ["K", "Q"], 3: ["Q"],
        4: ["K", "Q"], 5: ["Q"], 6: ["K", "Q"], 7: ["Q"]}
USE0 = {l: sum(len(USES[m]) for m in range(l)) for l in range(9)}
ROPE0 = {l: sum(u in ("K", "Q") for m in range(l) for u in USES[m]) for l in range(9)}
N_USE, N_ROPE, PRE = USE0[8], ROPE0[8], 3
SLICES = ["K", "Q0", "V", "Q1", "O0", "Q2", "Q3", "O1", "O2", "O3"]
EARLY = 4
LATE = {0: [4, 5], 2: [6, 7], 4: [8], 5: [9]}
RAW_E = 12


def program(nc, x, ctxT, smask, kmask, wq, wk, wv, wo, xw, ffw, ffscale, masks, tables, consts, tri, causal, out, scratch):
    fp32, f32r, bf16 = mybir.dt.float32, mybir.dt.float32r, mybir.dt.bfloat16
    u32, i32, u8 = mybir.dt.uint32, mybir.dt.int32, mybir.dt.uint8
    ALU, ACT, AX = mybir.AluOpType, mybir.ActivationFunctionType, mybir.AxisListType

    with ExitStack() as ctx:
        def sb(name, shape, dt=fp32):
            return ctx.enter_context(nc.sbuf_tensor(name, shape, dt))

        def pb(name, shape, dt=fp32):
            return ctx.enter_context(nc.psum_tensor(name, shape, dt))

        sems = {}

        def sem(name):
            sems[name] = ctx.enter_context(nc.semaphore(name))
            return sems[name]

        experts = sb("experts", [P, E_N, KC, H])
        exp_flat = experts[:, :, :, :].rearrange("p e k o -> p (e k o)")
        raw0 = RAW_E * KC * H
        raw = {}
        for i, name in enumerate(SLICES):
            raw[name] = exp_flat[:, raw0 + i * 1024:raw0 + (i + 1) * 1024]
        w_hi = sb("w_hi", [P, len(SLICES), 1024], f32r)
        w_lo = sb("w_lo", [P, len(SLICES), 1024], f32r)
        rows = sb("rows", [P, NT, ROW])
        xscore = sb("xscore", [P, NT, ROW])
        xnrow = sb("xnrow", [P, TT, H])
        xnT_hi = sb("xnT_hi", [P, KC, S], f32r)
        xnT_lo = sb("xnT_lo", [P, KC, S], f32r)
        qs = sb("qs", [P, 2, 2, 2, S])
        qt, swap = qs[:, 0], qs[:, 1]
        kt = sb("kt", [P, 2, S + NCH])
        values = sb("values", [P, TT, NG * D])
        pp = sb("pp", [P, 4, 384])
        probs, pT = pp[:, 0:2], pp[:, 2:4]
        oT_hi = sb("oT_hi", [P, 2, S], f32r)
        oT_lo = sb("oT_lo", [P, 2, S], f32r)
        tab_sb = sb("tab_sb", [P, 4, S])
        cos_sb, sin_sb, cosq_sb, sinq_sb = (tab_sb[:, i] for i in range(4))
        con_all = sb("con_all", [P, 256 + P])
        con, id_sb = con_all[:, 0:256], con_all[:, 256:256 + P]
        id_bf = sb("id_bf", [P, P], bf16)
        cau_bf = sb("cau_bf", [P, P], bf16)
        post = sb("post", [P, TT, H])
        bias_x = sb("bias_x", [P, TT, H], bf16)
        smask_sb = sb("smask_sb", [P, TT, S], u8)
        kmask_sb = sb("kmask_sb", [P, B, S], u8)
        small = sb("small", [P, 512])
        xw_all = sb("xw_all", [CTX, 2 * CTX + 2])
        xw_sb = xw_all[:, 0:2 * CTX].rearrange("p (a n) -> p a n", a=2)
        xb_sb = xw_all[:, 2 * CTX:2 * CTX + 2]
        idx8 = sb("idx8", [P, 8], u32)

        ffn_sb = sb("ffn_sb", [P, KC * H + KC * E_N])
        tern = ffn_sb[:, 0:KC * H].rearrange("p (k o) -> p k o", k=KC)
        rw_sb = ffn_sb[:, KC * H:KC * (H + E_N)].rearrange("p (k e) -> p k e", k=KC)
        tern_flat = tern[:, :, :].rearrange("p k o -> p (k o)")
        fs_sb = sb("fs_sb", [P, H])
        ctx_sb = experts[0:CTX, 6:8, :, :].rearrange("p e k o -> p (e k o)")
        slot_u = sb("slot_u", [P, NT], u32)
        tok_u = sb("tok_u", [P, NT], u32)
        seg_i = sb("seg_i", [P, 4, 48], i32)
        tri_sb = sin_sb[:, :].rearrange("p (a b) -> p a b", a=2)
        cau_f = probs[:, 1, 0:P]
        lg8x = sb("lg8x", [P, TT, 8])
        idxx = sb("idxx", [P, TT, 8], u32)
        xqk = experts[0:CTX, 8:12, :, :].rearrange("p e k o -> p (e k o)").rearrange("p (a n) -> p a n", a=2)
        oh = xnrow[:, 0, :]
        base = xnrow[:, 1, :]
        zero256 = cos_sb[:, :]
        sortedT = qs[:, :, :, :, :].rearrange("p a b c s -> p a (b c s)")
        expT = values[:, :, :].rearrange("p t n -> p (t n)")
        stage_x = pp[:, :, :].rearrange("p a n -> p (a n)")[:, 0:4 * H].rearrange("p (s k n) -> p s k n", s=4, k=KC)

        cand = con[:, 0:7]
        ncand = con[:, 8:15]
        iota_e = con[:, 72:104]
        iota_j = con[:, 104:104 + SEGS]
        bound = con[:, 144:151]
        tile1 = con[:, 152:159]
        eps2, neg_half2 = con[:, 176:178], con[:, 178:180]
        token = con[:, 160:168]

        nm = [small[:, 4 * i:4 * i + 4] for i in range(2)]
        top = small[:, 408:424].rearrange("p (h n) -> p h n", h=2)
        pick = small[:, 424:440].rearrange("p (h n) -> p h n", h=2)
        sums = [small[:, 16 + 4 * i:20 + 4 * i] for i in range(2)]
        rsum = [small[:, 24 + 4 * i:28 + 4 * i] for i in range(2)]
        gate = small[:, 32:64].rearrange("p (h n) -> p h n", h=2)
        mark = small[:, 208:240].rearrange("p (h n) -> p h n", h=2)
        selb = small[:, 64:80].rearrange("p (h n) -> p h n", h=2)
        bn = small[:, 80:92].rearrange("p (t s) -> p t s", t=2)
        mv = small[:, 92:96].rearrange("p (t s) -> p t s", t=2)
        rstd = small[:, 96:98]
        bn2 = small[:, 100:112].rearrange("p (t s) -> p t s", t=2)
        mv2 = small[:, 112:116].rearrange("p (t s) -> p t s", t=2)
        rstd2 = small[:, 116:118]
        xmx, xnm, xsum, xrs = (small[:, 120 + 2 * i:122 + 2 * i] for i in range(4))
        xany = small[:, 128:130]
        logit = small[:, 136:200].rearrange("p (t e) -> p t e", t=2)
        lnm, lsum = small[:, 200:202], small[:, 202:204]

        proj = pb("proj", [P, 2, 512])
        sc = pb("sc", [P, 4, 512])
        ot = pb("ot", [P, 512])
        y = pb("y", [P, TT, H])
        y_flat = y[:, :, :].rearrange("p t n -> p (t n)")
        sc_flat = sc[:, :, :].rearrange("p b n -> p (b n)")

        ld_x, ld_w, ld_c, ld_m = sem("ld_x"), [sem(f"ld_w{i}") for i in range(len(SLICES))], sem("ld_c"), sem("ld_m")
        w_hi_ok, w_lo_ok = sem("w_hi_ok"), sem("w_lo_ok")
        xnr_ok, xt_full, xt_hi_ok, xt_lo_ok = sem("xnr_ok"), sem("xt_full"), sem("xt_hi_ok"), sem("xt_lo_ok")
        pj_full, pj_act, pj_dve = sem("pj_full"), sem("pj_act"), sem("pj_dve")
        pool_t2, rope_ok, km_ok = sem("pool_t2"), sem("rope_ok"), sem("km_ok")
        rc_ok = sem("rc_ok")
        sc_full, nm_ok, exp_ok, pn_ok = sem("sc_full"), sem("nm_ok"), sem("exp_ok"), sem("pn_ok")
        pt_full, pt_ok = sem("pt_full"), sem("pt_ok")
        pv_full, ot_hi_ok, ot_lo_ok, o_done = sem("pv_full"), sem("ot_hi_ok"), sem("ot_lo_ok"), sem("o_done")
        d_sm, d_nm, d_ln, d_post = sem("d_sm"), sem("d_nm"), sem("d_ln"), sem("d_post")
        x1_ok, qc_ok, xm_ok, xs_ok = sem("x1_ok"), sem("qc_ok"), sem("xm_ok"), sem("xs_ok")
        xnm_ok, xexp_ok, xn3_ok, x3_full, x3_ok = sem("xnm_ok"), sem("xexp_ok"), sem("xn3_ok"), sem("x3_full"), sem("x3_ok")
        lg_m, lg_x = sem("lg_m"), sem("lg_x")
        lg_full, lg_ok, lnm_ok, lexp_ok, row_ok = sem("lg_full"), sem("lg_ok"), sem("lnm_ok"), sem("lexp_ok"), sem("row_ok")
        ld_x2, ld_k, ld_r, ld_f, ld_u = sem("ld_x2"), sem("ld_k"), sem("ld_r"), sem("ld_f"), sem("ld_u")
        mb_ok, pace = sem("mb_ok"), sem("pace")
        rs_add, rs2_add = sem("rs_add"), sem("rs2_add")
        mv_ok, rs_ok, mv2_ok, rs2_ok = sem("mv_ok"), sem("rs_ok"), sem("mv2_ok"), sem("rs2_ok")
        p_bias, p_w = sem("p_bias"), sem("p_w")
        su_pe, su_act, su_dve, su_pool = sem("su_pe"), sem("su_act"), sem("su_dve"), sem("su_pool")
        tl = {n: sem("tl_" + n) for n in ("oh", "pe", "dve", "slot", "scat", "xn", "xt", "xte", "id", "ide", "zero", "reg", "seg", "stage", "fin", "out")}
        back = [sem(f"tl_back{m}") for m in range(NT // 2)]

        def use(b, l, name):
            return PRE + N_USE * b + USE0[l] + USES[l].index(name)

        def bank(l, name):
            return (PRE + USE0[l] + USES[l].index(name)) % 2

        def rope(b, l, name):
            return PRE + N_ROPE * b + ROPE0[l] + (0 if name == "K" or l % 2 else 1)

        def need(eng, s, n):
            if not isinstance(n, int) or n > 0:
                eng.wait_ge(s, n)

        def batches(eng, body):
            body(0, True, False)
            with eng.Fori(1, B - 1) as b:
                body(b, False, False)
            body(B - 1, False, True)

        def w(name, part):
            t = w_hi if part == 0 else w_lo
            return t[:, SLICES.index(name), :]

        PARTS = ((0, 0), (0, 1), (1, 0))

        def load_row(engine, table, r):
            return nc.values_load_multi_w_load_instructions(seg_i[0:1, table, bass.ds(4 * r, 4)], engines=[engine],
                                                            min_val=0, max_val=((NT - 1) * H, E_N - 1, (NT - 1) * P)[table],
                                                            skip_runtime_bounds_check_because="a tile is a count of at most NT - 1 edges, and an expert lies below E_N as the last edge does")[1]

        block = ctx.enter_context(nc.Block())

        def read_back(eng, m):
            eng.dma_start(xscore[:, 2 * m:2 * m + 2, :], scratch[2 * m * P:2 * (m + 1) * P].rearrange("(i p) n -> p i n", p=P)).then_inc(back[m], 16)

        @block.sync
        def _(sp):
            xr = x.rearrange("b (t p) n -> p (b t) n", p=P)
            wsrc = {"K": wk, "V": wv}
            wsrc.update({f"Q{g}": wq[:, g * 1024:(g + 1) * 1024] for g in range(NG)})
            wsrc.update({f"O{g}": wo[:, g * 1024:(g + 1) * 1024] for g in range(NG)})

            def load_w(i):
                sp.dma_start(raw[SLICES[i]], wsrc[SLICES[i]]).then_inc(ld_w[i], 16)
            sp.dma_start(rows[:, 0:TT, 0:H], xr[:, 0:TT]).then_inc(ld_x, 16)
            load_w(0)
            load_w(1)
            sp.dma_start(tab_sb[:, :, :].rearrange("p a s -> p (a s)"), tables).then_inc(ld_r, 16)
            for i in range(2, len(SLICES)):
                load_w(i)
                if i == 3:
                    sp.dma_start(rows[:, TT:NT, 0:H], xr[:, TT:NT]).then_inc(ld_x2, 16)
            for i in range(8):
                if 4 * i == RAW_E:
                    sp.wait_ge(w_lo_ok, len(SLICES))
                    sp.wait_ge(w_hi_ok, len(SLICES))
                if i == 1:
                    sp.wait_ge(su_pe, 8)
                if i % 2 == 0 and i > 0:
                    sp.wait_ge(ld_m, 16 * i)
                sp.dma_start(experts[:, 4 * i:4 * i + 4].rearrange("p e k o -> p (e k o)"),
                             masks[:, 4 * i * KC * H:4 * (i + 1) * KC * H]).then_inc(ld_m, 16)

            sp.wait_ge(tl["scat"], 16 * NT)
            for m in range(0, NT // 2, 2):
                read_back(sp, m)

        @block.gpsimd
        def _(pool):
            def inverse_std(mv_, rstd_, s_in, n, s_out, s_add):
                pool.wait_ge(s_in, n)
                nc.gpsimd.tensor_tensor(rstd_, mv_[:, :, 1], eps2, ALU.add).then_inc(s_add, 1)
                pool.wait_ge(s_add, n)
                nc.gpsimd.tensor_tensor(rstd_, rstd_, neg_half2, ALU.pow).then_inc(s_out, 1)

            def rotate(i, r, n_, width, dst, free_sem, free_n):
                sw = swap[:, i % 2, 0:width, :]
                pool.wait_ge(pj_act, n_ + 1)
                nc.gpsimd.tensor_tensor(sw, sw, (sin_sb if width == 1 else sinq_sb)[:, :].unsqueeze(1).to_broadcast([P, width, S]), ALU.mult).then_inc(pool_t2, 1)
                pool.wait_ge(pj_dve, r + 1)
                pool.wait_ge(pool_t2, r + 1)
                nc.gpsimd.tensor_tensor(dst, dst, sw, ALU.add).then_inc(rope_ok, 1)

            pool.dma_start(cau_f, causal).then_inc(ld_u, 16)
            pool.wait_ge(ld_k, 16)
            inverse_std(mv, rstd, mv_ok, 1, rs_ok, rs_add)
            pool.dma_start(smask_sb[:, :, :], smask.rearrange("(t p) s -> p t s", p=P)).then_inc(p_bias, 16)
            pool.dma_start(kmask_sb[:, :, :].rearrange("p b s -> p (b s)"),
                           kmask.rearrange("b s -> (b s)").rearrange("(a n) -> a n", a=1).to_broadcast([P, B * S])).then_inc(p_bias, 16)
            pool.dma_start(ffn_sb[:, :], ffw).then_inc(ld_f, 16)
            pool.dma_start(fs_sb[:, :], ffscale.rearrange("(a n) -> a n", a=1).to_broadcast([P, H])).then_inc(ld_f, 16)
            pool.wait_ge(ld_r, 16)
            rotate(0, 0, 0, 1, kt[:, 0:1, 0:S], None, 0)
            rotate(1, 1, 1, 2, qt[:, 0], None, 0)
            rotate(2, 2, 2, 2, qt[:, 1], None, 0)

            def body(b, first, last):
                for l in range(STEPS):
                    v = b * STEPS + l
                    if not (last and l >= 6):
                        for name in USES[l]:
                            if name in ("K", "Q"):
                                r = rope(b, l, name)
                                i = PRE + ROPE0[l] + (0 if name == "K" or l % 2 else 1)
                                n_ = use(b, l, name)
                                if name == "K":
                                    g = (l // 2 + 1) % NG
                                    rotate(i, r, n_, 1, kt[:, g % 2:g % 2 + 1, 0:S], None, 0)
                                else:
                                    rotate(i, r, n_, 2, qt[:, l % 2], None, 0)
                    if l == 0:
                        pool.wait_ge(ld_m, 32 * (b + 1))
                    if first and l == 0:
                        pool.wait_ge(d_nm, 4)
                    e_ap = experts[:, bass.ds(b * STEPS + l, 1), :, :].rearrange("p a k o -> p (a k o)")
                    nc.gpsimd.tensor_tensor(e_ap, e_ap, tern_flat, ALU.mult).then_inc(p_w, 1)
                    if l == 3 and not last:
                        inverse_std(mv, rstd, mv_ok, b + 2, rs_ok, rs_add)
                    if not first and l in (1, 4):
                        inverse_std(mv2, rstd2, mv2_ok, 2 * (b - 1) + (1 if l == 1 else 2), rs2_ok, rs2_add)
                    if not first and l == 2:
                        cross_scores(b - 1)

            def cross_scores(p):
                pool.wait_ge(qc_ok, p + 1)
                if isinstance(p, int) and p == 0:
                    pool.wait_ge(su_dve, 6)
                nc.gpsimd.tensor_tensor(post[:, :, :], post[:, :, :], xscore[:, bass.ds(TT * p, TT), 0:S], ALU.mult).then_inc(xs_ok, 1)
                pool.wait_ge(xs_ok, 2 * p + 1)
                pool.wait_ge(mb_ok, 2 * p + 2)
                nc.gpsimd.tensor_tensor(post[:, :, :], post[:, :, :], bias_x[:, :, :], ALU.add).then_inc(xs_ok, 1)

            batches(pool, body)
            inverse_std(mv2, rstd2, mv2_ok, 2 * B - 1, rs2_ok, rs2_add)
            cross_scores(B - 1)
            inverse_std(mv2, rstd2, mv2_ok, 2 * B, rs2_ok, rs2_add)
            pool.wait_ge(rope_ok, PRE + N_ROPE * B - 3)
            pool.dma_start(tri_sb[:, :, :].rearrange("p a b -> p (a b)"), tri).then_inc(p_bias, 16)
            for i in range(NT):
                if i == 0:
                    pool.wait_ge(tl["slot"], 1)
                nc.gpsimd.indirect_dma_start(scratch, bass.IndirectOffsetOnAxis(slot_u[:, i:i + 1], 0),
                                             rows[:, i, :], None).then_inc(tl["scat"], 16)
            nc.gpsimd.memset(bias_x[:, :, :], 0.0).then_inc(tl["zero"], 1)
            pool.wait_ge(tl["dve"], TC_END)
            for i in range(NT):
                pool.wait_ge(tl["fin"], i // 2 + 1)
                nc.gpsimd.indirect_dma_start(out, bass.IndirectOffsetOnAxis(tok_u[:, i:i + 1], 0),
                                             xscore[:, i, 0:H], None).then_inc(tl["out"], 16)
            pool.wait_ge(tl["out"], 16 * NT)


        @block.scalar
        def _(act):
            act.dma_start(con_all[:, :], consts).then_inc(ld_k, 16)
            act.dma_start(xw_all[:, :], xw).then_inc(ld_c, 16)
            act.dma_start(ctx_sb, ctxT).then_inc(ld_c, 16)

            def split_hi(i):
                act.wait_ge(ld_w[i], 16)
                nc.scalar.activation(w_hi[:, i, :], raw[SLICES[i]], ACT.Copy).then_inc(w_hi_ok, 1)

            def copy_ot(dst, s_):
                nc.scalar.activation(dst, ot[:, :], ACT.Copy).then_inc(s_, 1)

            def halves(i, r, n_, bk, width):
                act.wait_ge(pj_full, n_ + 1)
                need(act, rope_ok, r - 1)
                src = proj[:, bk, 0:width * S].rearrange("p (h s) -> p h s", h=width)
                nc.scalar.activation(swap[0:64, i % 2, 0:width, :], src[64:128], ACT.Copy)
                nc.scalar.activation(swap[64:128, i % 2, 0:width, :], src[0:64], ACT.Copy).then_inc(pj_act, 1)

            split_hi(0)
            act.wait_ge(xt_full, 1)
            copy_ot(xnT_hi[:, :, :].rearrange("p k s -> p (k s)"), xt_hi_ok)
            for i in range(1, EARLY):
                split_hi(i)
            halves(0, 0, 0, 0, 1)
            halves(1, 1, 1, 1, 2)
            halves(2, 2, 2, 0, 2)
            spare = [sc[:, 2, :], sc[:, 3, :], y[:, :, :].rearrange("p t n -> p (t n)"), ot[:, :]]
            for i in range(4):
                act.wait_ge(su_pe, i + 1)
                nc.scalar.activation(xqk[:, i % 2, (i // 2) * 512:(i // 2 + 1) * 512], spare[i][0:CTX, :], ACT.Identity,
                                     bias=xb_sb[:, i % 2:i % 2 + 1]).then_inc(su_act, 1)

            def body(b, first, last):
                for l in range(STEPS):
                    v = b * STEPS + l
                    def swaps():
                        if not (last and l >= 6):
                            for name in USES[l]:
                                if name in ("K", "Q"):
                                    i = PRE + ROPE0[l] + (0 if name == "K" or l % 2 else 1)
                                    halves(i, rope(b, l, name), use(b, l, name), bank(l, name), 1 if name == "K" else 2)
                    swaps()
                    if not (first and l == 0):
                        act.wait_ge(pt_full, v)
                        need(act, pv_full, v - 1)
                        qq = (l - 1) % 2
                        nc.scalar.activation(pT[:, :, :], sc[:, 2 * qq:2 * qq + 2, 0:384], ACT.Copy).then_inc(pt_ok, 1)
                    if l == 5 and not last:
                        act.wait_ge(xt_full, b + 2)
                        nc.scalar.activation(xnT_hi[:, :, :].rearrange("p k s -> p (k s)"), proj[:, bank(6, "K"), :], ACT.Copy).then_inc(xt_hi_ok, 1)
                    act.wait_ge(nm_ok, v + 1)
                    need(act, pt_full, v)
                    q = l % 2
                    for h in range(2):
                        nc.scalar.activation(probs[:, h, 0:P], sc[:, 2 * q + h, 0:P], ACT.Exp, bias=nm[q][:, h:h + 1],
                                             scale=-1.0, accum_out=sums[q][:, h:h + 1])
                        last_i = nc.scalar.activation(probs[:, h, P:384], sc[:, 2 * q + h, P:384], ACT.Exp,
                                                      bias=nm[q][:, 2 + h:3 + h], scale=-1.0, accum_out=sums[q][:, 2 + h:3 + h])
                    last_i.then_inc(exp_ok, 1)
                    if not (first and l == 0):
                        act.wait_ge(pv_full, v)
                        need(act, o_done, v - 1)
                        copy_ot(oT_hi[:, :, :].rearrange("p k s -> p (k s)"), ot_hi_ok)
                    act.wait_ge(rc_ok, v + 1)
                    for h in range(2):
                        nc.scalar.activation(probs[:, h, 0:P], probs[:, h, 0:P], ACT.Copy, scale=rsum[q][:, h:h + 1])
                        last_i = nc.scalar.activation(probs[:, h, P:384], probs[:, h, P:384], ACT.Copy, scale=rsum[q][:, 2 + h:3 + h])
                    last_i.then_inc(pn_ok, 1)
                    if l == 0:
                        for i, name in enumerate(("V0", "V1")):
                            act.wait_ge(pj_full, use(b, 0, name) + 1)
                            nc.scalar.activation(values[:, i, :], proj[:, bank(0, name), :], ACT.Copy).then_inc(pj_act, 1)
                    if first:
                        for i in LATE.get(l, ()):
                            split_hi(i)
                    if not first:
                        post_act(b - 1, l)

            def post_act(p, l):
                if l == 3:
                    act.wait_ge(xnm_ok, p + 1)
                    for t in range(TT):
                        i = nc.scalar.activation(post[:, t, :], post[:, t, :], ACT.Exp, bias=xnm[:, t:t + 1],
                                                 accum_out=xsum[:, t:t + 1])
                    i.then_inc(xexp_ok, 1)
                if l == 6:
                    act.wait_ge(x3_full, p + 1)
                    copy_ot(post[:, :, :].rearrange("p k s -> p (k s)"), x3_ok)
                if l == 7:
                    act.wait_ge(lnm_ok, p + 1)
                    for t in range(TT):
                        i = nc.scalar.activation(logit[:, t, :], logit[:, t, :], ACT.Exp, bias=lnm[:, t:t + 1],
                                                 accum_out=lsum[:, t:t + 1])
                    i.then_inc(lexp_ok, 1)

            batches(act, body)
            V = B * STEPS
            act.wait_ge(pt_full, V)
            act.wait_ge(pv_full, V - 1)
            nc.scalar.activation(pT[:, :, :], sc[:, 2:4, 0:384], ACT.Copy).then_inc(pt_ok, 1)
            act.wait_ge(pv_full, V)
            act.wait_ge(o_done, V - 1)
            copy_ot(oT_hi[:, :, :].rearrange("p k s -> p (k s)"), ot_hi_ok)
            for l in range(STEPS):
                post_act(B - 1, l)
            act.wait_ge(tl["scat"], 16 * NT)
            for m in range(1, NT // 2, 2):
                read_back(act, m)
            for m in range(NT // 2):
                act.wait_ge(tl["xt"], m + 1)
                nc.scalar.activation(sortedT[:, :, 2 * m * P:2 * (m + 1) * P].rearrange("p k (i s) -> p i k s", i=2), (ot[:, :] if m % 2 == 0 else y_flat).rearrange("p (i k s) -> p i k s", i=2, k=KC),
                                     ACT.Copy).then_inc(tl["xte"], 1)
                if m % 2:
                    act.wait_ge(tl["id"], m // 2 + 1)
                    nc.scalar.activation(expT[:, (m // 2) * 512:(m // 2 + 1) * 512], proj[:, m // 2, :], ACT.Copy).then_inc(tl["ide"], 1)

        @block.vector
        def _(dve):
            def tt(out_, a, b_, op):
                return nc.vector.tensor_tensor(out_, a, b_, op)

            def carrier():
                dve.sem_inc(pace, 1)

            class Chain:
                def __init__(self, s, per):
                    self.s, self.per, self.base, self.n = s, per, 0, 0

                def at(self, base):
                    self.base, self.n = base, 0

                def count(self, ins):
                    self.n += 1
                    ins.then_inc(self.s, 1)

                def wait(self, carry=False):
                    dve.wait_ge(self.s, self.base + self.n)
                    if carry:
                        carrier()

                def __call__(self, ins, carry=False):
                    self.count(ins)
                    self.wait(carry)

            def split_lo(i):
                dve.wait_ge(w_hi_ok, i + 1)
                nc.vector.tensor_tensor(w_lo[:, i, :], raw[SLICES[i]], w_hi[:, i, :].bitcast(fp32), ALU.subtract).then_inc(w_lo_ok, 1)

            def row_stats(chain, src, bn_, mv_, done):
                carrier()
                for t in range(TT):
                    i = nc.vector.bn_stats(bn_[:, t, :], src[:, t, :])
                chain(i, carry=True)
                for t in range(TT):
                    i = nc.vector.bn_aggr(mv_[:, t, :], bn_[:, t, :])
                i.then_inc(done, 1)

            def row_apply(src, dst, mv_, rstd_, done):
                for t in range(TT):
                    i = nc.vector.tensor_scalar(dst[:, t, :], src[:, t, :], mv_[:, t, 0:1], rstd_[:, t:t + 1], ALU.subtract, ALU.mult)
                i.then_inc(done, 1)

            LN_N = 1
            ln = Chain(d_ln, LN_N)

            def norm_stats(b):
                ln.at(b * LN_N)
                if isinstance(b, int) and b == 0:
                    dve.wait_ge(ld_x, 16)
                else:
                    dve.wait_ge(ld_x2, 16)
                row_stats(ln, rows[:, bass.ds(TT * b, TT), 0:H], bn, mv, mv_ok)

            def norm_apply(b):
                need(dve, xt_full, b)
                dve.wait_ge(rs_ok, b + 1)
                row_apply(rows[:, bass.ds(TT * b, TT), 0:H], xnrow, mv, rstd, xnr_ok)

            def xt_lo(bank_):
                return nc.vector.tensor_tensor(xnT_lo[:, :, :].rearrange("p k s -> p (k s)"), bank_,
                                               xnT_hi[:, :, :].rearrange("p k s -> p (k s)").bitcast(fp32), ALU.subtract).then_inc(xt_lo_ok, 1)

            def times_cos(n_, bk, width, dst):
                dve.wait_ge(pj_act, n_ + 1)
                tt(dst, proj[:, bk, 0:width * S].rearrange("p (h s) -> p h s", h=width),
                   (cos_sb if width == 1 else cosq_sb)[:, :].unsqueeze(1).to_broadcast([P, width, S]), ALU.mult).then_inc(pj_dve, 1)

            def chunk_sums(g, u, r):
                dve.wait_ge(rope_ok, r + 1)
                nc.vector.tensor_reduce(kt[:, g % 2, S:S + NCH], kt[:, g % 2, 0:S].rearrange("p (n c) -> p n c", c=CHUNK),
                                        AX.X, ALU.add).then_inc(km_ok, 1)

            norm_stats(0)
            nc.vector.memset(selb, 0.0)
            nc.vector.memset(gate[:, :, NCAND:8], 2 * NEG)
            nc.vector.memset(gate[:, :, 8:16], MARK)
            nc.vector.memset(pick, MARK).then_inc(su_dve, 1)
            dve.sem_inc(lg_ok, 1)
            norm_apply(0)
            split_lo(0)
            dve.wait_ge(xt_full, 1)
            dve.wait_ge(xt_hi_ok, 1)
            xt_lo(ot[:, :])
            split_lo(1)
            dve.wait_ge(ld_r, 16)
            dve.wait_ge(ld_u, 16)
            nc.vector.tensor_copy(id_bf[:, :], id_sb[:, :])
            nc.vector.tensor_copy(cau_bf[:, :], cau_f[:, :]).then_inc(su_dve, 1)
            times_cos(0, 0, 1, kt[:, 0:1, 0:S])
            times_cos(1, 1, 2, qt[:, 0])
            chunk_sums(0, 0, 0)
            times_cos(2, 0, 2, qt[:, 1])
            for i in range(2, EARLY):
                split_lo(i)

            def cross_out():
                for i, bk in enumerate((sc[:, 2, :], sc[:, 3, :], y[:, :, :].rearrange("p t n -> p (t n)"), ot[:, :])):
                    dve.wait_ge(su_pe, 5 + i)
                    nc.vector.tensor_scalar(xscore[:, 2 * i:2 * i + 2, 0:S], bk.rearrange("p (t n) -> p t n", t=2),
                                            CTX ** -0.5, None, ALU.mult).then_inc(su_dve, 1)

            def ternary():
                dve.wait_ge(ld_f, 32)
                nc.vector.tensor_scalar(tern_flat, tern_flat, 2.0, 1.0, ALU.mult, ALU.min).then_inc(d_nm, 1)
                dve.wait_ge(d_nm, 1)
                nc.vector.tensor_scalar(tern_flat, tern_flat, -1.0, 12582912.0, ALU.max, ALU.add).then_inc(d_nm, 1)
                dve.wait_ge(d_nm, 2)
                nc.vector.tensor_scalar(tern_flat, tern_flat, 12582912.0, None, ALU.subtract).then_inc(d_nm, 1)
                dve.wait_ge(d_nm, 3)
                tt(tern[:, :, :], tern[:, :, :], fs_sb[:, :].unsqueeze(1).to_broadcast([P, KC, H]), ALU.mult).then_inc(d_nm, 1)

            SM_N = 5
            sm = Chain(d_sm, SM_N)

            def softmax_max(v, l):
                q = l % 2
                s2 = sc[:, 2 * q:2 * q + 2, :]
                sm.at(v * SM_N)
                dve.wait_ge(sc_full, v + 1)
                sm.count(tt(gate[:, :, 0:NCAND], cand.unsqueeze(1).to_broadcast([P, 2, NCAND]), s2[:, :, 384:384 + NCAND], ALU.subtract))
                nc.vector.tensor_reduce(nm[q][:, 0:2], s2[:, :, 0:P], AX.X, ALU.min)
                sm.wait(carry=True)
                for h in range(2):
                    i = nc.vector.max(top[:, h, :], gate[:, h, 0:8])
                sm(i)
                sm(nc.vector.tensor_copy(pick[:, :, 0:TOPK - 1], top[:, :, 0:TOPK - 1]), carry=True)
                for h in range(2):
                    i = nc.vector.match_replace(mark[:, h, :], pick[:, h, :], gate[:, h, :], PICKED)
                sm(i)
                sm(nc.vector.scalar_tensor_tensor(selb[:, :, 0:NCAND], mark[:, :, 0:NCAND], PICKED, ncand.unsqueeze(1).to_broadcast([P, 2, NCAND]),
                                                  ALU.is_lt, ALU.mult), carry=True)
                for h in range(2):
                    view = s2[:, h, P:384].rearrange("p (n c) -> p n c", c=CHUNK)
                    i = nc.vector.tensor_tensor_reduce(out=view, in0=view, in1=selb[:, h].unsqueeze(2).to_broadcast([P, NCH, CHUNK]),
                                                       scale=1.0, scalar=3.0e38, op0=ALU.add, op1=ALU.min, accum_out=nm[q][:, 2 + h:3 + h])
                i.then_inc(nm_ok, 1)

            def reciprocals(v, l):
                dve.wait_ge(exp_ok, v + 1)
                nc.vector.reciprocal(rsum[l % 2], sums[l % 2]).then_inc(rc_ok, 1)

            def ot_lo(v1):
                dve.wait_ge(ot_hi_ok, v1 + 1)
                tt(oT_lo[:, :, :].rearrange("p k s -> p (k s)"), ot[:, :], oT_hi[:, :, :].rearrange("p k s -> p (k s)").bitcast(fp32),
                   ALU.subtract).then_inc(ot_lo_ok, 1)

            def body(b, first, last):
                for l in range(STEPS):
                    v = b * STEPS + l
                    if first and l == 0:
                        cross_out()
                    softmax_max(v, l)

                    def cosines():
                        if not (last and l >= 6):
                            for name in USES[l]:
                                if name == "K":
                                    g = (l // 2 + 1) % NG
                                    times_cos(use(b, l, name), bank(l, name), 1, kt[:, g % 2:g % 2 + 1, 0:S])
                                if name == "Q":
                                    times_cos(use(b, l, name), bank(l, name), 2, qt[:, l % 2])
                    if not first and l == 7:
                        take_logits(b - 1)
                    cosines()
                    if l == 5 and not last:
                        dve.wait_ge(xt_hi_ok, b + 2)
                        xt_lo(proj[:, bank(6, "K"), :])
                    reciprocals(v, l)
                    if not (first and l == 0):
                        ot_lo(v - 1)
                    if "K" in USES[l] and not (last and l >= 6):
                        chunk_sums((l // 2 + 1) % NG, 4 * b + l // 2 + 1, rope(b, l, "K"))
                    if first and l == 0:
                        ternary()
                    if first:
                        for i in LATE.get(l, ()):
                            split_lo(i)
                    if l == 3 and not last:
                        norm_stats(b + 1)
                    if l == 4 and not last:
                        norm_apply(b + 1)
                    if not first:
                        post_dve(b - 1, l)

            POST_N = 8
            pc = Chain(d_post, POST_N)

            def take_logits(p):
                dve.wait_ge(lg_full, p + 1)
                nc.vector.tensor_copy(logit, ot[:, 0:TT * E_N].rearrange("p (t e) -> p t e", t=TT)).then_inc(lg_ok, 1)

            def post_dve(p, l):
                base = p * POST_N
                r2 = rows[:, bass.ds(TT * p, TT), 0:H]
                if l == 1:
                    dve.wait_ge(o_done, STEPS * (p + 1))
                    tt(r2, r2, y[:, :, :], ALU.add).then_inc(x1_ok, 1)
                    pc.at(base)
                    dve.wait_ge(x1_ok, p + 1)
                    row_stats(pc, r2, bn2, mv2, mv2_ok)
                if l == 0:
                    if isinstance(p, int) and p == 0 or not isinstance(p, int):
                        dve.wait_ge(p_bias, 32)
                    tt(bias_x[:, :, :], smask_sb[:, :, :], kmask_sb[:, bass.ds(p, 1), :].to_broadcast([P, TT, S]), ALU.max).then_inc(mb_ok, 1)
                    dve.wait_ge(mb_ok, 2 * p + 1)
                    nc.vector.tensor_scalar(bias_x[:, :, :], bias_x[:, :, :], NEG, None, ALU.mult).then_inc(mb_ok, 1)
                if l == 2:
                    dve.wait_ge(rs2_ok, 2 * p + 1)
                    row_apply(r2, post, mv2, rstd2, qc_ok)
                if l == 3:
                    dve.wait_ge(xs_ok, 2 * p + 2)
                    pc.at(base + 1)
                    pc(nc.vector.tensor_reduce(xmx, post[:, :, :], AX.X, ALU.max))
                    nc.vector.tensor_scalar(xnm, xmx, -1.0, None, ALU.mult).then_inc(xnm_ok, 1)
                if l == 4:
                    dve.wait_ge(xexp_ok, p + 1)
                    pc.at(base + 2)
                    pc(nc.vector.tensor_scalar(xany, xmx, NEG / 2, None, ALU.is_gt))
                    pc(tt(xsum, xsum, xany, ALU.mult))
                    pc(nc.vector.reciprocal(xrs, xsum))
                    pc(tt(xrs, xrs, xany, ALU.mult))
                    for t in range(TT):
                        i = nc.vector.scalar_tensor_tensor(rows[:, bass.ds(TT * p + t, 1), 0:H].rearrange("p a n -> p (a n)"), post[:, t, :], xrs[:, t:t + 1],
                                                           rows[:, bass.ds(TT * p + t, 1), 0:H].rearrange("p a n -> p (a n)"), ALU.mult, ALU.add)
                    i.then_inc(xm_ok, 1)
                    dve.wait_ge(xm_ok, p + 1)
                    row_stats(pc, r2, bn2, mv2, mv2_ok)
                if l == 5:
                    dve.wait_ge(rs2_ok, 2 * p + 2)
                    row_apply(r2, post, mv2, rstd2, xn3_ok)
                if l == 7:
                    dve.wait_ge(lg_ok, p + 2)
                    carrier()
                    for t in range(TT):
                        nc.vector.max(lg8x[:, t, :], logit[:, t, :]).then_inc(lg_m, 1)
                    dve.wait_ge(lg_m, 2 * p + 2)
                    nc.vector.tensor_scalar(lnm, lg8x[:, :, 0], -1.0, None, ALU.mult).then_inc(d_post, 1)
                    dve.wait_ge(d_post, base + 8)
                    carrier()
                    for t in range(TT):
                        nc.vector.max_index(idxx[:, t, :], lg8x[:, t, :], logit[:, t, :]).then_inc(lg_x, 1)
                    dve.wait_ge(lg_x, 2 * p + 2)
                    dve.wait_ge(d_post, base + 8)
                    nc.vector.tensor_scalar(rows[:, bass.ds(TT * p, TT), 256:257].rearrange("p t a -> p (t a)"), idxx[:, :, 0],
                                            float(E_N - 1), None, ALU.min).then_inc(lnm_ok, 1)
                    nc.vector.tensor_copy(rows[:, bass.ds(TT * p, TT), 259:260].rearrange("p t a -> p (t a)"), mv2[:, :, 0])
                    nc.vector.tensor_copy(rows[:, bass.ds(TT * p, TT), 260:261].rearrange("p t a -> p (t a)"), rstd2)
                    dve.wait_ge(lexp_ok, p + 1)
                    nc.vector.reciprocal(rows[:, bass.ds(TT * p, TT), 257:258].rearrange("p t a -> p (t a)"), lsum).then_inc(row_ok, 1)

            batches(dve, body)
            V = B * STEPS
            ot_lo(V - 1)
            for l in range(STEPS):
                if l == 7:
                    take_logits(B - 1)
                post_dve(B - 1, l)
            tc = Chain(tl["dve"], 0)
            dve.wait_ge(row_ok, B)
            tc(nc.vector.tensor_copy(rows[:, :, 258], token))
            tc(nc.vector.memset(rows[:, :, 261:264], 0.0))
            tc(nc.vector.memset(zero256, 0.0))
            nc.vector.memset(seg_i[:, :, 0:1], 0).then_inc(tl["reg"], 1)
            oh3 = oh.rearrange("p (i e) -> p i e", i=NT)
            tt(oh3, rows[:, :, 256].unsqueeze(2).to_broadcast([P, NT, E_N]), iota_e.unsqueeze(1).to_broadcast([P, NT, E_N]),
               ALU.is_equal).then_inc(tl["oh"], 1)
            dve.wait_ge(tl["pe"], 2)
            cnt = post[:, 0, :].rearrange("p (e i) -> p e i", e=E_N)
            run = post[:, 1, :]
            tc(nc.vector.tensor_copy(cnt, proj[:, 1, 0:256].rearrange("p (i e) -> p e i", i=NT)))
            tc(nc.vector.tensor_tensor_scan(run, post[:, 0, :], zero256, 0.0, ALU.add, ALU.add))
            tc(tt(base, run, post[:, 0, :], ALU.subtract))
            wk1 = probs[:, 0, 0:256].rearrange("p (i e) -> p i e", i=NT)
            tc(tt(wk1, proj[:, 0, 0:256].rearrange("p (i e) -> p i e", i=NT), base.rearrange("p (e i) -> p i e", e=E_N), ALU.add))
            tc(tt(wk1, wk1, oh3, ALU.mult))
            place = small[:, 0:NT]
            tc(nc.vector.tensor_reduce(place, wk1, AX.X, ALU.add))
            nc.vector.tensor_copy(slot_u[:, :], place).then_inc(tl["slot"], 1)
            edge_c = probs[:, 1, 0:7 * E_N].rearrange("p (i e) -> p i e", i=NT - 1)
            incl = run.rearrange("p (e i) -> p e i", e=E_N)[:, :, NT - 1]
            tc(tt(edge_c, incl.unsqueeze(1).to_broadcast([P, NT - 1, E_N]), bound.unsqueeze(2).to_broadcast([P, NT - 1, E_N]), ALU.is_lt))
            edge = small[:, 16:23]
            tc(nc.vector.tensor_reduce(edge, edge_c, AX.X, ALU.add))
            tc(tt(edge, edge, tile1, ALU.add))
            seg_c = post[:, :, :].rearrange("p a b -> p (a b)")[:, 0:SEGS * (NT - 1)].rearrange("p (j i) -> p j i", i=NT - 1)
            tc(tt(seg_c, edge.unsqueeze(1).to_broadcast([P, SEGS, NT - 1]), iota_j.unsqueeze(2).to_broadcast([P, SEGS, NT - 1]), ALU.is_le))
            tile_f = small[:, 32:32 + SEGS]
            tc(nc.vector.tensor_reduce(tile_f, seg_c, AX.X, ALU.add))
            exp_f = small[:, 80:80 + SEGS]
            tc(tt(exp_f, iota_j, tile_f, ALU.subtract))
            nc.vector.tensor_scalar(seg_i[:, 0, 1:1 + SEGS], tile_f, float(H), None, ALU.mult)
            nc.vector.tensor_scalar(seg_i[:, 2, 1:1 + SEGS], tile_f, float(P), None, ALU.mult)
            nc.vector.tensor_copy(seg_i[:, 1, 1:1 + SEGS], exp_f).then_inc(tl["reg"], 1)
            for i in range(NT):
                dve.wait_ge(back[i // 2], 16)
                if i > 3:
                    dve.wait_ge(tl["xt"], i // 2 - 1)
                nc.vector.tensor_scalar((xnrow, post)[(i // 2) % 2][:, i % 2, :], xscore[:, i, 0:H], xscore[:, i, 259:260], xscore[:, i, 260:261],
                                        ALU.subtract, ALU.mult).then_inc(tl["xn"], 1)
            dve.wait_ge(tl["reg"], 2)
            tc(nc.vector.tensor_copy(tok_u[:, :], xscore[:, :, 258]))
            assert tc.n == TC_END

            def stage(r, first, last):
                cols = load_row(mybir.EngineType.DVE, 2, r)
                for k in range(1 if first else 0, 4):
                    j = 4 * r + k - 1
                    if isinstance(j, int) and j < NT:
                        dve.wait_ge(tl["xte"], j // 2 + 1)
                        dve.wait_ge(tl["ide"], j // 4 + 1)
                    need(dve, tl["seg"], j - 3)
                    nc.vector.scalar_tensor_tensor(stage_x[:, k], expT[:, bass.ds(cols[k], P)].unsqueeze(1).to_broadcast([P, KC, P]), exp_f[:, bass.ds(j, 1)],
                                                   sortedT[:, :, bass.ds(cols[k], P)], ALU.is_equal, ALU.mult).then_inc(tl["stage"], 1)

            def finish(m):
                dve.wait_ge(tl["seg"], E_N + 2 * m + 1)
                for i in (2 * m, 2 * m + 1):
                    last_i = nc.vector.scalar_tensor_tensor(xscore[:, i, 0:H], sc[:, m, (i % 2) * H:(i % 2 + 1) * H], xscore[:, i, 257:258],
                                                            xscore[:, i, 0:H], ALU.mult, ALU.add)
                last_i.then_inc(tl["fin"], 1)
            stage(0, True, False)
            stage(1, False, False)
            with dve.Fori(2, SEG_ROWS) as r:
                stage(r, False, False)
            for m in range(NT // 2):
                finish(m)

        @block.tensor
        def _(pe):
            mm = nc.tensor.matmul

            spare = [sc[:, 2, :], sc[:, 3, :], y[:, :, :].rearrange("p t n -> p (t n)"), ot[:, :]]

            def transposes(src, bank_):
                for t in range(TT):
                    for kc in range(KC):
                        i = nc.tensor.transpose(bank_[:, kc * S + t * P:kc * S + (t + 1) * P], src[:, t, kc * P:(kc + 1) * P], id_sb[:, :])
                return i
            pe.wait_ge(ld_k, 16)
            pe.wait_ge(xnr_ok, 1)
            transposes(xnrow, ot).then_inc(xt_full, 1)

            def cross_attention():
                pe.wait_ge(ld_c, 32)
                for i in (0, 1, 2, 3):
                    if i == 3:
                        pe.wait_ge(xt_lo_ok, 1)
                    mm(spare[i][0:CTX, :], xw_sb[:, i % 2, :], ctx_sb[:, (i // 2) * 512:(i // 2 + 1) * 512],
                       start=True, stop=True).then_inc(su_pe, 1)
                pe.wait_ge(su_act, 4)
                for i in range(NT):
                    bb, t = i // TT, i % TT
                    xs = mm(spare[i // 2][:, (i % 2) * S:(i % 2 + 1) * S], xqk[:, 0, bb * S + t * P:bb * S + (t + 1) * P],
                            xqk[:, 1, bb * S:(bb + 1) * S], start=True, stop=True)
                    if i % 2:
                        xs.then_inc(su_pe, 1)

            def dve_seen(n_, b, l, name):
                if isinstance(n_, int) and n_ < PRE:
                    return n_ - 1
                before = [u for m in range(l + 1) for u in USES[m]][:USE0[l] + USES[l].index(name)]
                before = (["K", "Q", "Q"] + before) if False else before
                cut = before[:-1] if before else None
                if cut is None:
                    return PRE + N_ROPE * b - 1
                return PRE + N_ROPE * b + sum(u in ("K", "Q") for u in cut)

            def project(name, b, l, n_, bk, g):
                need(pe, pj_act, n_ - 1)
                need(pe, pj_dve, dve_seen(n_, b, l, name))
                if name == "K":
                    for n, (a, c) in enumerate(PARTS):
                        for kc in range(KC):
                            i = mm(proj[:, bk, 0:S], w("K", a)[:, kc * 512 + g * D:kc * 512 + (g + 1) * D],
                                   (xnT_hi if c == 0 else xnT_lo)[:, kc, :], start=(n + kc == 0), stop=(n == 2 and kc == KC - 1))
                elif name == "Q":
                    for h in range(2):
                        hh = 2 * (l % 2) + h
                        for n, (a, c) in enumerate(PARTS):
                            for kc in range(KC):
                                i = mm(proj[:, bk, h * S:(h + 1) * S], w(f"Q{g}", a)[:, kc * 512 + hh * D:kc * 512 + (hh + 1) * D],
                                       (xnT_hi if c == 0 else xnT_lo)[:, kc, :], start=(n + kc == 0), stop=(n == 2 and kc == KC - 1))
                else:
                    t = int(name[1])
                    for n, (a, c) in enumerate(PARTS):
                        for kc in range(KC):
                            i = mm(proj[:, bk, :], (xnT_hi if c == 0 else xnT_lo)[:, kc, t * P:(t + 1) * P],
                                   w("V", a)[:, kc * 512:(kc + 1) * 512], start=(n + kc == 0), stop=(n == 2 and kc == KC - 1))
                i.then_inc(pj_full, 1)

            def scores(v, l, u):
                q, g = l % 2, l // 2
                r = 2 + v if isinstance(v, int) and v < 2 else None
                need(pe, pt_ok, v - 1)
                for h in range(2):
                    bk = sc[:, 2 * q + h, :]
                    mm(bk[:, 0:P], qt[:, q, h, 0:P], kt[:, g % 2, 0:P], start=True, stop=False)
                    mm(bk[:, 0:P], id_bf[:, :], cau_bf[:, :], start=False, stop=True)
                    mm(bk[:, P:P + S + NCH], qt[:, q, h, P:S], kt[:, g % 2, :], start=True, stop=False)
                    i = mm(bk[:, S:S + P], id_bf[:, :], cau_bf[:, :], start=False, stop=True)
                i.then_inc(sc_full, 1)

            def transpose_probs(v, q):
                pe.wait_ge(pn_ok, v + 1)
                for h in range(2):
                    for n in range(3):
                        i = nc.tensor.transpose(sc[:, 2 * q + h, n * P:(n + 1) * P], probs[:, h, n * P:(n + 1) * P], id_sb[:, :])
                i.then_inc(pt_full, 1)

            def weigh(v, g):
                pe.wait_ge(pt_ok, v + 1)
                need(pe, ot_hi_ok, v)
                need(pe, ot_lo_ok, v)
                for h in range(2):
                    mm(ot[:, h * S:(h + 1) * S], values[:, 0, g * D:(g + 1) * D], pT[:, h, 0:S], start=True, stop=False)
                    i = mm(ot[:, h * S + P:(h + 1) * S], values[:, 1, g * D:(g + 1) * D], pT[:, h, S:384], start=False, stop=True)
                i.then_inc(pv_full, 1)

            def output(v, l):
                pe.wait_ge(ot_hi_ok, v + 1)
                pe.wait_ge(ot_lo_ok, v + 1)
                for h in range(2):
                    hh = 2 * (l % 2) + h
                    for t in range(TT):
                        for n, (a, c) in enumerate(PARTS):
                            i = mm(y[:, t, :], (oT_hi, oT_lo)[a][:, h, t * P:(t + 1) * P], w(f"O{l // 2}", c)[:, hh * H:(hh + 1) * H],
                                   start=(l == 0 and h == 0 and t == 0 and n == 0), stop=(l == 7 and h == 1 and n == 2), skip_group_check=True)
                i.then_inc(o_done, 1)

            pe.wait_ge(w_lo_ok, 1)
            pe.wait_ge(xt_lo_ok, 1)
            project("K", 0, 0, 0, 0, 0)
            pe.wait_ge(w_lo_ok, 2)
            project("Q", 0, 0, 1, 1, 0)
            project("Q", 0, 1, 2, 0, 0)
            cross_attention()

            def body(b, first, last):
                for l in range(STEPS):
                    v = b * STEPS + l

                    def projections():
                        if last and l >= 6:
                            return
                        for name in USES[l]:
                            if name[0] == "V":
                                continue
                            g = ((l + 2) // 2) % NG
                            if first:
                                pe.wait_ge(w_lo_ok, SLICES.index(f"Q{g}") + 1)
                            project(name, b, l, use(b, l, name), bank(l, name), g)
                    if first and l < 2:
                        pe.wait_ge(rope_ok, 2 + l)
                    else:
                        lv = (l - 2) % STEPS
                        pe.wait_ge(rope_ok, rope(b if l >= 2 else b - 1, lv, "Q") + 1)
                    pe.wait_ge(km_ok, NG * b + l // 2 + 1)
                    if first and l == 0:
                        pe.wait_ge(su_dve, 2)
                    if first and l == 1:
                        pe.wait_ge(su_dve, 6)
                    scores(v, l, None)
                    if not first and l == 7:
                        post_pe(b - 1, l, v - 1)
                    if l == 6 and not last:
                        pe.wait_ge(xt_hi_ok, b + 2)
                        pe.wait_ge(xt_lo_ok, b + 2)
                    projections()
                    if l == 5 and not last:
                        pe.wait_ge(xnr_ok, b + 2)
                        pe.wait_ge(pj_act, use(b, 6, "K") - 1)
                        pe.wait_ge(pj_dve, dve_seen(use(b, 6, "K"), b, 6, "K"))
                        transposes(xnrow, proj[:, bank(6, "K"), :]).then_inc(xt_full, 1)
                    if not (first and l == 0):
                        transpose_probs(v - 1, (l - 1) % 2)
                    if not (first and l < 2):
                        if first and l % 2 == 0:
                            pe.wait_ge(w_lo_ok, SLICES.index(f"O{(l - 2) // 2}") + 1)
                        if l == 2:
                            need(pe, x1_ok, b)
                        output(v - 2, (l - 2) % STEPS)
                    if not (first and l == 0):
                        if not first and l == 7:
                            pe.wait_ge(lg_ok, b + 1)
                        if l == 1:
                            pe.wait_ge(pj_act, use(b, 0, "V1") + 1)
                        weigh(v - 1, ((l - 1) % STEPS) // 2)
                    if first and l == 7:
                        pe.wait_ge(w_lo_ok, len(SLICES))
                    if l == 0:
                        if first:
                            pe.wait_ge(w_lo_ok, 3)
                        for name in ("V0", "V1"):
                            project(name, b, 0, use(b, 0, name), bank(0, name), 0)
                    if not first and l == 6:
                        post_pe(b - 1, l, v)

            def post_pe(p, l, v):
                if l == 6:
                    pe.wait_ge(xn3_ok, p + 1)
                    pe.wait_ge(ot_hi_ok, v)
                    pe.wait_ge(ot_lo_ok, v)
                    transposes(post, ot).then_inc(x3_full, 1)
                if l == 7:
                    pe.wait_ge(x3_ok, p + 1)
                    pe.wait_ge(ot_hi_ok, v)
                    pe.wait_ge(ot_lo_ok, v)
                    for t in range(TT):
                        for kc in range(KC):
                            i = mm(ot[:, t * E_N:(t + 1) * E_N], post[:, kc, t * P:(t + 1) * P], rw_sb[:, kc, :], start=(kc == 0), stop=(kc == KC - 1))
                    i.then_inc(lg_full, 1)

            batches(pe, body)
            V = B * STEPS
            transpose_probs(V - 1, 1)
            output(V - 2, 6)
            pe.wait_ge(lg_ok, B)
            weigh(V - 1, NG - 1)
            output(V - 1, 7)
            for l in range(STEPS):
                post_pe(B - 1, l, V)
            pe.wait_ge(tl["oh"], 1)
            pe.wait_ge(p_bias, 48)
            mm(proj[:, 0, 0:256], tri_sb[:, 0, :], oh, start=True, stop=True).then_inc(tl["pe"], 1)
            mm(proj[:, 1, 0:256], tri_sb[:, 1, :], oh, start=True, stop=True).then_inc(tl["pe"], 1)
            pe.wait_ge(tl["zero"], 1)
            for m in range(NT // 2):
                mm(sc[:, m, :], id_bf[:, :], bias_x[:, :, :].rearrange("p t s -> p (t s)"), start=True, stop=False, skip_group_check=True)
            for m in range(NT // 2):
                pe.wait_ge(tl["xn"], 2 * m + 2)
                need(pe, tl["xte"], m - 1)
                for i in (2 * m, 2 * m + 1):
                    for kc in range(KC):
                        t_ = nc.tensor.transpose((ot[:, :] if m % 2 == 0 else y_flat)[:, ((i % 2) * KC + kc) * P:((i % 2) * KC + kc + 1) * P],
                                                 (xnrow, post)[m % 2][:, i % 2, kc * P:(kc + 1) * P], id_sb[:, :])
                t_.then_inc(tl["xt"], 1)
                for i in (2 * m, 2 * m + 1):
                    e_ = mm(proj[:, m // 2, (i % 4) * P:(i % 4 + 1) * P], xscore[:, i, 256:257].to_broadcast([P, P]), id_sb[:, :], start=True, stop=True)
                if m % 2:
                    e_.then_inc(tl["id"], 1)
            pe.wait_ge(tl["reg"], 2)
            pe.wait_ge(p_w, E_N)

            def multiply(r, first):
                cols = load_row(mybir.EngineType.PE, 0, r)
                exs = load_row(mybir.EngineType.PE, 1, r)
                for k in range(1 if first else 0, 4):
                    j = 4 * r + k - 1
                    pe.wait_ge(tl["stage"], j + 1)
                    for kc in range(KC):
                        i = mm(sc_flat[:, bass.ds(cols[k], H)], stage_x[:, k, kc, :],
                               experts[:, bass.ds(exs[k], 1), kc, :].rearrange("p a n -> p (a n)"), start=False, stop=False, skip_group_check=True)
                    i.then_inc(tl["seg"], 1)
            multiply(0, True)
            with pe.Fori(1, SEG_ROWS) as r:
                multiply(r, False)


def kernel(x, ctx_512, mask_SxS2_bk1, mask_BxS2_bf0, L0_attn_wq, L0_attn_wk, L0_attn_wv, L0_attn_wo, L0_xattn_Wq,
           L0_xattn_bq, L0_xattn_Wk, L0_xattn_bk, L0_ffn_weight, L0_ffn_scale, L0_ffn_expert_masks, L0_ffn_router_w):
    import numpy as np
    import concourse.bacc as bacc
    from concourse.bass_utils import run_bass_kernel_spmd

    def lay(a):
        return np.ascontiguousarray(a)

    def bits(a):
        return lay(a)

    inv = (1.0 / np.float32(10000.0) ** (np.arange(0, D, 2, dtype=np.float32) / np.float32(D))).astype(np.float32)
    ang = (np.arange(S, dtype=np.float32)[:, None] * inv[None, :]).astype(np.float32)
    cos, sin = np.cos(ang).astype(np.float32).T, np.sin(ang).astype(np.float32).T
    p_, f_ = np.arange(P)[:, None], np.arange(P)[None, :]
    con = np.zeros((P, 256), np.float32)
    past = np.arange(NCAND)[None, :] < (P // CHUNK + p_ // CHUNK)
    con[:, 0:7] = np.where(past, 0.0, NEG)
    con[:, 8:15] = np.where(past, -NEG, 0.0)
    con[:, 72:104] = np.arange(E_N)
    con[:, 104:104 + SEGS] = np.arange(SEGS)
    con[:, 144:151] = P * np.arange(1, NT)
    con[:, 152:159] = np.arange(1, NT)
    con[:, 176:178], con[:, 178:180] = EPS, -0.5
    con[:, 160:168] = P * np.arange(NT)[None, :] + p_
    tri = np.stack([(p_ < f_) * 1.0, np.ones((P, P))], 1).astype(np.float32)

    def by_slices(a, cols):
        return lay(a.reshape(KC, P, -1, cols).transpose(1, 2, 0, 3).reshape(P, -1))

    c2, s2 = np.concatenate([cos, cos], 0), np.concatenate([-sin, sin], 0)
    arrays = {
        "x": lay(x),
        "ctxT": lay(ctx_512.reshape(B * S, CTX).T),
        "smask": bits(mask_SxS2_bk1),
        "kmask": bits(mask_BxS2_bf0),
        "wq": by_slices(L0_attn_wq, HG * D),
        "wk": by_slices(L0_attn_wk, NG * D),
        "wv": by_slices(L0_attn_wv, NG * D),
        "wo": lay(L0_attn_wo.reshape(NH, D, H).transpose(1, 0, 2).reshape(D, NH * H)),
        "xw": lay(np.concatenate([L0_xattn_Wq.T, L0_xattn_Wk.T, L0_xattn_bq[:, None], L0_xattn_bk[:, None]], 1)),
        "ffw": lay(np.concatenate([by_slices(L0_ffn_weight.T, H), by_slices(L0_ffn_router_w.T, E_N)], 1)),
        "ffscale": lay(L0_ffn_scale),
        "masks": lay(L0_ffn_expert_masks.reshape(E_N, H, KC, P).transpose(3, 0, 2, 1).reshape(P, E_N * KC * H)),
        "tables": lay(np.concatenate([c2, s2, c2 * np.float32(-SCALE), s2 * np.float32(-SCALE)], 1)),
        "consts": lay(np.concatenate([con, np.eye(P, dtype=np.float32)], 1)),
        "tri": lay(tri.reshape(P, 2 * P)),
        "causal": np.where(f_ <= p_, 0.0, -NEG).astype(np.float32),
    }
    nc = bacc.Bacc("TRN2", target_bir_lowering=False, num_devices=1, dynamic_dma_scratch_size=8192)
    feeds, args = {}, []
    for name, a in arrays.items():
        feeds[f"in_{name}_dram"] = a
        args.append(nc.dram_tensor(f"in_{name}_dram", a.shape, mybir.dt.from_np(a.dtype), kind="ExternalInput").ap())
    out = nc.dram_tensor("out_0_dram", (B * S, H), mybir.dt.float32, kind="ExternalOutput").ap()
    scratch = nc.dram_tensor("scratch_rows", (B * S, ROW), mybir.dt.float32, kind="Internal").ap()
    program(nc, *args, out, scratch)
    r = run_bass_kernel_spmd(nc, [feeds], core_ids=[0])
    return r.results[0]["out_0_dram"].reshape(B, S, H)
```

```python
import concourse.bass as bass
from concourse import mybir
from contextlib import ExitStack

B, S, H = 4, 256, 256
NH, NG, D = 16, 4, 128
HG = NH // NG
CHUNK, NCH, TOPK = 32, 8, 4
E_N = 32
CTX = 64
P = 128
KC = H // P
TT = S // P
NT = B * TT
STEPS = NG * 2
SEGS = NT + E_N - 1
SEG_ROWS = (SEGS + 1) // 4
ROW = 264
EPS = 1e-5
SCALE = float(D) ** -0.5
NEG = -1.0e30
MARK, PICKED = 2.0e38, 3.0e38
NCAND = NCH - 1

USES = {0: ["K", "Q", "V0", "V1"], 1: ["Q"], 2: ["K", "Q"], 3: ["Q"],
        4: ["K", "Q"], 5: ["Q"], 6: ["K", "Q"], 7: ["Q"]}
USE0 = {l: sum(len(USES[m]) for m in range(l)) for l in range(9)}
ROPE0 = {l: sum(u in ("K", "Q") for m in range(l) for u in USES[m]) for l in range(9)}
N_USE, N_ROPE, PRE = USE0[8], ROPE0[8], 3
SLICES = ["K", "Q0", "V", "Q1", "O0", "Q2", "Q3", "O1", "O2", "O3"]
LATE_HI = {0: 6, 1: 7, 2: 8, 3: 9}
LATE_LO = {0: 5, 1: 6, 2: 7, 3: 8, 4: 9}
RAW_E = 12


def program(nc, x, ctxT, smask, kmask, wq, wk, wv, wo, xw, ffw, ffscale, masks, tables, consts, causal, out, scratch):
    fp32, f32r, bf16 = mybir.dt.float32, mybir.dt.float32r, mybir.dt.bfloat16
    u32, i32, u8 = mybir.dt.uint32, mybir.dt.int32, mybir.dt.uint8
    ALU, ACT, AX = mybir.AluOpType, mybir.ActivationFunctionType, mybir.AxisListType

    with ExitStack() as ctx:
        def sb(name, shape, dt=fp32):
            return ctx.enter_context(nc.sbuf_tensor(name, shape, dt))

        def pb(name, shape, dt=fp32):
            return ctx.enter_context(nc.psum_tensor(name, shape, dt))

        def sem(name):
            return ctx.enter_context(nc.semaphore(name))

        experts = sb("experts", [P, E_N, KC, H])
        exp_flat = experts[:, :, :, :].rearrange("p e k o -> p (e k o)")
        raw0 = RAW_E * KC * H
        raw = {}
        for i, name in enumerate(SLICES):
            raw[name] = exp_flat[:, raw0 + i * 1024:raw0 + (i + 1) * 1024]
        w_hi = sb("w_hi", [P, len(SLICES), 1024], f32r)
        w_lo = sb("w_lo", [P, len(SLICES), 1024], f32r)
        rows = sb("rows", [P, NT, ROW])
        xscore = sb("xscore", [P, NT, ROW])
        xnrow = sb("xnrow", [P, TT, H])
        xnT_hi = sb("xnT_hi", [P, KC, S], f32r)
        xnT_lo = sb("xnT_lo", [P, KC, S], f32r)
        qs = sb("qs", [P, 2, 2, 2, S])
        qt, swap = qs[:, 0], qs[:, 1]
        kt = sb("kt", [P, 2, S + NCH])
        values = sb("values", [P, TT, NG * D])
        pp = sb("pp", [P, 4, 384])
        probs, pT = pp[:, 0:2], pp[:, 2:4]
        oT_hi = sb("oT_hi", [P, 2, S], f32r)
        oT_lo = sb("oT_lo", [P, 2, S], f32r)
        tab_sb = sb("tab_sb", [P, 4, S])
        cos_sb, sin_sb, cosq_sb, sinq_sb = (tab_sb[:, i] for i in range(4))
        con_all = sb("con_all", [P, 256 + P])
        con, id_sb = con_all[:, 0:256], con_all[:, 256:256 + P]
        id_bf = sb("id_bf", [P, P], bf16)
        ct_bf = sb("ct_bf", [P, 3, P], bf16)
        cau_bf, tri_bf = ct_bf[:, 0], ct_bf[:, 1:3]
        post = sb("post", [P, TT, H])
        bias_x = sb("bias_x", [P, TT, H], bf16)
        smask_sb = sb("smask_sb", [P, TT, S], u8)
        kmask_sb = sb("kmask_sb", [P, B, S], u8)
        small = sb("small", [P, 512])
        xw_all = sb("xw_all", [CTX, 2 * CTX + 2])
        xw_sb = xw_all[:, 0:2 * CTX].rearrange("p (a n) -> p a n", a=2)
        xb_sb = xw_all[:, 2 * CTX:2 * CTX + 2]
        ffn_sb = sb("ffn_sb", [P, KC * H + KC * E_N])
        tern = ffn_sb[:, 0:KC * H].rearrange("p (k o) -> p k o", k=KC)
        rw_sb = ffn_sb[:, KC * H:KC * (H + E_N)].rearrange("p (k e) -> p k e", k=KC)
        tern_flat = tern[:, :, :].rearrange("p k o -> p (k o)")
        fs_sb = sb("fs_sb", [P, H])
        ctx_sb = experts[0:CTX, 6:8, :, :].rearrange("p e k o -> p (e k o)")
        slot_u = sb("slot_u", [P, NT], u32)
        tok_u = sb("tok_u", [P, NT], u32)
        seg_i = sb("seg_i", [P, 3, 4 * SEG_ROWS], i32)
        ct_f = probs[:, 0, :]
        lg8x = sb("lg8x", [P, TT, 8])
        idxx = sb("idxx", [P, TT, 8], u32)
        xqk = experts[0:CTX, 8:12, :, :].rearrange("p e k o -> p (e k o)").rearrange("p (a n) -> p a n", a=2)
        oh = xnrow[:, 0, 0:NT * E_N // 2].bitcast(bf16)
        zero256 = cos_sb
        sortedT = qs[:, :, :, :, :].rearrange("p a b c s -> p a (b c s)")
        expT = values[:, :, :].rearrange("p t n -> p (t n)")
        stage_x = pp[:, :, :].rearrange("p a n -> p (a n)")[:, 0:4 * H].rearrange("p (s k n) -> p s k n", s=4, k=KC)

        cand = con[:, 0:7]
        ncand = con[:, 8:15]
        iota_e = con[:, 72:104]
        iota_j = con[:, 104:104 + SEGS]
        bound = con[:, 144:151]
        tile_no = con[:, 152:159]
        eps2, neg_half2 = con[:, 176:178], con[:, 178:180]
        token = con[:, 160:168]

        nm = [small[:, 4 * i:4 * i + 4] for i in range(2)]
        top = small[:, 408:424].rearrange("p (h n) -> p h n", h=2)
        pick = small[:, 424:440].rearrange("p (h n) -> p h n", h=2)
        sums = [small[:, 16 + 4 * i:20 + 4 * i] for i in range(2)]
        rsum = [small[:, 24 + 4 * i:28 + 4 * i] for i in range(2)]
        gate = small[:, 32:64].rearrange("p (h n) -> p h n", h=2)
        mark = small[:, 208:240].rearrange("p (h n) -> p h n", h=2)
        selb = small[:, 64:80].rearrange("p (h n) -> p h n", h=2)
        bn = small[:, 80:92].rearrange("p (t s) -> p t s", t=2)
        mv = small[:, 92:96].rearrange("p (t s) -> p t s", t=2)
        rstd = small[:, 96:98]
        bn2 = small[:, 100:112].rearrange("p (t s) -> p t s", t=2)
        mv2 = small[:, 112:116].rearrange("p (t s) -> p t s", t=2)
        rstd2 = small[:, 116:118]
        xmx, xnm, xsum, xrs = (small[:, 120 + 2 * i:122 + 2 * i] for i in range(4))
        xany = small[:, 128:130]
        logit = small[:, 136:200].rearrange("p (t e) -> p t e", t=2)
        exp_q = small[:, 240:248]
        lnm, lsum = small[:, 200:202], small[:, 202:204]

        banks = pb("banks", [P, 8, 512])
        proj = banks[:, 0:2]
        sc = banks[:, 2:6]
        ot = banks[:, 6]
        y_flat = banks[:, 7]
        y = y_flat.rearrange("p (t n) -> p t n", t=TT)
        sums_flat = banks[:, :, :].rearrange("p b n -> p (b n)")[:, 2 * 512 - H:2 * 512 + (NT - 1) * H]

        x0_loaded, cross_loaded, masks_loaded = sem("x0_loaded"), sem("cross_loaded"), sem("masks_loaded")
        weight_loaded = [sem(f"weight_loaded{i}") for i in range(len(SLICES))]
        w_hi_ready, w_lo_ready = sem("w_hi_ready"), sem("w_lo_ready")
        normed_rows_ready, xnT_in_bank, xnT_hi_ready, xnT_lo_ready = sem("normed_rows_ready"), sem("xnT_in_bank"), sem("xnT_hi_ready"), sem("xnT_lo_ready")
        proj_filled, proj_read_by_act, proj_read_by_dve = sem("proj_filled"), sem("proj_read_by_act"), sem("proj_read_by_dve")
        sin_part_ready, rotation_done, chunk_sums_ready = sem("sin_part_ready"), sem("rotation_done"), sem("chunk_sums_ready")
        recips_ready = sem("recips_ready")
        scores_ready, row_min_ready, exp_ready, probs_ready = sem("scores_ready"), sem("row_min_ready"), sem("exp_ready"), sem("probs_ready")
        probsT_in_bank, probsT_ready = sem("probsT_in_bank"), sem("probsT_ready")
        product_in_bank, oT_hi_ready, oT_lo_ready, output_added = sem("product_in_bank"), sem("oT_hi_ready"), sem("oT_lo_ready"), sem("output_added")
        dve_softmax, dve_ternary, dve_norm, dve_post = sem("dve_softmax"), sem("dve_ternary"), sem("dve_norm"), sem("dve_post")
        x1_ready, x1_normed, x2_ready, cross_scored = sem("x1_ready"), sem("x1_normed"), sem("x2_ready"), sem("cross_scored")
        cross_max_ready, cross_exp_ready, x2_normed, x2T_in_bank = sem("cross_max_ready"), sem("cross_exp_ready"), sem("x2_normed"), sem("x2T_in_bank")
        x2T_ready = sem("x2T_ready")
        top_found, top_indexed = sem("top_found"), sem("top_indexed")
        logits_in_bank, logits_read, expert_ready, logit_exp_ready = sem("logits_in_bank"), sem("logits_read"), sem("expert_ready"), sem("logit_exp_ready")
        row_facts_ready = sem("row_facts_ready")
        x_rest_loaded, consts_loaded, tables_loaded, ffn_loaded = sem("x_rest_loaded"), sem("consts_loaded"), sem("tables_loaded"), sem("ffn_loaded")
        causal_loaded = sem("causal_loaded")
        mask_bias_ready, pace = sem("mask_bias_ready"), sem("pace")
        var_eps_ready, var_eps2_ready = sem("var_eps_ready"), sem("var_eps2_ready")
        stats_ready, rstd_ready, stats2_ready, rstd2_ready = sem("stats_ready"), sem("rstd_ready"), sem("stats2_ready"), sem("rstd2_ready")
        key_masks_loaded, experts_ready = sem("key_masks_loaded"), sem("experts_ready")
        setup_by_pe, setup_by_act, setup_by_dve = sem("setup_by_pe"), sem("setup_by_act"), sem("setup_by_dve")
        tl = {n: sem("tl_" + n) for n in ("onehot", "counts", "chain", "places", "scattered", "tokens", "row_experts", "normed", "transposed",
                                          "sortedT", "expert_columns", "expT", "zeros", "tables", "segment", "staged", "finished", "written")}
        back = [sem(f"tl_back{m}") for m in range(NT // 2)]

        def use(b, l, name):
            return PRE + N_USE * b + USE0[l] + USES[l].index(name)

        def bank(l, name):
            return (PRE + USE0[l] + USES[l].index(name)) % 2

        def rope(b, l, name):
            return PRE + N_ROPE * b + ROPE0[l] + (0 if name == "K" or l % 2 else 1)

        def need(eng, s, n):
            if not isinstance(n, int) or n > 0:
                eng.wait_ge(s, n)

        def batches(eng, body):
            body(0, True, False)
            with eng.Fori(1, B - 1) as b:
                body(b, False, False)
            body(B - 1, False, True)

        def w(name, part):
            t = w_hi if part == 0 else w_lo
            return t[:, SLICES.index(name), :]

        PARTS = ((0, 0), (0, 1), (1, 0))

        def load_row(engine, table, r):
            return nc.values_load_multi_w_load_instructions(
                seg_i[0:1, table, bass.ds(4 * r, 4)], engines=[engine], min_val=0, max_val=((NT - 1) * H, E_N - 1, (NT - 1) * P)[table],
                skip_runtime_bounds_check_because="a tile is a count of at most NT - 1 edges, and an expert lies below E_N as the last edge does")[1]

        block = ctx.enter_context(nc.Block())

        def read_back(eng, m):
            eng.dma_start(xscore[:, 2 * m:2 * m + 2, :], scratch[2 * m * P:2 * (m + 1) * P].rearrange("(i p) n -> p i n", p=P)).then_inc(back[m], 16)

        @block.sync
        def _(sp):
            xr = x.rearrange("b (t p) n -> p (b t) n", p=P)
            wsrc = {"K": wk, "V": wv}
            wsrc.update({f"Q{g}": wq[:, g * 1024:(g + 1) * 1024] for g in range(NG)})
            wsrc.update({f"O{g}": wo[:, g * 1024:(g + 1) * 1024] for g in range(NG)})

            def load_w(i):
                sp.dma_start(raw[SLICES[i]], wsrc[SLICES[i]]).then_inc(weight_loaded[i], 16)
            sp.dma_start(rows[:, 0:TT, 0:H], xr[:, 0:TT]).then_inc(x0_loaded, 16)
            load_w(0)
            load_w(1)
            sp.dma_start(tab_sb[:, :, :].rearrange("p a s -> p (a s)"), tables).then_inc(tables_loaded, 16)
            for i in range(2, len(SLICES)):
                load_w(i)
                if i == 3:
                    sp.dma_start(rows[:, TT:NT, 0:H], xr[:, TT:NT]).then_inc(x_rest_loaded, 16)
            for i in range(8):
                if 4 * i == RAW_E:
                    sp.wait_ge(w_lo_ready, len(SLICES))
                    sp.wait_ge(w_hi_ready, len(SLICES))
                if i == 1:
                    sp.wait_ge(setup_by_pe, 8)
                if i % 2 == 0 and i > 0:
                    sp.wait_ge(masks_loaded, 16 * i)
                sp.dma_start(experts[:, 4 * i:4 * i + 4].rearrange("p e k o -> p (e k o)"),
                             masks[:, 4 * i * KC * H:4 * (i + 1) * KC * H]).then_inc(masks_loaded, 16)

            sp.wait_ge(tl["scattered"], 16 * NT)
            for m in range(0, NT // 2, 2):
                read_back(sp, m)

        @block.gpsimd
        def _(pool):
            def inverse_std(mv_, rstd_, s_in, n, s_out, s_add):
                pool.wait_ge(s_in, n)
                nc.gpsimd.tensor_tensor(rstd_, mv_[:, :, 1], eps2, ALU.add).then_inc(s_add, 1)
                pool.wait_ge(s_add, n)
                nc.gpsimd.tensor_tensor(rstd_, rstd_, neg_half2, ALU.pow).then_inc(s_out, 1)

            def rotate(i, r, n_, width, dst):
                sw = swap[:, i % 2, 0:width, :]
                pool.wait_ge(proj_read_by_act, n_ + 1)
                nc.gpsimd.tensor_tensor(sw, sw, (sin_sb if width == 1 else sinq_sb)[:, :].unsqueeze(1).to_broadcast([P, width, S]), ALU.mult).then_inc(sin_part_ready, 1)
                pool.wait_ge(proj_read_by_dve, r + 1)
                pool.wait_ge(sin_part_ready, r + 1)
                nc.gpsimd.tensor_tensor(dst, dst, sw, ALU.add).then_inc(rotation_done, 1)

            pool.dma_start(ct_f, causal).then_inc(causal_loaded, 16)
            pool.wait_ge(consts_loaded, 16)
            inverse_std(mv, rstd, stats_ready, 1, rstd_ready, var_eps_ready)
            pool.dma_start(smask_sb[:, :, :], smask.rearrange("(t p) s -> p t s", p=P)).then_inc(key_masks_loaded, 16)
            pool.dma_start(kmask_sb[:, :, :].rearrange("p b s -> p (b s)"),
                           kmask.rearrange("b s -> (b s)").rearrange("(a n) -> a n", a=1).to_broadcast([P, B * S])).then_inc(key_masks_loaded, 16)
            pool.dma_start(ffn_sb[:, :], ffw).then_inc(ffn_loaded, 16)
            pool.dma_start(fs_sb[:, :], ffscale.rearrange("(a n) -> a n", a=1).to_broadcast([P, H])).then_inc(ffn_loaded, 16)
            pool.wait_ge(tables_loaded, 16)
            rotate(0, 0, 0, 1, kt[:, 0:1, 0:S])
            rotate(1, 1, 1, 2, qt[:, 0])
            rotate(2, 2, 2, 2, qt[:, 1])

            def body(b, first, last):
                for l in range(STEPS):
                    v = b * STEPS + l
                    if not (last and l >= 6):
                        for name in USES[l]:
                            if name in ("K", "Q"):
                                r = rope(b, l, name)
                                i = PRE + ROPE0[l] + (0 if name == "K" or l % 2 else 1)
                                n_ = use(b, l, name)
                                if name == "K":
                                    g = (l // 2 + 1) % NG
                                    rotate(i, r, n_, 1, kt[:, g % 2:g % 2 + 1, 0:S])
                                else:
                                    rotate(i, r, n_, 2, qt[:, l % 2])
                    if l == 0:
                        pool.wait_ge(masks_loaded, 32 * (b + 1))
                    if first and l == 0:
                        pool.wait_ge(dve_ternary, 4)
                    e_ap = experts[:, bass.ds(b * STEPS + l, 1), :, :].rearrange("p a k o -> p (a k o)")
                    nc.gpsimd.tensor_tensor(e_ap, e_ap, tern_flat, ALU.mult).then_inc(experts_ready, 1)
                    if l == 3 and not last:
                        inverse_std(mv, rstd, stats_ready, b + 2, rstd_ready, var_eps_ready)
                    if not first and l in (1, 4):
                        inverse_std(mv2, rstd2, stats2_ready, 2 * (b - 1) + (1 if l == 1 else 2), rstd2_ready, var_eps2_ready)
                    if not first and l == 2:
                        cross_scores(b - 1)

            def cross_scores(p):
                pool.wait_ge(x1_normed, p + 1)
                if isinstance(p, int) and p == 0:
                    pool.wait_ge(setup_by_act, 8)
                nc.gpsimd.tensor_tensor(post[:, :, :], post[:, :, :], xscore[:, bass.ds(TT * p, TT), 0:S], ALU.mult).then_inc(cross_scored, 1)
                pool.wait_ge(cross_scored, 2 * p + 1)
                pool.wait_ge(mask_bias_ready, 2 * p + 2)
                nc.gpsimd.tensor_tensor(post[:, :, :], post[:, :, :], bias_x[:, :, :], ALU.add).then_inc(cross_scored, 1)

            batches(pool, body)
            inverse_std(mv2, rstd2, stats2_ready, 2 * B - 1, rstd2_ready, var_eps2_ready)
            inverse_std(mv2, rstd2, stats2_ready, 2 * B, rstd2_ready, var_eps2_ready)
            pool.wait_ge(cross_scored, 2 * B)
            nc.gpsimd.memset(bias_x[:, :, :], 0.0).then_inc(tl["zeros"], 1)
            for i in range(NT):
                if i == 0:
                    pool.wait_ge(tl["places"], 1)
                nc.gpsimd.indirect_dma_start(scratch, bass.IndirectOffsetOnAxis(slot_u[:, i:i + 1], 0),
                                             rows[:, i, :], None).then_inc(tl["scattered"], 16)
            pool.wait_ge(tl["tokens"], 1)
            for i in range(NT):
                pool.wait_ge(tl["finished"], i + 1)
                nc.gpsimd.indirect_dma_start(out, bass.IndirectOffsetOnAxis(tok_u[:, i:i + 1], 0),
                                             xscore[:, i, 0:H], None).then_inc(tl["written"], 16)
            pool.wait_ge(tl["written"], 16 * NT)


        @block.scalar
        def _(act):
            act.dma_start(con_all[:, :], consts).then_inc(consts_loaded, 16)
            act.dma_start(xw_all[:, :], xw).then_inc(cross_loaded, 16)
            act.dma_start(ctx_sb, ctxT).then_inc(cross_loaded, 16)

            def split_hi(i):
                act.wait_ge(weight_loaded[i], 16)
                nc.scalar.activation(w_hi[:, i, :], raw[SLICES[i]], ACT.Copy).then_inc(w_hi_ready, 1)

            def copy_ot(dst, s_):
                nc.scalar.activation(dst, ot[:, :], ACT.Copy).then_inc(s_, 1)

            def halves(i, r, n_, bk, width):
                act.wait_ge(proj_filled, n_ + 1)
                need(act, rotation_done, r - 1)
                src = proj[:, bk, 0:width * S].rearrange("p (h s) -> p h s", h=width)
                nc.scalar.activation(swap[0:64, i % 2, 0:width, :], src[64:128], ACT.Copy)
                nc.scalar.activation(swap[64:128, i % 2, 0:width, :], src[0:64], ACT.Copy).then_inc(proj_read_by_act, 1)

            split_hi(0)
            act.wait_ge(xnT_in_bank, 1)
            copy_ot(xnT_hi[:, :, :].rearrange("p k s -> p (k s)"), xnT_hi_ready)
            split_hi(1)
            halves(0, 0, 0, 0, 1)
            split_hi(2)
            halves(1, 1, 1, 1, 2)
            halves(2, 2, 2, 0, 2)
            split_hi(3)
            spare = [sc[:, 2, :], sc[:, 3, :], y[:, :, :].rearrange("p t n -> p (t n)"), ot[:, :]]
            for i in range(4):
                act.wait_ge(setup_by_pe, i + 1)
                nc.scalar.activation(xqk[:, i % 2, (i // 2) * 512:(i // 2 + 1) * 512], spare[i][0:CTX, :], ACT.Identity,
                                     bias=xb_sb[:, i % 2:i % 2 + 1]).then_inc(setup_by_act, 1)
            for i in range(NT // 2):
                act.wait_ge(setup_by_pe, 5 + i)
                nc.scalar.activation(xscore[:, 2 * i:2 * i + 2, 0:S], spare[i].rearrange("p (t n) -> p t n", t=2), ACT.Copy,
                                     scale=CTX ** -0.5).then_inc(setup_by_act, 1)
                if i == 0:
                    split_hi(4)
            split_hi(5)

            def body(b, first, last):
                for l in range(STEPS):
                    v = b * STEPS + l
                    def swaps():
                        if not (last and l >= 6):
                            for name in USES[l]:
                                if name in ("K", "Q"):
                                    i = PRE + ROPE0[l] + (0 if name == "K" or l % 2 else 1)
                                    halves(i, rope(b, l, name), use(b, l, name), bank(l, name), 1 if name == "K" else 2)
                    if not first and l == 7:
                        post_act(b - 1, 6)
                    swaps()
                    if l == 5 and not last:
                        act.wait_ge(xnT_in_bank, b + 2)
                        nc.scalar.activation(xnT_hi[:, :, :].rearrange("p k s -> p (k s)"), proj[:, bank(6, "K"), :], ACT.Copy).then_inc(xnT_hi_ready, 1)
                    if not (first and l == 0):
                        act.wait_ge(probsT_in_bank, v)
                        need(act, product_in_bank, v - 1)
                        qq = (l - 1) % 2
                        nc.scalar.activation(pT[:, :, :], sc[:, 2 * qq:2 * qq + 2, 0:384], ACT.Copy).then_inc(probsT_ready, 1)
                    act.wait_ge(row_min_ready, v + 1)
                    need(act, probsT_in_bank, v)
                    q = l % 2
                    for h in range(2):
                        nc.scalar.activation(probs[:, h, 0:P], sc[:, 2 * q + h, 0:P], ACT.Exp, bias=nm[q][:, h:h + 1],
                                             scale=-1.0, accum_out=sums[q][:, h:h + 1])
                        last_i = nc.scalar.activation(probs[:, h, P:384], sc[:, 2 * q + h, P:384], ACT.Exp,
                                                      bias=nm[q][:, 2 + h:3 + h], scale=-1.0, accum_out=sums[q][:, 2 + h:3 + h])
                    last_i.then_inc(exp_ready, 1)

                    def product_hi():
                        act.wait_ge(product_in_bank, v)
                        need(act, output_added, v - 1)
                        copy_ot(oT_hi[:, :, :].rearrange("p k s -> p (k s)"), oT_hi_ready)

                    if not (first and l == 0) and not (last and l == 7):
                        product_hi()
                    act.wait_ge(recips_ready, v + 1)
                    for h in range(2):
                        nc.scalar.activation(probs[:, h, 0:P], probs[:, h, 0:P], ACT.Copy, scale=rsum[q][:, h:h + 1])
                        last_i = nc.scalar.activation(probs[:, h, P:384], probs[:, h, P:384], ACT.Copy, scale=rsum[q][:, 2 + h:3 + h])
                    last_i.then_inc(probs_ready, 1)
                    if last and l == 7:
                        product_hi()
                    if first and l in LATE_HI:
                        split_hi(LATE_HI[l])
                    if l == 0:
                        for i, name in enumerate(("V0", "V1")):
                            act.wait_ge(proj_filled, use(b, 0, name) + 1)
                            nc.scalar.activation(values[:, i, :], proj[:, bank(0, name), :], ACT.Copy).then_inc(proj_read_by_act, 1)
                    if not first and l != 6 and not (last and l == 7):
                        post_act(b - 1, l)

            def post_act(p, l):
                if l == 3:
                    act.wait_ge(cross_max_ready, p + 1)
                    for t in range(TT):
                        i = nc.scalar.activation(post[:, t, :], post[:, t, :], ACT.Exp, bias=xnm[:, t:t + 1],
                                                 accum_out=xsum[:, t:t + 1])
                    i.then_inc(cross_exp_ready, 1)
                if l == 6:
                    act.wait_ge(x2T_in_bank, p + 1)
                    copy_ot(post[:, :, :].rearrange("p k s -> p (k s)"), x2T_ready)
                if l == 7:
                    act.wait_ge(expert_ready, p + 1)
                    for t in range(TT):
                        i = nc.scalar.activation(logit[:, t, :], logit[:, t, :], ACT.Exp, bias=lnm[:, t:t + 1],
                                                 accum_out=lsum[:, t:t + 1])
                    i.then_inc(logit_exp_ready, 1)

            batches(act, body)
            V = B * STEPS
            act.wait_ge(probsT_in_bank, V)
            act.wait_ge(product_in_bank, V - 1)
            nc.scalar.activation(pT[:, :, :], sc[:, 2:4, 0:384], ACT.Copy).then_inc(probsT_ready, 1)
            post_act(B - 2, 7)
            act.wait_ge(product_in_bank, V)
            act.wait_ge(output_added, V - 1)
            copy_ot(oT_hi[:, :, :].rearrange("p k s -> p (k s)"), oT_hi_ready)
            for l in range(STEPS):
                post_act(B - 1, l)
            act.wait_ge(tl["scattered"], 16 * NT)
            for m in range(1, NT // 2, 2):
                read_back(act, m)
            act.wait_ge(tl["expert_columns"], 1)
            nc.scalar.activation(expT[:, 0:4 * P], proj[:, 0], ACT.Copy)
            nc.scalar.activation(expT[:, 4 * P:NT * P], y_flat, ACT.Copy).then_inc(tl["expT"], 1)
            for m in range(NT // 2):
                act.wait_ge(tl["transposed"], m + 1)
                nc.scalar.activation(sortedT[:, :, 2 * m * P:2 * (m + 1) * P].rearrange("p k (i s) -> p i k s", i=2),
                                     (ot[:, :] if m % 2 == 0 else y_flat).rearrange("p (i k s) -> p i k s", i=2, k=KC), ACT.Copy).then_inc(tl["sortedT"], 1)

        @block.vector
        def _(dve):
            def tt(out_, a, b_, op):
                return nc.vector.tensor_tensor(out_, a, b_, op)

            def carrier():
                dve.sem_inc(pace, 1)

            class Chain:
                def __init__(self, s, per):
                    self.s, self.per, self.base, self.n = s, per, 0, 0

                def at(self, base):
                    self.base, self.n = base, 0

                def count(self, ins):
                    self.n += 1
                    ins.then_inc(self.s, 1)

                def wait(self, carry=False):
                    dve.wait_ge(self.s, self.base + self.n)
                    if carry:
                        carrier()

                def __call__(self, ins, carry=False):
                    self.count(ins)
                    self.wait(carry)

            def split_lo(i):
                dve.wait_ge(w_hi_ready, i + 1)
                nc.vector.tensor_tensor(w_lo[:, i, :], raw[SLICES[i]], w_hi[:, i, :].bitcast(fp32), ALU.subtract).then_inc(w_lo_ready, 1)

            def row_stats(chain, src, bn_, mv_, done):
                carrier()
                for t in range(TT):
                    i = nc.vector.bn_stats(bn_[:, t, :], src[:, t, :])
                chain(i, carry=True)
                for t in range(TT):
                    i = nc.vector.bn_aggr(mv_[:, t, :], bn_[:, t, :])
                i.then_inc(done, 1)

            def row_apply(src, dst, mv_, rstd_, done):
                for t in range(TT):
                    i = nc.vector.tensor_scalar(dst[:, t, :], src[:, t, :], mv_[:, t, 0:1], rstd_[:, t:t + 1], ALU.subtract, ALU.mult)
                i.then_inc(done, 1)

            LN_N = 1
            ln = Chain(dve_norm, LN_N)

            def norm_stats(b):
                ln.at(b * LN_N)
                if isinstance(b, int) and b == 0:
                    dve.wait_ge(x0_loaded, 16)
                else:
                    dve.wait_ge(x_rest_loaded, 16)
                row_stats(ln, rows[:, bass.ds(TT * b, TT), 0:H], bn, mv, stats_ready)

            def norm_apply(b):
                need(dve, xnT_in_bank, b)
                dve.wait_ge(rstd_ready, b + 1)
                row_apply(rows[:, bass.ds(TT * b, TT), 0:H], xnrow, mv, rstd, normed_rows_ready)

            def xt_lo(bank_):
                return nc.vector.tensor_tensor(xnT_lo[:, :, :].rearrange("p k s -> p (k s)"), bank_,
                                               xnT_hi[:, :, :].rearrange("p k s -> p (k s)").bitcast(fp32), ALU.subtract).then_inc(xnT_lo_ready, 1)

            def times_cos(n_, bk, width, dst):
                dve.wait_ge(proj_read_by_act, n_ + 1)
                tt(dst, proj[:, bk, 0:width * S].rearrange("p (h s) -> p h s", h=width),
                   (cos_sb if width == 1 else cosq_sb)[:, :].unsqueeze(1).to_broadcast([P, width, S]), ALU.mult).then_inc(proj_read_by_dve, 1)

            def chunk_sums(g, r):
                dve.wait_ge(rotation_done, r + 1)
                nc.vector.tensor_reduce(kt[:, g % 2, S:S + NCH], kt[:, g % 2, 0:S].rearrange("p (n c) -> p n c", c=CHUNK),
                                        AX.X, ALU.add).then_inc(chunk_sums_ready, 1)

            norm_stats(0)
            nc.vector.memset(selb, 0.0)
            nc.vector.memset(gate[:, :, NCAND:8], 2 * NEG)
            nc.vector.memset(gate[:, :, 8:16], MARK)
            nc.vector.memset(pick, MARK).then_inc(setup_by_dve, 1)
            dve.sem_inc(logits_read, 1)
            norm_apply(0)
            split_lo(0)
            dve.wait_ge(xnT_in_bank, 1)
            dve.wait_ge(xnT_hi_ready, 1)
            xt_lo(ot[:, :])
            split_lo(1)
            dve.wait_ge(tables_loaded, 16)
            dve.wait_ge(causal_loaded, 16)
            nc.vector.tensor_copy(id_bf[:, :], id_sb[:, :])
            nc.vector.tensor_copy(ct_bf[:, :, :].rearrange("p a b -> p (a b)"), ct_f).then_inc(setup_by_dve, 1)
            times_cos(0, 0, 1, kt[:, 0:1, 0:S])
            times_cos(1, 1, 2, qt[:, 0])
            chunk_sums(0, 0)
            times_cos(2, 0, 2, qt[:, 1])
            for i in range(2, 5):
                split_lo(i)

            def ternary():
                dve.wait_ge(ffn_loaded, 32)
                nc.vector.tensor_scalar(tern_flat, tern_flat, 2.0, 1.0, ALU.mult, ALU.min).then_inc(dve_ternary, 1)
                dve.wait_ge(dve_ternary, 1)
                nc.vector.tensor_scalar(tern_flat, tern_flat, -1.0, 12582912.0, ALU.max, ALU.add).then_inc(dve_ternary, 1)
                dve.wait_ge(dve_ternary, 2)
                nc.vector.tensor_scalar(tern_flat, tern_flat, 12582912.0, None, ALU.subtract).then_inc(dve_ternary, 1)
                dve.wait_ge(dve_ternary, 3)
                tt(tern[:, :, :], tern[:, :, :], fs_sb[:, :].unsqueeze(1).to_broadcast([P, KC, H]), ALU.mult).then_inc(dve_ternary, 1)

            SM_N = 5
            sm = Chain(dve_softmax, SM_N)

            def softmax_max(v, l):
                q = l % 2
                s2 = sc[:, 2 * q:2 * q + 2, :]
                sm.at(v * SM_N)
                dve.wait_ge(scores_ready, v + 1)
                sm.count(tt(gate[:, :, 0:NCAND], cand.unsqueeze(1).to_broadcast([P, 2, NCAND]), s2[:, :, 384:384 + NCAND], ALU.subtract))
                nc.vector.tensor_reduce(nm[q][:, 0:2], s2[:, :, 0:P], AX.X, ALU.min)
                sm.wait(carry=True)
                for h in range(2):
                    i = nc.vector.max(top[:, h, :], gate[:, h, 0:8])
                sm(i)
                sm(nc.vector.tensor_copy(pick[:, :, 0:TOPK - 1], top[:, :, 0:TOPK - 1]), carry=True)
                for h in range(2):
                    i = nc.vector.match_replace(mark[:, h, :], pick[:, h, :], gate[:, h, :], PICKED)
                sm(i)
                sm(nc.vector.scalar_tensor_tensor(selb[:, :, 0:NCAND], mark[:, :, 0:NCAND], PICKED, ncand.unsqueeze(1).to_broadcast([P, 2, NCAND]),
                                                  ALU.is_lt, ALU.mult), carry=True)
                for h in range(2):
                    view = s2[:, h, P:384].rearrange("p (n c) -> p n c", c=CHUNK)
                    i = nc.vector.tensor_tensor_reduce(out=view, in0=view, in1=selb[:, h].unsqueeze(2).to_broadcast([P, NCH, CHUNK]),
                                                       scale=1.0, scalar=3.0e38, op0=ALU.add, op1=ALU.min, accum_out=nm[q][:, 2 + h:3 + h])
                i.then_inc(row_min_ready, 1)

            def reciprocals(v, l):
                dve.wait_ge(exp_ready, v + 1)
                nc.vector.reciprocal(rsum[l % 2], sums[l % 2]).then_inc(recips_ready, 1)

            def ot_lo(v1):
                dve.wait_ge(oT_hi_ready, v1 + 1)
                tt(oT_lo[:, :, :].rearrange("p k s -> p (k s)"), ot[:, :], oT_hi[:, :, :].rearrange("p k s -> p (k s)").bitcast(fp32),
                   ALU.subtract).then_inc(oT_lo_ready, 1)

            def body(b, first, last):
                for l in range(STEPS):
                    v = b * STEPS + l
                    softmax_max(v, l)

                    def cosines():
                        if not (last and l >= 6):
                            for name in USES[l]:
                                if name == "K":
                                    g = (l // 2 + 1) % NG
                                    times_cos(use(b, l, name), bank(l, name), 1, kt[:, g % 2:g % 2 + 1, 0:S])
                                if name == "Q":
                                    times_cos(use(b, l, name), bank(l, name), 2, qt[:, l % 2])
                    if not first and l == 7:
                        take_logits(b - 1)
                    if l == 5 and not last:
                        dve.wait_ge(xnT_hi_ready, b + 2)
                        xt_lo(proj[:, bank(6, "K"), :])
                    cosines()
                    reciprocals(v, l)
                    if not (first and l == 0):
                        ot_lo(v - 1)
                    if "K" in USES[l] and not (last and l >= 6):
                        chunk_sums((l // 2 + 1) % NG, rope(b, l, "K"))
                    if first and l == 0:
                        ternary()
                    if first and l in LATE_LO:
                        split_lo(LATE_LO[l])
                    if l == 4 and not last:
                        norm_apply(b + 1)
                    if not first:
                        post_dve(b - 1, l)
                    if l == 3 and not last:
                        norm_stats(b + 1)

            POST_N = 7
            pc = Chain(dve_post, POST_N)

            def top_weight(p):
                dve.wait_ge(logit_exp_ready, p + 1)
                nc.vector.reciprocal(rows[:, bass.ds(TT * p, TT), 257:258].rearrange("p t a -> p (t a)"), lsum).then_inc(row_facts_ready, 1)

            def take_logits(p):
                dve.wait_ge(logits_in_bank, p + 1)
                nc.vector.tensor_copy(logit, ot[:, 0:TT * E_N].rearrange("p (t e) -> p t e", t=TT)).then_inc(logits_read, 1)

            def post_dve(p, l):
                base = p * POST_N
                r2 = rows[:, bass.ds(TT * p, TT), 0:H]
                if l == 1:
                    dve.wait_ge(output_added, STEPS * (p + 1))
                    tt(r2, r2, y[:, :, :], ALU.add).then_inc(x1_ready, 1)
                    pc.at(base)
                    dve.wait_ge(x1_ready, p + 1)
                    row_stats(pc, r2, bn2, mv2, stats2_ready)
                if l == 0:
                    if isinstance(p, int) and p == 0 or not isinstance(p, int):
                        dve.wait_ge(key_masks_loaded, 32)
                    tt(bias_x[:, :, :], smask_sb[:, :, :], kmask_sb[:, bass.ds(p, 1), :].to_broadcast([P, TT, S]), ALU.max).then_inc(mask_bias_ready, 1)
                    dve.wait_ge(mask_bias_ready, 2 * p + 1)
                    nc.vector.tensor_scalar(bias_x[:, :, :], bias_x[:, :, :], NEG, None, ALU.mult).then_inc(mask_bias_ready, 1)
                if l == 2:
                    dve.wait_ge(rstd2_ready, 2 * p + 1)
                    row_apply(r2, post, mv2, rstd2, x1_normed)
                    if isinstance(p, int) and p == B - 1:
                        dve.wait_ge(x1_normed, B)
                        tt(post[:, :, :], post[:, :, :], xscore[:, TT * p:TT * (p + 1), 0:S], ALU.mult).then_inc(cross_scored, 1)
                        dve.wait_ge(cross_scored, 2 * p + 1)
                        for t in range(TT):
                            i = nc.vector.tensor_tensor_reduce(out=post[:, t, :], in0=post[:, t, :], in1=bias_x[:, t, :], scale=1.0,
                                                               scalar=2 * NEG, op0=ALU.add, op1=ALU.max, accum_out=xmx[:, t:t + 1])
                        i.then_inc(cross_scored, 1)
                if l == 3:
                    dve.wait_ge(cross_scored, 2 * p + 2)
                    pc.at(base + 1)
                    if isinstance(p, int) and p == B - 1:
                        pc.count(nc.vector.nop())
                    else:
                        pc(nc.vector.tensor_reduce(xmx, post[:, :, :], AX.X, ALU.max))
                    nc.vector.tensor_scalar(xnm, xmx, -1.0, None, ALU.mult).then_inc(cross_max_ready, 1)
                if l == 4:
                    pc.at(base + 2)
                    pc(nc.vector.tensor_scalar(xany, xmx, NEG / 2, None, ALU.is_gt))
                    dve.wait_ge(cross_exp_ready, p + 1)
                    pc(tt(xsum, xsum, xany, ALU.mult))
                    pc(nc.vector.reciprocal(xrs, xsum))
                    pc(tt(xrs, xrs, xany, ALU.mult))
                    for t in range(TT):
                        i = nc.vector.scalar_tensor_tensor(rows[:, bass.ds(TT * p + t, 1), 0:H].rearrange("p a n -> p (a n)"), post[:, t, :], xrs[:, t:t + 1],
                                                           rows[:, bass.ds(TT * p + t, 1), 0:H].rearrange("p a n -> p (a n)"), ALU.mult, ALU.add)
                    i.then_inc(x2_ready, 1)
                    dve.wait_ge(x2_ready, p + 1)
                    row_stats(pc, r2, bn2, mv2, stats2_ready)
                if l == 5:
                    dve.wait_ge(rstd2_ready, 2 * p + 2)
                    row_apply(r2, post, mv2, rstd2, x2_normed)
                if l == 7:
                    dve.wait_ge(logits_read, p + 2)
                    carrier()
                    for t in range(TT):
                        nc.vector.max(lg8x[:, t, :], logit[:, t, :]).then_inc(top_found, 1)
                    dve.wait_ge(top_found, 2 * p + 2)
                    carrier()
                    for t in range(TT):
                        nc.vector.max_index(idxx[:, t, :], lg8x[:, t, :], logit[:, t, :]).then_inc(top_indexed, 1)
                    nc.vector.tensor_scalar(lnm, lg8x[:, :, 0], -1.0, None, ALU.mult)
                    dve.wait_ge(top_indexed, 2 * p + 2)
                    nc.vector.tensor_scalar(rows[:, bass.ds(TT * p, TT), 256:257].rearrange("p t a -> p (t a)"), idxx[:, :, 0],
                                            float(E_N - 1), None, ALU.min).then_inc(expert_ready, 1)
                    nc.vector.tensor_copy(rows[:, bass.ds(TT * p, TT), 259:260].rearrange("p t a -> p (t a)"), mv2[:, :, 0])
                    nc.vector.tensor_copy(rows[:, bass.ds(TT * p, TT), 260:261].rearrange("p t a -> p (t a)"), rstd2)
                    if not (isinstance(p, int) and p == B - 1):
                        top_weight(p)

            batches(dve, body)
            V = B * STEPS
            post_dve(B - 1, 0)
            tc = Chain(tl["chain"], 0)
            tc.count(nc.vector.tensor_copy(rows[:, :, 258], token))
            tc.count(nc.vector.memset(rows[:, :, 261:264], 0.0))
            tc.count(nc.vector.memset(zero256, 0.0))
            nc.vector.memset(seg_i[:, :, 0:1], 0).then_inc(tl["tables"], 1)
            ot_lo(V - 1)
            for l in range(1, STEPS):
                if l == 7:
                    take_logits(B - 1)
                post_dve(B - 1, l)
            dve.wait_ge(expert_ready, B)
            oh3 = oh.rearrange("p (e i) -> p i e", i=NT)
            tt(oh3, rows[:, :, 256].unsqueeze(2).to_broadcast([P, NT, E_N]), iota_e.unsqueeze(1).to_broadcast([P, NT, E_N]),
               ALU.is_equal).then_inc(tl["onehot"], 1)
            top_weight(B - 1)
            dve.wait_ge(tl["counts"], 1)
            tc.wait()
            cnt = proj[:, 1, 0:256]
            run = post[:, 1, :]
            run3 = run.rearrange("p (e i) -> p e i", e=E_N)
            tc(nc.vector.tensor_tensor_scan(run, cnt, zero256, 0.0, ALU.add, ALU.add))
            dve.wait_ge(tl["counts"], 2)
            wk1 = probs[:, 0, 0:256]
            tc(tt(wk1, proj[:, 0, 0:256], run, ALU.add))
            tc(tt(wk1, wk1, oh, ALU.mult))
            place = small[:, 0:NT]
            tc(nc.vector.tensor_reduce(place, wk1.rearrange("p (e i) -> p i e", i=NT), AX.X, ALU.add))
            nc.vector.tensor_copy(slot_u[:, :], place).then_inc(tl["places"], 1)
            q_c = swap[:, 0, 0, :].rearrange("p (i e) -> p i e", i=NT)
            incl = run3[:, :, NT - 1]
            tc(tt(q_c, incl.unsqueeze(1).to_broadcast([P, NT, E_N]), token.unsqueeze(2).to_broadcast([P, NT, E_N]), ALU.is_le))
            nc.vector.tensor_reduce(exp_q, q_c, AX.X, ALU.add).then_inc(tl["row_experts"], 1)
            edge_c = probs[:, 1, 0:7 * E_N].rearrange("p (i e) -> p i e", i=NT - 1)
            tc(tt(edge_c, incl.unsqueeze(1).to_broadcast([P, NT - 1, E_N]), bound.unsqueeze(2).to_broadcast([P, NT - 1, E_N]), ALU.is_lt))
            edge = small[:, 16:23]
            tc(nc.vector.tensor_reduce(edge, edge_c, AX.X, ALU.add))
            tc(tt(edge, edge, tile_no, ALU.add))
            seg_c = post[:, :, :].rearrange("p a b -> p (a b)")[:, 0:SEGS * (NT - 1)].rearrange("p (j i) -> p j i", i=NT - 1)
            tc(tt(seg_c, edge.unsqueeze(1).to_broadcast([P, SEGS, NT - 1]), iota_j.unsqueeze(2).to_broadcast([P, SEGS, NT - 1]), ALU.is_le))
            tile_f = small[:, 32:32 + SEGS]
            tc(nc.vector.tensor_reduce(tile_f, seg_c, AX.X, ALU.add))
            exp_f = small[:, 80:80 + SEGS]
            tc(tt(exp_f, iota_j, tile_f, ALU.subtract))
            nc.vector.tensor_scalar(seg_i[:, 0, 1:1 + SEGS], tile_f, float(H), None, ALU.mult)
            nc.vector.tensor_scalar(seg_i[:, 2, 1:1 + SEGS], tile_f, float(P), None, ALU.mult)
            nc.vector.tensor_copy(seg_i[:, 1, 1:1 + SEGS], exp_f).then_inc(tl["tables"], 1)

            def normalise(i):
                dve.wait_ge(back[i // 2], 16)
                if i > 3:
                    dve.wait_ge(tl["transposed"], i // 2 - 1)
                nc.vector.tensor_scalar((xnrow, post)[(i // 2) % 2][:, i % 2, :], xscore[:, i, 0:H], xscore[:, i, 259:260], xscore[:, i, 260:261],
                                        ALU.subtract, ALU.mult).then_inc(tl["normed"], 1)

            def stage(r, first, between=None):
                cols = load_row(mybir.EngineType.DVE, 2, r)
                for k in range(1 if first else 0, 4):
                    j = 4 * r + k - 1
                    if isinstance(j, int) and j < NT:
                        dve.wait_ge(tl["sortedT"], j // 2 + 1)
                        dve.wait_ge(tl["expT"], 1)
                    need(dve, tl["segment"], j - 3)
                    nc.vector.scalar_tensor_tensor(stage_x[:, k], expT[:, bass.ds(cols[k], P)].unsqueeze(1).to_broadcast([P, KC, P]), exp_f[:, bass.ds(j, 1)],
                                                   sortedT[:, :, bass.ds(cols[k], P)], ALU.is_equal, ALU.mult).then_inc(tl["staged"], 1)
                    if between and k < 3:
                        between(k)

            def finish(first_tile, last_tile):
                dve.wait_ge(tl["segment"], E_N + last_tile)
                for i in range(first_tile, last_tile + 1):
                    nc.vector.scalar_tensor_tensor(xscore[:, i, 0:H], sums_flat[:, i * H:(i + 1) * H], xscore[:, i, 257:258],
                                                   xscore[:, i, 0:H], ALU.mult, ALU.add).then_inc(tl["finished"], 1)

            def normalise_pair(m):
                normalise(2 * m)
                normalise(2 * m + 1)
            normalise_pair(0)
            normalise_pair(1)
            dve.wait_ge(tl["tables"], 2)
            stage(0, True, lambda k: normalise_pair(k + 1))
            stage(1, False)
            nc.vector.tensor_copy(tok_u[:, :], xscore[:, :, 258]).then_inc(tl["tokens"], 1)
            with dve.Fori(2, SEG_ROWS - 1) as r:
                stage(r, False)
            stage(SEG_ROWS - 1, False, lambda k: finish(0, 0) if k == 0 else finish(1, 2) if k == 1 else None)
            finish(3, 4)
            finish(5, 6)
            finish(7, 7)

        @block.tensor
        def _(pe):
            mm = nc.tensor.matmul

            spare = [sc[:, 2, :], sc[:, 3, :], y[:, :, :].rearrange("p t n -> p (t n)"), ot[:, :]]

            def transposes(src, bank_):
                for t in range(TT):
                    for kc in range(KC):
                        i = nc.tensor.transpose(bank_[:, kc * S + t * P:kc * S + (t + 1) * P], src[:, t, kc * P:(kc + 1) * P], id_sb[:, :])
                return i
            pe.wait_ge(consts_loaded, 16)
            pe.wait_ge(normed_rows_ready, 1)
            transposes(xnrow, ot).then_inc(xnT_in_bank, 1)

            def cross_attention():
                pe.wait_ge(cross_loaded, 32)
                for i in (0, 1, 2, 3):
                    if i == 3:
                        pe.wait_ge(xnT_lo_ready, 1)
                    mm(spare[i][0:CTX, :], xw_sb[:, i % 2, :], ctx_sb[:, (i // 2) * 512:(i // 2 + 1) * 512],
                       start=True, stop=True).then_inc(setup_by_pe, 1)
                for i in range(NT):
                    if i % 4 == 0:
                        pe.wait_ge(setup_by_act, 2 + i // 2)
                    bb, t = i // TT, i % TT
                    xs = mm(spare[i // 2][:, (i % 2) * S:(i % 2 + 1) * S], xqk[:, 0, bb * S + t * P:bb * S + (t + 1) * P],
                            xqk[:, 1, bb * S:(bb + 1) * S], start=True, stop=True)
                    if i % 2:
                        xs.then_inc(setup_by_pe, 1)

            def dve_seen(n_, b, l, name):
                if isinstance(n_, int) and n_ < PRE:
                    return n_ - 1
                before = [u for m in range(l + 1) for u in USES[m]][:USE0[l] + USES[l].index(name)]
                if not before:
                    return PRE + N_ROPE * b - 1
                return PRE + N_ROPE * b + sum(u in ("K", "Q") for u in before[:-1])

            def project(name, b, l, n_, bk, g):
                need(pe, proj_read_by_act, n_ - 1)
                need(pe, proj_read_by_dve, dve_seen(n_, b, l, name))
                if name == "K":
                    for n, (a, c) in enumerate(PARTS):
                        for kc in range(KC):
                            i = mm(proj[:, bk, 0:S], w("K", a)[:, kc * 512 + g * D:kc * 512 + (g + 1) * D],
                                   (xnT_hi if c == 0 else xnT_lo)[:, kc, :], start=(n + kc == 0), stop=(n == 2 and kc == KC - 1))
                elif name == "Q":
                    for h in range(2):
                        hh = 2 * (l % 2) + h
                        for n, (a, c) in enumerate(PARTS):
                            for kc in range(KC):
                                i = mm(proj[:, bk, h * S:(h + 1) * S], w(f"Q{g}", a)[:, kc * 512 + hh * D:kc * 512 + (hh + 1) * D],
                                       (xnT_hi if c == 0 else xnT_lo)[:, kc, :], start=(n + kc == 0), stop=(n == 2 and kc == KC - 1))
                else:
                    t = int(name[1])
                    for n, (a, c) in enumerate(PARTS):
                        for kc in range(KC):
                            i = mm(proj[:, bk, :], (xnT_hi if c == 0 else xnT_lo)[:, kc, t * P:(t + 1) * P],
                                   w("V", a)[:, kc * 512:(kc + 1) * 512], start=(n + kc == 0), stop=(n == 2 and kc == KC - 1))
                i.then_inc(proj_filled, 1)

            def scores(v, l):
                q, g = l % 2, l // 2
                need(pe, probsT_ready, v - 1)
                for h in range(2):
                    bk = sc[:, 2 * q + h, :]
                    mm(bk[:, 0:P], qt[:, q, h, 0:P], kt[:, g % 2, 0:P], start=True, stop=False)
                    mm(bk[:, 0:P], id_bf[:, :], cau_bf[:, :], start=False, stop=True)
                    mm(bk[:, P:P + S + NCH], qt[:, q, h, P:S], kt[:, g % 2, :], start=True, stop=False)
                    i = mm(bk[:, S:S + P], id_bf[:, :], cau_bf[:, :], start=False, stop=True)
                i.then_inc(scores_ready, 1)

            def transpose_probs(v, q):
                pe.wait_ge(probs_ready, v + 1)
                for h in range(2):
                    for n in range(3):
                        i = nc.tensor.transpose(sc[:, 2 * q + h, n * P:(n + 1) * P], probs[:, h, n * P:(n + 1) * P], id_sb[:, :])
                i.then_inc(probsT_in_bank, 1)

            def weigh(v, g):
                pe.wait_ge(probsT_ready, v + 1)
                need(pe, oT_hi_ready, v)
                need(pe, oT_lo_ready, v)
                for h in range(2):
                    mm(ot[:, h * S:(h + 1) * S], values[:, 0, g * D:(g + 1) * D], pT[:, h, 0:S], start=True, stop=False)
                    i = mm(ot[:, h * S + P:(h + 1) * S], values[:, 1, g * D:(g + 1) * D], pT[:, h, S:384], start=False, stop=True)
                i.then_inc(product_in_bank, 1)

            def output(v, l):
                pe.wait_ge(oT_hi_ready, v + 1)
                pe.wait_ge(oT_lo_ready, v + 1)
                for h in range(2):
                    hh = 2 * (l % 2) + h
                    for t in range(TT):
                        for n, (a, c) in enumerate(PARTS):
                            i = mm(y[:, t, :], (oT_hi, oT_lo)[a][:, h, t * P:(t + 1) * P], w(f"O{l // 2}", c)[:, hh * H:(hh + 1) * H],
                                   start=(l == 0 and h == 0 and t == 0 and n == 0), stop=(l == 7 and h == 1 and n == 2), skip_group_check=True)
                i.then_inc(output_added, 1)

            pe.wait_ge(w_lo_ready, 1)
            pe.wait_ge(xnT_lo_ready, 1)
            project("K", 0, 0, 0, 0, 0)
            pe.wait_ge(w_lo_ready, 2)
            project("Q", 0, 0, 1, 1, 0)
            project("Q", 0, 1, 2, 0, 0)
            cross_attention()

            def body(b, first, last):
                for l in range(STEPS):
                    v = b * STEPS + l

                    def projections():
                        if last and l >= 6:
                            return
                        for name in USES[l]:
                            if name[0] == "V":
                                continue
                            g = ((l + 2) // 2) % NG
                            if first:
                                pe.wait_ge(w_lo_ready, SLICES.index(f"Q{g}") + 1)
                            project(name, b, l, use(b, l, name), bank(l, name), g)
                    if first and l < 2:
                        pe.wait_ge(rotation_done, 2 + l)
                    else:
                        lv = (l - 2) % STEPS
                        pe.wait_ge(rotation_done, rope(b if l >= 2 else b - 1, lv, "Q") + 1)
                    pe.wait_ge(chunk_sums_ready, NG * b + l // 2 + 1)
                    if first and l == 0:
                        pe.wait_ge(setup_by_dve, 2)
                    if first and l == 1:
                        pe.wait_ge(setup_by_act, 8)
                    scores(v, l)
                    if not first and l == 7:
                        post_pe(b - 1, 6, v - 1)
                    if l == 6 and not last:
                        pe.wait_ge(xnT_hi_ready, b + 2)
                        pe.wait_ge(xnT_lo_ready, b + 2)
                    projections()
                    if last and l == 7:
                        transpose_probs(v - 1, (l - 1) % 2)
                    if not first and l == 7:
                        post_pe(b - 1, 7, v - 1)
                    if l == 5 and not last:
                        pe.wait_ge(normed_rows_ready, b + 2)
                        pe.wait_ge(proj_read_by_act, use(b, 6, "K") - 1)
                        pe.wait_ge(proj_read_by_dve, dve_seen(use(b, 6, "K"), b, 6, "K"))
                        transposes(xnrow, proj[:, bank(6, "K"), :]).then_inc(xnT_in_bank, 1)
                    if not (first and l == 0) and not (last and l == 7):
                        transpose_probs(v - 1, (l - 1) % 2)
                    if not (first and l < 2):
                        if first and l % 2 == 0:
                            pe.wait_ge(w_lo_ready, SLICES.index(f"O{(l - 2) // 2}") + 1)
                        if l == 2:
                            need(pe, x1_ready, b)
                        output(v - 2, (l - 2) % STEPS)
                    if not (first and l == 0):
                        if not first and l == 7:
                            pe.wait_ge(logits_read, b + 1)
                        if l == 1:
                            pe.wait_ge(proj_read_by_act, use(b, 0, "V1") + 1)
                        weigh(v - 1, ((l - 1) % STEPS) // 2)
                    if first and l == 7:
                        pe.wait_ge(w_lo_ready, len(SLICES))
                    if l == 0:
                        if first:
                            pe.wait_ge(w_lo_ready, 3)
                        for name in ("V0", "V1"):
                            project(name, b, 0, use(b, 0, name), bank(0, name), 0)

            def post_pe(p, l, v):
                if l == 6:
                    pe.wait_ge(x2_normed, p + 1)
                    pe.wait_ge(oT_hi_ready, v)
                    pe.wait_ge(oT_lo_ready, v)
                    transposes(post, ot).then_inc(x2T_in_bank, 1)
                if l == 7:
                    pe.wait_ge(x2T_ready, p + 1)
                    pe.wait_ge(oT_hi_ready, v)
                    pe.wait_ge(oT_lo_ready, v)
                    for t in range(TT):
                        for kc in range(KC):
                            i = mm(ot[:, t * E_N:(t + 1) * E_N], post[:, kc, t * P:(t + 1) * P], rw_sb[:, kc, :], start=(kc == 0), stop=(kc == KC - 1))
                    i.then_inc(logits_in_bank, 1)

            batches(pe, body)
            V = B * STEPS
            transpose_probs(V - 1, 1)
            output(V - 2, 6)
            pe.wait_ge(logits_read, B)
            weigh(V - 1, NG - 1)
            output(V - 1, 7)
            for l in range(STEPS):
                post_pe(B - 1, l, V)
            pe.wait_ge(tl["onehot"], 1)
            mm(proj[:, 1, 0:256], tri_bf[:, 1], oh, start=True, stop=True).then_inc(tl["counts"], 1)
            mm(proj[:, 0, 0:256], tri_bf[:, 0], oh, start=True, stop=True).then_inc(tl["counts"], 1)
            pe.wait_ge(tl["row_experts"], 1)
            pe.wait_ge(tl["places"], 1)
            for i in range(NT):
                e_ = mm((proj[:, 0], y_flat)[i // 4][:, (i % 4) * P:(i % 4 + 1) * P], exp_q[:, i:i + 1].to_broadcast([P, P]), id_sb[:, :], start=True, stop=True)
            e_.then_inc(tl["expert_columns"], 1)
            pe.wait_ge(tl["zeros"], 1)
            pe.wait_ge(tl["scattered"], 16 * NT)
            for m in (1, 2, 3, 4, 5, 1, 2, 3):
                mm(banks[:, m, :], id_bf[:, :], bias_x[:, :, :].rearrange("p t s -> p (t s)"), start=True, stop=False, skip_group_check=True)

            def transpose_sorted(m):
                pe.wait_ge(tl["normed"], 2 * m + 2)
                need(pe, tl["sortedT"], m - 1)
                if m == 1:
                    pe.wait_ge(tl["expT"], 1)
                for i in (2 * m, 2 * m + 1):
                    for kc in range(KC):
                        t_ = nc.tensor.transpose((ot[:, :] if m % 2 == 0 else y_flat)[:, ((i % 2) * KC + kc) * P:((i % 2) * KC + kc + 1) * P],
                                                 (xnrow, post)[m % 2][:, i % 2, kc * P:(kc + 1) * P], id_sb[:, :])
                t_.then_inc(tl["transposed"], 1)

            def multiply(r, first, between=None):
                cols = load_row(mybir.EngineType.PE, 0, r)
                exs = load_row(mybir.EngineType.PE, 1, r)
                for k in range(1 if first else 0, 4):
                    j = 4 * r + k - 1
                    pe.wait_ge(tl["staged"], j + 1)
                    for kc in range(KC):
                        i = mm(sums_flat[:, bass.ds(cols[k], H)], stage_x[:, k, kc, :],
                               experts[:, bass.ds(exs[k], 1), kc, :].rearrange("p a n -> p (a n)"), start=False, stop=False, skip_group_check=True)
                    i.then_inc(tl["segment"], 1)
                    if between and k < 3:
                        between(k)
            transpose_sorted(0)
            transpose_sorted(1)
            pe.wait_ge(tl["tables"], 2)
            pe.wait_ge(experts_ready, E_N)
            multiply(0, True, lambda k: transpose_sorted(k + 1))
            with pe.Fori(1, SEG_ROWS) as r:
                multiply(r, False)


def kernel(x, ctx_512, mask_SxS2_bk1, mask_BxS2_bf0, L0_attn_wq, L0_attn_wk, L0_attn_wv, L0_attn_wo, L0_xattn_Wq,
           L0_xattn_bq, L0_xattn_Wk, L0_xattn_bk, L0_ffn_weight, L0_ffn_scale, L0_ffn_expert_masks, L0_ffn_router_w):
    import numpy as np
    import concourse.bacc as bacc
    from concourse.bass_utils import run_bass_kernel_spmd

    def lay(a):
        return np.ascontiguousarray(a)

    inv = (1.0 / np.float32(10000.0) ** (np.arange(0, D, 2, dtype=np.float32) / np.float32(D))).astype(np.float32)
    ang = (np.arange(S, dtype=np.float32)[:, None] * inv[None, :]).astype(np.float32)
    cos, sin = np.cos(ang).astype(np.float32).T, np.sin(ang).astype(np.float32).T
    p_, f_ = np.arange(P)[:, None], np.arange(P)[None, :]
    con = np.zeros((P, 256), np.float32)
    past = np.arange(NCAND)[None, :] < (P // CHUNK + p_ // CHUNK)
    con[:, 0:7] = np.where(past, 0.0, NEG)
    con[:, 8:15] = np.where(past, -NEG, 0.0)
    con[:, 72:104] = np.arange(E_N)
    con[:, 104:104 + SEGS] = np.arange(SEGS)
    con[:, 144:151] = P * np.arange(1, NT)
    con[:, 152:159] = np.arange(1, NT)
    con[:, 176:178], con[:, 178:180] = EPS, -0.5
    con[:, 160:168] = P * np.arange(NT)[None, :] + p_

    def by_slices(a, cols):
        return lay(a.reshape(KC, P, -1, cols).transpose(1, 2, 0, 3).reshape(P, -1))

    c2, s2 = np.concatenate([cos, cos], 0), np.concatenate([-sin, sin], 0)
    arrays = {
        "x": lay(x),
        "ctxT": lay(ctx_512.reshape(B * S, CTX).T),
        "smask": lay(mask_SxS2_bk1),
        "kmask": lay(mask_BxS2_bf0),
        "wq": by_slices(L0_attn_wq, HG * D),
        "wk": by_slices(L0_attn_wk, NG * D),
        "wv": by_slices(L0_attn_wv, NG * D),
        "wo": lay(L0_attn_wo.reshape(NH, D, H).transpose(1, 0, 2).reshape(D, NH * H)),
        "xw": lay(np.concatenate([L0_xattn_Wq.T, L0_xattn_Wk.T, L0_xattn_bq[:, None], L0_xattn_bk[:, None]], 1)),
        "ffw": lay(np.concatenate([by_slices(L0_ffn_weight.T, H), by_slices(L0_ffn_router_w.T, E_N)], 1)),
        "ffscale": lay(L0_ffn_scale),
        "masks": lay(L0_ffn_expert_masks.reshape(E_N, H, KC, P).transpose(3, 0, 2, 1).reshape(P, E_N * KC * H)),
        "tables": lay(np.concatenate([c2, s2, c2 * np.float32(-SCALE), s2 * np.float32(-SCALE)], 1)),
        "consts": lay(np.concatenate([con, np.eye(P, dtype=np.float32)], 1)),
        "causal": lay(np.concatenate([np.where(f_ <= p_, 0.0, -NEG), (p_ < f_) - 1.0, np.ones((P, P))], 1).astype(np.float32)),
    }
    nc = bacc.Bacc("TRN2", target_bir_lowering=False, num_devices=1, dynamic_dma_scratch_size=8192)
    feeds, args = {}, []
    for name, a in arrays.items():
        feeds[f"in_{name}_dram"] = a
        args.append(nc.dram_tensor(f"in_{name}_dram", a.shape, mybir.dt.from_np(a.dtype), kind="ExternalInput").ap())
    out = nc.dram_tensor("out_0_dram", (B * S, H), mybir.dt.float32, kind="ExternalOutput").ap()
    scratch = nc.dram_tensor("scratch_rows", (B * S, ROW), mybir.dt.float32, kind="Internal").ap()
    program(nc, *args, out, scratch)
    r = run_bass_kernel_spmd(nc, [feeds], core_ids=[0])
    return r.results[0]["out_0_dram"].reshape(B, S, H)
```
